# Optimizing a Trainium2 kernel written in Bass

```python
import numpy as np
import jax
import jax.numpy as jnp

def _softmax(x, axis=-1):
    return jax.nn.softmax(x, axis=axis)

def _gelu(x):
    return jax.nn.gelu(x, approximate=True)

def _silu(x):
    return jax.nn.silu(x)

def _sigmoid(x):
    return jax.nn.sigmoid(x)

def _layernorm(x, axis=-1, eps=1e-05):
    m = jnp.mean(x, axis=axis, keepdims=True)
    v = jnp.var(x, axis=axis, keepdims=True)
    return (x - m) / jnp.sqrt(v + eps)

def _scatter_add(tgt, idx, src, axis=0):
    return tgt.at[idx].add(src)

def _segment_sum(src, seg, n):
    return jax.ops.segment_sum(src, seg, n)
kernel_name = 'mk_seq_postln_d1_jaxref_r8_1b7d3c'

def setup_inputs(seed: int=0):
    np.random.seed(seed)
    _w = jnp.asarray

    def _L0_attn_setup():
        import jax, jax.numpy as jnp
        import numpy as np
        H, P, N, DM = (32, 64, 64, 128)
        DI = H * P
        TH = H * (N // 2)
        DPROJ = 2 * DI + 2 * N + H + TH + H

        def _rms(x, w, eps=1e-05):
            return x * jax.lax.rsqrt(jnp.mean(x * x, -1, keepdims=True) + eps) * w
        key = jax.random.key(seed)
        ks = jax.random.split(key, 5)
        return {'u': jax.random.normal(ks[0], (2, 256, DM), jnp.float32), 'in_proj_w': jax.random.normal(ks[1], (DPROJ, DM), jnp.float32) * (1.0 / np.sqrt(DM)), 'dt_bias': jax.random.normal(ks[2], (H,), jnp.float32), 'A_log': jnp.log(jax.random.uniform(ks[3], (H,), jnp.float32, 1.0, 16.0)), 'D': jnp.ones((H,), jnp.float32), 'B_norm_w': jnp.ones((N,), jnp.float32), 'C_norm_w': jnp.ones((N,), jnp.float32), 'B_bias': jnp.ones((H, N), jnp.float32), 'C_bias': jnp.ones((H, N), jnp.float32), 'norm_w': jnp.ones((DI,), jnp.float32), 'out_proj_w': jax.random.normal(ks[4], (DM, DI), jnp.float32) * (1.0 / np.sqrt(DI))}
    _L0_attn_in = _L0_attn_setup()

    def _L0_ffn_setup():
        import jax, jax.numpy as jnp
        import numpy as np
        TOP_K = 2
        CAP_FACTOR = 1.25
        MIN_CAPACITY = 4
        key = jax.random.key(seed)
        k1, k2, k3, k4 = jax.random.split(key, 4)
        B, T, C, E = (8, 256, 128, 8)
        x = jax.random.normal(k1, (B, T, C), dtype=jnp.float32)
        w_g = jax.random.normal(k2, (E, C), dtype=jnp.float32) * 0.02
        c_fc = jax.random.normal(k3, (E, C, 4 * C), dtype=jnp.float32) * 0.02
        c_proj = jax.random.normal(k4, (E, 4 * C, C), dtype=jnp.float32) * 0.02
        return {'x': x, 'w_g': w_g, 'c_fc': c_fc, 'c_proj': c_proj}
    _L0_ffn_in = _L0_ffn_setup()
    _d = {'L0_attn_u': _L0_attn_in['u'], 'L0_attn_in_proj_w': _L0_attn_in['in_proj_w'], 'L0_attn_dt_bias': _L0_attn_in['dt_bias'], 'L0_attn_A_log': _L0_attn_in['A_log'], 'L0_attn_D': _L0_attn_in['D'], 'L0_attn_B_norm_w': _L0_attn_in['B_norm_w'], 'L0_attn_C_norm_w': _L0_attn_in['C_norm_w'], 'L0_attn_B_bias': _L0_attn_in['B_bias'], 'L0_attn_C_bias': _L0_attn_in['C_bias'], 'L0_attn_norm_w': _L0_attn_in['norm_w'], 'L0_attn_out_proj_w': _L0_attn_in['out_proj_w'], 'L0_ffn_w_g': _L0_ffn_in['w_g'], 'L0_ffn_c_fc': _L0_ffn_in['c_fc'], 'L0_ffn_c_proj': _L0_ffn_in['c_proj']}
    _x0 = _d['L0_attn_u']
    _d['L0_attn_u'] = jax.random.normal(jax.random.fold_in(jax.random.key(seed), 1), (8, 256, 128), dtype=_x0.dtype)
    del _x0
    return _d

def reference(L0_attn_u, L0_attn_in_proj_w, L0_attn_dt_bias, L0_attn_A_log, L0_attn_D, L0_attn_B_norm_w, L0_attn_C_norm_w, L0_attn_B_bias, L0_attn_C_bias, L0_attn_norm_w, L0_attn_out_proj_w, L0_ffn_w_g, L0_ffn_c_fc, L0_ffn_c_proj):

    def _L0_attn_ref(u, in_proj_w, dt_bias, A_log, D, B_norm_w, C_norm_w, B_bias, C_bias, norm_w, out_proj_w):
        import jax, jax.numpy as jnp
        import numpy as np
        H, P, N, DM = (32, 64, 64, 128)
        DI = H * P
        TH = H * (N // 2)
        DPROJ = 2 * DI + 2 * N + H + TH + H

        def _rms(x, w, eps=1e-05):
            return x * jax.lax.rsqrt(jnp.mean(x * x, -1, keepdims=True) + eps) * w
        Bsz, L, _ = u.shape
        proj = u @ in_proj_w.T
        z = proj[..., :DI]
        xin = proj[..., DI:2 * DI]
        Braw = proj[..., 2 * DI:2 * DI + N]
        Craw = proj[..., 2 * DI + N:2 * DI + 2 * N]
        off = 2 * DI + 2 * N
        dt_raw = proj[..., off:off + H]
        theta = proj[..., off + H:off + H + TH].reshape(Bsz, L, H, N // 2)
        lam = jax.nn.sigmoid(proj[..., off + H + TH:])
        dt = jax.nn.softplus(dt_raw + dt_bias)
        A = -jnp.exp(A_log)
        Bm = _rms(Braw, B_norm_w)[:, :, None, :] + B_bias
        Cm = _rms(Craw, C_norm_w)[:, :, None, :] + C_bias
        tc = jnp.cumsum(theta, axis=1)
        cos_t, sin_t = (jnp.cos(tc), jnp.sin(tc))

        def rope(v):
            v1, v2 = (v[..., :N // 2], v[..., N // 2:])
            return jnp.concatenate([v1 * cos_t - v2 * sin_t, v1 * sin_t + v2 * cos_t], -1)
        Bm, Cm = (rope(Bm), rope(Cm))
        xh = xin.reshape(Bsz, L, H, P)
        alpha = jnp.exp(dt * A)
        gamma = lam * dt
        beta = (1.0 - lam) * dt * alpha
        tofirst = lambda a: jnp.moveaxis(a, 1, 0)
        xs = (tofirst(xh), tofirst(Bm), tofirst(Cm), tofirst(alpha), tofirst(gamma), tofirst(beta))
        h0 = jnp.zeros((Bsz, H, P, N), jnp.float32)

        def step(carry, inp):
            h, prevBx = carry
            x_t, B_t, C_t, a_t, g_t, b_t = inp
            Bx = jnp.einsum('bhp,bhn->bhpn', x_t, B_t)
            h = a_t[..., None, None] * h + g_t[..., None, None] * Bx + b_t[..., None, None] * prevBx
            y = jnp.einsum('bhpn,bhn->bhp', h, C_t)
            return ((h, Bx), y)
        _, ys = jax.lax.scan(step, (h0, h0), xs)
        y = jnp.moveaxis(ys, 0, 1)
        y = y + xh * D[None, None, :, None]
        y = y.reshape(Bsz, L, DI)
        y = y * jax.nn.silu(z)
        y = _rms(y, norm_w)
        return y @ out_proj_w.T

    def _L0_ffn_ref(x, w_g, c_fc, c_proj):
        import jax, jax.numpy as jnp
        import numpy as np
        TOP_K = 2
        CAP_FACTOR = 1.25
        MIN_CAPACITY = 4
        B, T, C = x.shape
        E = w_g.shape[0]
        N = B * T
        capacity = max(MIN_CAPACITY, int(CAP_FACTOR * N * TOP_K / E))
        xf = x.reshape(N, C)
        logits = xf @ w_g.T
        top_logits, top_idx = jax.lax.top_k(logits, TOP_K)
        router_probs = jax.nn.softmax(top_logits, axis=-1)
        oh = jax.nn.one_hot(top_idx, E, dtype=jnp.int32)
        oh_t = oh.transpose(1, 0, 2).reshape(TOP_K * N, E)
        pos = jnp.cumsum(oh_t, axis=0).reshape(TOP_K, N, E).transpose(1, 0, 2)
        rank = jnp.sum((pos - 1) * oh, axis=-1)
        valid = rank < capacity
        probs_masked = router_probs * valid.astype(router_probs.dtype)
        rank_c = jnp.clip(rank, 0, capacity - 1)
        contrib = xf[:, None, :] * valid[..., None].astype(xf.dtype)
        buf = jnp.zeros((E, capacity, C), dtype=xf.dtype).at[top_idx, rank_c].add(contrib)
        h = jnp.einsum('ecd,edf->ecf', buf, c_fc)
        h = jnp.square(jax.nn.relu(h))
        expert_out = jnp.einsum('ecf,efd->ecd', h, c_proj)
        gathered = expert_out[top_idx, rank_c]
        out = jnp.sum(gathered * probs_masked[..., None], axis=1)
        return out.reshape(B, T, C)
    x = L0_attn_u
    x = _layernorm(x + _L0_attn_ref(x, L0_attn_in_proj_w, L0_attn_dt_bias, L0_attn_A_log, L0_attn_D, L0_attn_B_norm_w, L0_attn_C_norm_w, L0_attn_B_bias, L0_attn_C_bias, L0_attn_norm_w, L0_attn_out_proj_w), axis=-1)
    x = _layernorm(x + _L0_ffn_ref(x, L0_ffn_w_g, L0_ffn_c_fc, L0_ffn_c_proj), axis=-1)
    return x

_drawn_inputs = setup_inputs


def setup_inputs(seed=0):
    import zlib

    import numpy as np

    out = dict(_drawn_inputs(seed))
    spreads = {'L0_attn_D': (1.0, 0.6),
     'L0_attn_B_norm_w': (1.0, 0.6),
     'L0_attn_C_norm_w': (1.0, 0.6),
     'L0_attn_B_bias': (1.0, 0.6),
     'L0_attn_C_bias': (1.0, 0.6),
     'L0_attn_norm_w': (1.0, 0.2)}
    factors = {'L0_ffn_w_g': 3.229, 'L0_ffn_c_fc': 3.105, 'L0_ffn_c_proj': 2.85}
    for name, (base, spread) in spreads.items():
        noise = np.random.default_rng([zlib.crc32(name.encode()), seed]).standard_normal(out[name].shape)
        drawn = base * np.exp(spread * noise) if base else spread * noise
        out[name] = jnp.asarray(drawn.astype(out[name].dtype))
    for name, factor in factors.items():
        out[name] = (out[name] * factor).astype(out[name].dtype)
    return out
```

```python
from contextlib import ExitStack

import concourse.bass as bass
import numpy as np
from concourse import mybir

F32 = mybir.dt.float32
BF16 = mybir.dt.bfloat16
ALU = mybir.AluOpType
ACT = mybir.ActivationFunctionType
AX = mybir.AxisListType

BATCH, L, DM = 8, 256, 128
H, P, N = 32, 64, 64
DI = H * P
NH = N // 2
TOK = BATCH * L
TP = 128
NT = TOK // TP
TB = L // TP
EXP, TOPK, FF = 8, 2, 4 * DM
CAP = max(4, int(1.25 * TOK * TOPK / EXP))
EPS = 1e-5

HALVES = 2
HU = H // HALVES
PU = HU // 2
UNITS = BATCH * HALVES
DU = HU * P
W_S = L + TP

CR = 3 * HU
CN = 64

ROUND = float(1.5 * 2 ** 23)
TWO_PI = float(np.nextafter(np.float32(2 * np.pi), np.float32(0)))
HALF_PI = float(np.float32(np.pi / 2))
NEG = -1e30


def sbuf(nc, stack, name, shape, dt=F32):
    return stack.enter_context(nc.sbuf_tensor(name, shape, dt))


def semaphores(nc, stack, names):
    return {n: stack.enter_context(nc.semaphore(n)) for n in names.split()}


def setup_phase(nc, ins, keep, dram):
    st = ExitStack()
    with st:
        uT = sbuf(nc, st, "su_uT", [128, TOK + 1])
        uni = sbuf(nc, st, "su_uni", [128, L])
        cum = sbuf(nc, st, "su_cum", [128, TOK])
        wsm = sbuf(nc, st, "su_wsm", [128, 2 * N + 2 * H])
        raw = sbuf(nc, st, "su_raw", [128, NT, 2 * N + 4 * H])
        tri = sbuf(nc, st, "su_tri", [128, 128])
        ones = sbuf(nc, st, "su_ones", [128, 128])
        dtb = sbuf(nc, st, "su_dtb", [128, H])
        alog = sbuf(nc, st, "su_alog", [128, H])
        dsk = sbuf(nc, st, "su_dsk", [128, H])
        nw = sbuf(nc, st, "su_nw", [128, 2, N])
        bbT = sbuf(nc, st, "su_bbT", [128, 2, H])
        bcp = sbuf(nc, st, "su_bcp", [128, H])
        identb = sbuf(nc, st, "su_identb", [128, 128], BF16)
        ident = sbuf(nc, st, "su_ident", [128, 128])
        x2 = sbuf(nc, st, "su_x2", [128, NT, 2, H])
        ab2 = sbuf(nc, st, "su_ab2", [128, NT, 2, H])
        dt2 = sbuf(nc, st, "su_dt2", [128, NT, 2, H])
        sg = sbuf(nc, st, "su_sg", [128, NT, 2, H])
        expa = sbuf(nc, st, "su_expa", [128, H])
        gam = sbuf(nc, st, "su_gam", [128, NT, H])
        dA = sbuf(nc, st, "su_dA", [128, 2, BATCH, H])
        cA = sbuf(nc, st, "su_cA", [128, BATCH, 2, H])
        rem = sbuf(nc, st, "su_rem", [128, BATCH, 2, H])
        cs = sbuf(nc, st, "su_cs", [128, NT, HALVES, 128], BF16)
        cT = sbuf(nc, st, "su_cT", [64, HALVES, TOK], BF16)
        sq = sbuf(nc, st, "su_sq", [128, NT, 2, N])
        ss = sbuf(nc, st, "su_ss", [128, NT, 2])
        ms = sbuf(nc, st, "su_ms", [128, NT, 2])
        rs = sbuf(nc, st, "su_rs", [128, NT, 2])
        nt = sbuf(nc, st, "su_nt", [128, NT, 2])
        nb = sbuf(nc, st, "su_nb", [128, NT, 2, N])
        vin = sbuf(nc, st, "su_vin", [128, NT, 4, 128])
        bcd = sbuf(nc, st, "su_bcd", [128, NT])
        ps = [st.enter_context(nc.psum_tensor(f"su_ps{i}", [128, 512], F32)) for i in range(6)]
        pb = [st.enter_context(nc.psum_tensor(f"su_pb{i}", [128, 1024], BF16)) for i in range(2)]
        s = semaphores(nc, st, "su_u su_small su_a_ld su_raw_ps su_raw_sb su_dve su_dt_x su_dt_l su_cA_ps su_cs su_ct_ps su_ct_sb "
                               "su_ms su_rs su_vin su_vin2 su_v_ps su_v_sb su_bc_ps su_cum su_memset su_out su_act su_expa su_bcp")
        blk = st.enter_context(nc.Block())

        @blk.sync
        def _(sp):
            sp.dma_start(uT[:, 0:TOK], ins["uT"][:, :]).then_inc(s["su_u"], 16)
            sp.dma_start(wsm[:], ins["w_small"][:, :]).then_inc(s["su_u"], 16)
            for dst, src in ((tri[:], ins["tri"][:, :]), (ident[:], ins["ident"][:, :]), (identb[:], ins["ident_b"][:, :]),
                             (dtb[:], ins["dt_bias"].partition_broadcast(128)), (alog[:], ins["A_log"].partition_broadcast(128)),
                             (dsk[:], ins["D"].partition_broadcast(128)),
                             (nw[:, 0, :], ins["B_norm"].partition_broadcast(128)), (nw[:, 1, :], ins["C_norm"].partition_broadcast(128)),
                             (bbT[0:N, 0, :], ins["B_biasT"][:, :]), (bbT[0:N, 1, :], ins["C_biasT"][:, :])):
                sp.dma_start(dst, src).then_inc(s["su_small"], 16)
            for name in ("w_theta", "w_x", "w_z", "w_out", "norm_w", "bias", "mask", "hot"):
                t = keep[name]
                sp.dma_start(t[:], ins[name]).then_inc(s["su_a_ld"], 16)
            sp.dma_start(keep["ident"][:], ins["ident"][:, :]).then_inc(s["su_a_ld"], 16)
            sp.dma_start(keep["ident_b"][:], ins["ident_b"][:, :]).then_inc(s["su_a_ld"], 16)
            sp.wait_ge(s["su_cum"], 1)
            sp.dma_start(dram["cum"][:, :], cum[:]).then_inc(s["su_out"], 16)
            sp.wait_ge(s["su_ct_sb"], 2 * 8)
            sp.dma_start(dram["cT"].rearrange("h r t -> r h t"), cT[0:CR]).then_inc(s["su_out"], 16)
            sp.wait_ge(s["su_v_sb"], NT)
            for tt in range(TB):
                for b in range(BATCH):
                    sp.dma_start(dram["v"][b, :, :, tt * TP:(tt + 1) * TP], vin[:, TB * b + tt]).then_inc(s["su_out"], 16)
            sp.wait_ge(s["su_out"], 32 + 16 * NT)
            sp.wait_ge(s["su_a_ld"], 160)

        @blk.gpsimd
        def _(pool):
            nc.gpsimd.memset(ones[:], 1.0).then_inc(s["su_memset"], 1)
            nc.gpsimd.memset(cs[:], 0.0).then_inc(s["su_memset"], 1)
            pool.wait_ge(s["su_memset"], 2)
            nc.gpsimd.memset(bbT[N:128], 0.0).then_inc(s["su_memset"], 1)
            pool.wait_ge(s["su_memset"], 3)
            nc.gpsimd.memset(bcp[N:128], 0.0).then_inc(s["su_memset"], 1)
            pool.wait_ge(s["su_memset"], 4)
            nc.gpsimd.memset(keep["LS"][0:64], 1.0).then_inc(s["su_memset"], 1)
            pool.wait_ge(s["su_memset"], 5)
            pool.wait_ge(s["su_vin"], 1)
            for k in range(2):
                for o in range(2):
                    nc.gpsimd.tensor_copy(vin[:, :, 2 * k, o * N:(o + 1) * N], nb[:, :, k, :]).then_inc(s["su_vin2"], 1)

        @blk.tensor
        def _(pe):
            pe.wait_ge(s["su_u"], 32)
            pe.wait_ge(s["su_memset"], 5)
            pe.wait_ge(s["su_dve"], 1)
            for i in range(NT):
                if i >= 4:
                    pe.wait_ge(s["su_raw_sb"], i - 3)
                o = ps[i % 4]
                nc.tensor.matmul(o[:, 0:192], uT[:, i * TP:(i + 1) * TP], wsm[:], start=True, stop=True)
                nc.tensor.matmul(o[:, 192:256], uT[:, i * TP + 1:(i + 1) * TP + 1], wsm[:, 128:192],
                                 start=True, stop=True).then_inc(s["su_raw_ps"], 1)
            pe.wait_ge(s["su_small"], 160)
            pe.wait_ge(s["su_dt_l"], 2)
            nc.tensor.matmul(ps[4][:, 0:256], tri[:], dA[:, 0], start=True, stop=True)
            nc.tensor.matmul(ps[4][:, 256:512], tri[:], dA[:, 1], start=True, stop=False)
            nc.tensor.matmul(ps[4][:, 256:512], ones[:], dA[:, 0], start=False, stop=True).then_inc(s["su_cA_ps"], 1)
            pe.wait_ge(s["su_vin"], 2)
            pe.wait_ge(s["su_vin2"], 4)
            for i in range(NT):
                if i >= 4:
                    pe.wait_ge(s["su_v_sb"], i - 3)
                else:
                    pe.wait_ge(s["su_raw_sb"], NT)
                for k in range(4):
                    last = nc.tensor.transpose(ps[i % 4][:, k * 128:(k + 1) * 128], vin[:, i, k, :], ident[:])
                last.then_inc(s["su_v_ps"], 1)
            pe.wait_ge(s["su_cs"], 1)
            for i in range(8):
                if i >= 2:
                    pe.wait_ge(s["su_ct_sb"], 2 * (i - 1))
                for q in range(4):
                    last = nc.tensor.transpose(pb[i % 2][:, q * 128:(q + 1) * 128], cs[:, 2 * i + q % 2, q // 2, :], identb[:])
                last.then_inc(s["su_ct_ps"], 1)
            pe.wait_ge(s["su_v_sb"], NT)
            pe.wait_ge(s["su_bcp"], 1)
            for i in range(NT):
                o = ps[5][:, i * H:(i + 1) * H]
                nc.tensor.matmul(o, vin[:, i, 0, :], bbT[:, 1, :], start=True, stop=False)
                nc.tensor.matmul(o, vin[:, i, 2, :], bbT[:, 0, :], start=False, stop=False)
                last = nc.tensor.matmul(o, ones[:], bcp[:], start=False, stop=True)
            last.then_inc(s["su_bc_ps"], 1)

        @blk.scalar
        def _(act):
            for i in range(NT):
                act.wait_ge(s["su_raw_ps"], i + 1)
                nc.scalar.activation(raw[:, i, :], ps[i % 4][:, 0:256], ACT.Copy).then_inc(s["su_raw_sb"], 1)
            act.wait_ge(s["su_raw_sb"], NT)
            nc.scalar.activation(sg[:, :, 0, :], raw[:, :, 160:192], ACT.Sigmoid).then_inc(s["su_act"], 1)
            nc.scalar.activation(sg[:, :, 1, :], raw[:, :, 224:256], ACT.Sigmoid, scale=-1.0).then_inc(s["su_act"], 1)
            act.wait_ge(s["su_ms"], 1)
            nc.scalar.activation(rs[:], nt[:], ACT.Sqrt).then_inc(s["su_rs"], 1)
            act.wait_ge(s["su_small"], 160)
            nc.scalar.activation(expa[:], alog[:], ACT.Exp).then_inc(s["su_expa"], 1)
            act.wait_ge(s["su_dt_x"], 1)
            nc.scalar.activation(ab2[:], ab2[:], ACT.Exp, scale=-1.0).then_inc(s["su_act"], 1)
            act.wait_ge(s["su_act"], 3)
            nc.scalar.activation(ab2[:], ab2[:], ACT.Ln, bias=1.0).then_inc(s["su_dt_l"], 1)
            for i in range(NT):
                act.wait_ge(s["su_v_ps"], i + 1)
                nc.scalar.activation(vin[:, i], ps[i % 4][:].rearrange("p (k t) -> p k t", k=4), ACT.Copy).then_inc(s["su_v_sb"], 1)

        @blk.vector
        def _(dve):
            chain = [0]

            def link(ins_):
                chain[0] += 1
                ins_.then_inc(s["su_dve"], 1)
                dve.wait_ge(s["su_dve"], chain[0])

            V = nc.vector
            link(V.memset(uT[:, TOK:TOK + 1], 0.0))
            link(V.memset(uni[:], 1.0))
            dve.wait_ge(s["su_u"], 32)
            for b in range(BATCH):
                V.tensor_tensor_scan(cum[:, b * L:(b + 1) * L], uni[:], uT[:, b * L:(b + 1) * L],
                                     0.0, ALU.mult, ALU.add).then_inc(s["su_dve"], 1)
            chain[0] += BATCH
            dve.wait_ge(s["su_dve"], chain[0])
            V.tensor_scalar(cum[:], cum[:], float(1 / (2 * np.pi)), None, ALU.mult).then_inc(s["su_cum"], 1)
            dve.wait_ge(s["su_small"], 160)
            dve.wait_ge(s["su_memset"], 5)
            V.tensor_tensor(bcp[0:N], bbT[0:N, 0, :], bbT[0:N, 1, :], ALU.mult).then_inc(s["su_bcp"], 1)
            dve.wait_ge(s["su_raw_sb"], NT)
            bc = raw[:, :, 0:2 * N].rearrange("p t (k n) -> p t k n", k=2)
            link(V.tensor_tensor(sq[:], bc, bc, ALU.mult))
            link(V.tensor_reduce(ss[:], sq[:], AX.X, ALU.add))
            link(V.tensor_scalar(ms[:], ss[:], 1.0 / N, EPS, ALU.mult, ALU.add))
            V.reciprocal(nt[:], ms[:]).then_inc(s["su_ms"], 1)
            for k in range(2):
                c = 128 + 64 * k
                link(V.tensor_tensor(x2[:, :, k, :], raw[:, :, c:c + H], dtb[:].unsqueeze(1).to_broadcast([128, NT, H]), ALU.add))
            link(V.tensor_scalar(dt2[:], x2[:], -1.0, None, ALU.mult))
            V.tensor_tensor(ab2[:], x2[:], dt2[:], ALU.max).then_inc(s["su_dt_x"], 1)
            dve.wait_ge(s["su_rs"], 1)
            link(V.tensor_tensor(nt[:], rs[:], rs[:], ALU.mult))
            link(V.tensor_tensor(nt[:], nt[:], ms[:], ALU.mult))
            link(V.tensor_scalar(nt[:], nt[:], -0.5, 1.5, ALU.mult, ALU.add))
            link(V.tensor_tensor(rs[:], rs[:], nt[:], ALU.mult))
            link(V.tensor_tensor(nb[:], bc, rs[:].unsqueeze(3).to_broadcast([128, NT, 2, N]), ALU.mult))
            V.tensor_tensor(nb[:], nb[:], nw[:].unsqueeze(1).to_broadcast([128, NT, 2, N]), ALU.mult).then_inc(s["su_vin"], 1)
            dve.wait_ge(s["su_vin"], 1)
            for k in range(2):
                for o in range(2):
                    link(V.tensor_scalar(vin[:, :, 2 * k + 1, 64 * o:64 * o + NH], nb[:, :, k, NH:N], -1.0, None, ALU.mult))
                    link(V.tensor_copy(vin[:, :, 2 * k + 1, 64 * o + NH:64 * o + N], nb[:, :, k, 0:NH]))
            V.tensor_tensor(sq[:, :, 0, :], nb[:, :, 0, :], nb[:, :, 1, :], ALU.mult).then_inc(s["su_vin"], 1)
            dve.wait_ge(s["su_dt_l"], 1)
            dve.wait_ge(s["su_act"], 3)
            dve.wait_ge(s["su_expa"], 1)
            link(V.scalar_tensor_tensor(dt2[:], x2[:], 0.0, ab2[:], ALU.max, ALU.add))
            link(V.tensor_tensor(gam[:], sg[:, :, 0, :], dt2[:, :, 0, :], ALU.mult))
            link(V.tensor_tensor(sg[:, :, 1, :], sg[:, :, 1, :], dt2[:, :, 1, :], ALU.mult))
            link(V.tensor_tensor(keep["w"][:], gam[:], sg[:, :, 1, :], ALU.add))
            for a in range(2):
                ins_ = V.scalar_tensor_tensor(dA[:, a], dt2[:, :, 0, :].rearrange("p (b a) h -> p b a h", a=2)[:, :, a, :],
                                              -1.0, expa[:].unsqueeze(1).to_broadcast([128, BATCH, H]), ALU.mult, ALU.mult)
                if a == 0:
                    link(ins_)
                else:
                    ins_.then_inc(s["su_dt_l"], 1)
            dve.wait_ge(s["su_cA_ps"], 1)
            link(V.tensor_copy(cA[:].rearrange("p b a h -> p a b h"), ps[4][:].rearrange("p (a b h) -> p a b h", a=2, h=H)))
            ca = cA[:].rearrange("p b a (f h) -> p (b a) f h", f=HALVES)
            re = rem[:].rearrange("p b a (f h) -> p (b a) f h", f=HALVES)
            part = [cs[:, :, :, k * HU:(k + 1) * HU] for k in range(3)]
            link(V.tensor_copy(part[0], ca))
            link(V.tensor_tensor(re, ca, part[0], ALU.subtract))
            link(V.tensor_copy(part[1], re))
            link(V.tensor_tensor(re, re, part[1], ALU.subtract))
            link(V.tensor_copy(part[2], re))
            V.tensor_scalar(cs[:, :, :, CN:CN + CR], cs[:, :, :, 0:CR], -1.0, None, ALU.mult).then_inc(s["su_cs"], 1)
            for i in range(8):
                dve.wait_ge(s["su_ct_ps"], i + 1)
                src = pb[i % 2][:, 0:512].rearrange("p (f t) -> p f t", f=2)
                V.tensor_copy(cT[:, :, i * 256:(i + 1) * 256], src[0:64]).then_inc(s["su_ct_sb"], 1)
                V.tensor_copy(keep["LS"][64:128, :, i * 256:(i + 1) * 256], src[64:128]).then_inc(s["su_ct_sb"], 1)
            dve.wait_ge(s["su_vin"], 2)
            link(V.tensor_reduce(bcd[:], sq[:, :, 0, :], AX.X, ALU.add))
            dve.wait_ge(s["su_bc_ps"], 1)
            own = keep["own"]
            link(V.tensor_tensor(own[:], ps[5][:].rearrange("p (t h) -> p t h", h=H), bcd[:].unsqueeze(2).to_broadcast([128, NT, H]), ALU.add))
            link(V.tensor_tensor(own[:], own[:], gam[:], ALU.mult))
            link(V.tensor_tensor(own[:], own[:], dsk[:].unsqueeze(1).to_broadcast([128, NT, H]), ALU.add))
            dve.wait_ge(s["su_a_ld"], 160)
            for k in (1, 3):
                for q in (0, 64):
                    link(V.tensor_scalar(keep["bias"][q:q + NH, k, :], keep["bias"][q:q + NH, k, :], -1.0, None, ALU.mult))
            dve.wait_ge(s["su_a_ld"], 160)
            link(V.tensor_tensor(keep["w_out"][:], keep["w_out"][:], keep["norm_w"][:].unsqueeze(2).to_broadcast([128, DI // 128, DM]), ALU.mult))


def attention_phase(nc, ins, keep, dram):
    st = ExitStack()
    with st:
        ub = sbuf(nc, st, "at_u", [128, L])
        cb_ = sbuf(nc, st, "at_cum", [128, L])
        v = sbuf(nc, st, "at_v", [128, 4, L])
        rh = [sbuf(nc, st, f"at_rh{i}", [128, HU, L], BF16) for i in range(2)]
        km = sbuf(nc, st, "at_km", [128, 512])
        rr = sbuf(nc, st, "at_r", [128, 2, 512])
        ra = sbuf(nc, st, "at_ra", [128, 512])
        sn = sbuf(nc, st, "at_sin", [128, 4, 512])
        co = sbuf(nc, st, "at_cos", [128, 4, 512])
        tmp = sbuf(nc, st, "at_tmp", [128, 4, L])
        Br = sbuf(nc, st, "at_B", [128, PU, L])
        Cr = sbuf(nc, st, "at_C", [128, PU, 2, L])
        ex = sbuf(nc, st, "at_ex", [128, 2, W_S])
        G = sbuf(nc, st, "at_G", [128, 2, W_S])
        xw = sbuf(nc, st, "at_xw", [128, 2, TB, DU])
        xo = sbuf(nc, st, "at_xo", [128, 2, TB, DU])
        sz = sbuf(nc, st, "at_sz", [128, 2, TB, DU])
        yz = sbuf(nc, st, "at_yz", [128, TB, DU])
        yT = sbuf(nc, st, "at_yT", [128, PU, L])
        junk = sbuf(nc, st, "at_junk", [128, DU], BF16)
        pp = [st.enter_context(nc.psum_tensor(f"at_pp{i}", [128, 512], F32)) for i in range(2)]
        pc = [st.enter_context(nc.psum_tensor(f"at_pc{i}", [128, 512], F32)) for i in range(2)]
        pe_ = [st.enter_context(nc.psum_tensor(f"at_pe{i}", [128, 512], F32)) for i in range(2)]
        py = [st.enter_context(nc.psum_tensor("at_py", [128, 512], F32)), pp[1]]
        pt = [st.enter_context(nc.psum_tensor("at_pt", [128, 512], F32)), pp[0]]
        s = semaphores(nc, st, "c_zero c_low u_in cum_in v_in rh_in0 rh_in1 zeroed th_ps z_ps x_ps km_ok r_ok abs_ok sc_ok silu_ok "
                               "xw_ok xs_ok xo_ok rope1 rope_ok b_ok c_ok e_ps e_ok c_ps g_ok y_ps y1_ok y2_ok t_ps t_ok sq_ok o_ps o_ok")
        blk = st.enter_context(nc.Block())
        w_theta, w_x, w_z, w_out = keep["w_theta"], keep["w_x"], keep["w_z"], keep["w_out"]
        bias, mask, identb, ident, LS = keep["bias"], keep["mask"], keep["ident_b"], keep["ident"], keep["LS"]

        def slots(eng, slot):
            slot(0, 0, 0, True, False)
            slot(1, 0, 1, False, False)
            with eng.Fori(1, BATCH) as b:
                slot(2 * b, b, 0, False, False)
                slot(2 * b + 1, b, 1, False, False)
            slot(UNITS, BATCH, 0, False, True)

        @blk.sync
        def _(sp):
            sp.wait_ge(s["zeroed"], 2)

            def load_seq(b):
                sp.dma_start(cb_[:], dram["cum"][:, bass.ds(b * L, L)]).then_inc(s["cum_in"], 16)
                sp.dma_start(ub[:], ins["uT"][:, bass.ds(b * L, L)]).then_inc(s["u_in"], 16)

            def load_v(b):
                sp.dma_start(v[:], dram["v"][bass.ds(b, 1)].rearrange("o p k t -> (o p) k t")).then_inc(s["v_in"], 16)

            def slot(m, b, par, first, last):
                if last:
                    return
                if not (first or (isinstance(m, int) and m < 2)):
                    sp.wait_ge(s["e_ps"], HU * (m - 1))
                for h in range(HU):
                    sp.dma_start(rh[par][h:CR:HU, h, :],
                                 dram["cT"][par, h:CR:HU, bass.ds(b * L, L)]).then_inc(s[f"rh_in{par}"], 16)
                if par == 1 and not (isinstance(m, int) and m == UNITS - 1):
                    sp.wait_ge(s["x_ps"], 4 * (m + 1))
                    load_seq(b + 1)
                    sp.wait_ge(s["rope_ok"], PU * (m + 1))
                    load_v(b + 1)

            load_seq(0)
            load_v(0)
            slot(0, 0, 0, True, False)
            for h in range(HU):
                sp.dma_start(rh[1][h:CR:HU, h, :], dram["cT"][1, h:CR:HU, 0:L]).then_inc(s["rh_in1"], 16)
            sp.wait_ge(s["x_ps"], 8)
            load_seq(1)
            sp.wait_ge(s["rope_ok"], 2 * PU)
            load_v(1)
            with sp.Fori(1, BATCH - 1) as b:
                slot(2 * b, b, 0, False, False)
                slot(2 * b + 1, b, 1, False, False)
            slot(UNITS - 2, BATCH - 1, 0, False, False)
            slot(UNITS - 1, BATCH - 1, 1, False, False)

        @blk.tensor
        def _(pe):
            def slot(m, b, par, first, last):
                n = m - 1
                po = 1 - par
                if not last:
                    if not first:
                        if not (isinstance(m, int) and m == 1):
                            pe.wait_ge(s["o_ok"], m - 1)
                        pe.wait_ge(s["xs_ok"], 4 * m)
                    pe.wait_ge(s["cum_in"], 16 * (b + 1))
                    for q in range(4):
                        if q >= 2:
                            pe.wait_ge(s["r_ok"], 4 * m + q - 1)
                        for k in range(2):
                            j = par * PU + 2 * q + k
                            last_i = nc.tensor.matmul(pp[q % 2][:, k * L:(k + 1) * L], w_theta[:, j * 128:(j + 1) * 128], cb_[:],
                                                      start=True, stop=True)
                        last_i.then_inc(s["th_ps"], 1)
                    pe.wait_ge(s["u_in"], 16 * (b + 1))
                    for w_, ready, done, prev in ((w_z, "z_ps", "silu_ok", "r_ok"), (w_x, "x_ps", "xs_ok", "silu_ok")):
                        for q in range(4):
                            tt, c = divmod(q, 2)
                            if q < 2:
                                pe.wait_ge(s[prev], 4 * m + q + 3)
                            else:
                                pe.wait_ge(s[done], 4 * m + q - 1)
                            o = par * DU + c * 512
                            nc.tensor.matmul(pp[q % 2][:], ub[:, tt * TP:(tt + 1) * TP], w_[:, o:o + 512],
                                             start=True, stop=True).then_inc(s[ready], 1)
                if first:
                    return
                t0 = (b if po == 0 else b - 1) * L if par == 0 else b * L
                pe.wait_ge(s[f"rh_in{po}"], 16 * HU * ((b if par == 1 else b - 1) + 1))

                def decay(h):
                    if first_unit(n) and h < 2:
                        pass
                    else:
                        pe.wait_ge(s["e_ok"], HU * n + h - 1)
                    e = pe_[h % 2]
                    nc.tensor.matmul(e[:, 0:L], LS[:, po, bass.ds(t0, TP)], rh[po][:, h, :], start=True, stop=False)
                    nc.tensor.matmul(e[:, 0:TP], identb[:], mask[:], start=False, stop=True)
                    nc.tensor.matmul(e[:, L:W_S], LS[:, po, bass.ds(t0 + TP, TP)], rh[po][:, h, TP:L], start=True, stop=False)
                    nc.tensor.matmul(e[:, L:W_S], identb[:], mask[:], start=False, stop=True).then_inc(s["e_ps"], 1)

                def scores(h):
                    j, k = divmod(h, 2)
                    if k == 0:
                        pe.wait_ge(s["b_ok"], PU * n + j + 1)
                        pe.wait_ge(s["c_ok"], PU * n + j + 1)
                    if not (first_unit(n) and h < 2):
                        pe.wait_ge(s["g_ok"], HU * n + h - 1)
                    c = pc[h % 2]
                    nc.tensor.matmul(c[:, 0:L], Br[:, j, 0:TP], Cr[:, j, k, :], start=True, stop=True)
                    nc.tensor.matmul(c[:, L:W_S], Br[:, j, TP:L], Cr[:, j, k, TP:L], start=True, stop=True).then_inc(s["c_ps"], 1)

                def output(h):
                    j, k = divmod(h, 2)
                    pe.wait_ge(s["g_ok"], HU * n + h + 1)
                    if k == 0 and not (first_unit(n) and j < 2):
                        pe.wait_ge(s["y1_ok"], PU * n + j - 1)
                    if h == 2 and not last:
                        pe.wait_ge(s["xs_ok"], 4 * m + 4)
                    y = py[j % 2][:, 0:L].rearrange("p (a c) -> p a c", a=TB)
                    g = G[:, h % 2]
                    c = slice(h * P, (h + 1) * P)
                    nc.tensor.matmul(y[:, 0, k * P:(k + 1) * P], g[:, 0:TP], xw[:, po, 0, c], start=True, stop=True)
                    nc.tensor.matmul(y[:, 1, k * P:(k + 1) * P], g[:, TP:L], xw[:, po, 0, c], start=True, stop=False)
                    nc.tensor.matmul(y[:, 1, k * P:(k + 1) * P], g[:, L:W_S], xw[:, po, 1, c], start=False, stop=True).then_inc(s["y_ps"], 1)

                def turn(j):
                    pe.wait_ge(s["y2_ok"], PU * n + j + 1)
                    if not (first_unit(n) and j < 2):
                        pe.wait_ge(s["t_ok"], PU * n + j - 1)
                    for tt in range(TB):
                        last_i = nc.tensor.transpose(pt[j % 2][:, tt * TP:(tt + 1) * TP], yz[:, tt, j * 128:(j + 1) * 128], ident[:])
                    last_i.then_inc(s["t_ps"], 1)

                pe.wait_ge(s["xw_ok"], 4 * n + 4)
                decay(0)
                for h in range(HU):
                    if h + 1 < HU:
                        decay(h + 1)
                    scores(h)
                    if h >= 1:
                        output(h - 1)
                    if h % 2 == 1 and h >= 5:
                        turn((h - 5) // 2)
                output(HU - 1)
                turn(PU - 2)
                turn(PU - 1)
                pe.wait_ge(s["t_ok"], PU * n + PU)
                for tt in range(TB):
                    for k in range(PU):
                        last_i = nc.tensor.matmul(pp[0][:, tt * DM:(tt + 1) * DM], yT[:, k, tt * TP:(tt + 1) * TP],
                                                  w_out[:, po * PU + k, :], start=(k == 0), stop=(k == PU - 1))
                last_i.then_inc(s["o_ps"], 1)

            slots(pe, slot)

        @blk.scalar
        def _(act):
            def slot(m, b, par, first, last):
                n = m - 1
                if not last:
                    for q in range(4):
                        act.wait_ge(s["r_ok"], 4 * m + q + 1)
                        if not first:
                            act.wait_ge(s["rope_ok"], PU * n + 2 * q + 2)
                        nc.scalar.activation(sn[:, q, :], rr[:, q % 2], ACT.Sin, scale=-TWO_PI).then_inc(s["sc_ok"], 1)
                        if q > 0 or not first:
                            act.wait_ge(s["sc_ok"], 8 * m + 2 * q)
                        nc.scalar.activation(ra[:], rr[:, q % 2], ACT.Abs).then_inc(s["abs_ok"], 1)
                        act.wait_ge(s["abs_ok"], 4 * m + q + 1)
                        nc.scalar.activation(co[:, q, :], ra[:], ACT.Sin, scale=-TWO_PI, bias=keep["half_pi"][:, 0:1]).then_inc(s["sc_ok"], 1)
                    if not (first or (isinstance(m, int) and m == 1)):
                        act.wait_ge(s["y2_ok"], PU * (m - 1))
                    for q in range(4):
                        tt, c = divmod(q, 2)
                        act.wait_ge(s["z_ps"], 4 * m + q + 1)
                        nc.scalar.activation(sz[:, par, tt, c * 512:(c + 1) * 512], pp[q % 2][:], ACT.Silu).then_inc(s["silu_ok"], 1)
                    for q in range(4):
                        tt, c = divmod(q, 2)
                        act.wait_ge(s["x_ps"], 4 * m + q + 1)
                        nc.scalar.activation(xo[:, par, tt, c * 512:(c + 1) * 512], pp[q % 2][:], ACT.Copy).then_inc(s["xs_ok"], 1)
                if first:
                    return

                def decay(h):
                    act.wait_ge(s["e_ps"], HU * n + h + 1)
                    if not (first_unit(n) and h < 2):
                        act.wait_ge(s["g_ok"], HU * n + h - 1)
                    nc.scalar.activation(ex[:, h % 2], pe_[h % 2][:, 0:W_S], ACT.Exp).then_inc(s["e_ok"], 1)

                def turn(j):
                    act.wait_ge(s["t_ps"], PU * n + j + 1)
                    if not first_unit(n):
                        act.wait_ge(s["o_ps"], n)
                    nc.scalar.activation(yT[:, j, :], pt[j % 2][:, 0:L], ACT.Copy).then_inc(s["t_ok"], 1)

                decay(0)
                for h in range(HU):
                    if h + 1 < HU:
                        decay(h + 1)
                    if h % 2 == 1 and h >= 5:
                        turn((h - 5) // 2)
                turn(PU - 2)
                turn(PU - 1)
                act.wait_ge(s["y2_ok"], PU * n + PU)
                for tt in range(TB):
                    if tt or not first_unit(n):
                        act.wait_ge(s["sq_ok"], TB * n + tt)
                    nc.scalar.activation(junk[:], yz[:, tt, :], ACT.Square,
                                         accum_out=keep["ssq"][:, bass.ds(2 * n + tt, 1)]).then_inc(s["sq_ok"], 1)

            slots(act, slot)

        @blk.gpsimd
        def _(pool):
            nc.gpsimd.memset(Cr[0:64, :, 1, :], 0.0).then_inc(s["c_zero"], 1)
            pool.wait_ge(s["c_zero"], 1)
            nc.gpsimd.memset(Cr[64:128, :, 0, :], 0.0).then_inc(s["c_zero"], 1)
            pool.wait_ge(s["c_zero"], 2)

            def slot(m, b, par, first, last):
                if last:
                    return
                n = m - 1
                for q in range(4):
                    tt, c = divmod(q, 2)
                    pool.wait_ge(s["xs_ok"], 4 * m + q + 1)
                    pool.wait_ge(s["xw_ok"], 4 * m + q + 1)
                    x3 = xo[:, par, tt, c * 512:(c + 1) * 512].rearrange("p (h e) -> p h e", e=P)
                    own = keep["own"][:, bass.ds(TB * b + tt, 1), par * HU + c * 8:par * HU + c * 8 + 8]
                    nc.gpsimd.tensor_tensor(x3, x3, own.rearrange("p o h -> p (o h)").unsqueeze(2).to_broadcast([128, 8, P]),
                                            ALU.mult).then_inc(s["xo_ok"], 1)
                for j in range(PU):
                    pool.wait_ge(s["rope_ok"], PU * m + j + 1)
                    if not first:
                        pool.wait_ge(s["c_ps"], HU * n + 2 * j + 2)
                    nc.gpsimd.tensor_tensor(Br[:, j, :], tmp[:, 0], tmp[:, 1], ALU.add).then_inc(s["b_ok"], 1)
                    pool.wait_ge(s["b_ok"], PU * m + j + 1)
                    nc.gpsimd.tensor_tensor(Cr[0:64, j, 0, :], tmp[0:64, 2], tmp[0:64, 3], ALU.add).then_inc(s["c_low"], 1)
                    pool.wait_ge(s["c_low"], PU * m + j + 1)
                    nc.gpsimd.tensor_tensor(Cr[64:128, j, 1, :], tmp[64:128, 2], tmp[64:128, 3], ALU.add).then_inc(s["c_ok"], 1)
                    pool.wait_ge(s["c_ok"], PU * m + j + 1)

            slots(pool, slot)

        @blk.vector
        def _(dve):
            V = nc.vector
            for i in range(2):
                V.memset(rh[i][0:64], 0.0).then_inc(s["zeroed"], 1)
                V.tensor_copy(rh[i][64:128], keep["hot"][64:128].unsqueeze(2).to_broadcast([64, HU, L])).then_inc(s["km_ok"], 1)

            def slot(m, b, par, first, last):
                n = m - 1
                po = 1 - par
                if not last:
                    for q in range(4):
                        dve.wait_ge(s["th_ps"], 4 * m + q + 1)
                        if q > 0 or not first:
                            dve.wait_ge(s["r_ok"], 4 * m + q)
                        V.tensor_scalar(km[:], pp[q % 2][:], ROUND, None, ALU.add).then_inc(s["km_ok"], 1)
                        dve.wait_ge(s["km_ok"], 2 + 4 * m + q + 1)
                        if q >= 2 or not first:
                            dve.wait_ge(s["sc_ok"], 8 * m + 2 * q - 2)
                        V.scalar_tensor_tensor(rr[:, q % 2], km[:], ROUND, pp[q % 2][:], ALU.subtract, ALU.subtract).then_inc(s["r_ok"], 1)
                    for q in range(4):
                        tt, c = divmod(q, 2)
                        dve.wait_ge(s["xs_ok"], 4 * m + q + 1)
                        if not first and not (isinstance(m, int) and m == 1):
                            dve.wait_ge(s["y_ps"], HU * (m - 1))
                        w3 = keep["w"][:, bass.ds(TB * b + tt, 1), par * HU + c * 8:par * HU + c * 8 + 8]
                        V.tensor_tensor(xw[:, par, tt, c * 512:(c + 1) * 512].rearrange("p (h e) -> p h e", e=P),
                                        xo[:, par, tt, c * 512:(c + 1) * 512].rearrange("p (h e) -> p h e", e=P),
                                        w3.rearrange("p o h -> p (o h)").unsqueeze(2).to_broadcast([128, 8, P]),
                                        ALU.mult).then_inc(s["xw_ok"], 1)

                def rotate(j):
                    q, k = divmod(j, 2)
                    J = par * PU + j
                    dve.wait_ge(s["sc_ok"], 8 * m + 2 * q + 2)
                    if j == 0:
                        dve.wait_ge(s["v_in"], 16 * (b + 1))
                    if not (first and j == 0):
                        dve.wait_ge(s["c_ok"], PU * m + j)
                        dve.wait_ge(s["b_ok"], PU * m + j)
                    for kind in range(4):
                        angle = (co, sn)[kind % 2][:, q, k * L:(k + 1) * L]
                        last_i = V.scalar_tensor_tensor(tmp[:, kind], v[:, kind, :], bias[:, kind, J:J + 1], angle, ALU.add, ALU.mult)
                    last_i.then_inc(s["rope_ok"], 1)

                def weigh(h):
                    dve.wait_ge(s["e_ok"], HU * n + h + 1)
                    dve.wait_ge(s["c_ps"], HU * n + h + 1)
                    if not (first_unit(n) and h < 2):
                        dve.wait_ge(s["y_ps"], HU * n + h - 1)
                    V.tensor_tensor(G[:, h % 2], pc[h % 2][:, 0:W_S], ex[:, h % 2], ALU.mult).then_inc(s["g_ok"], 1)

                def gate(j):
                    c = slice(j * 128, (j + 1) * 128)
                    dve.wait_ge(s["y_ps"], HU * n + 2 * j + 2)
                    dve.wait_ge(s["xo_ok"], 4 * n + 4)
                    if not first_unit(n):
                        dve.wait_ge(s["t_ps"], PU * n)
                        dve.wait_ge(s["sq_ok"], 2 * n)
                    V.tensor_tensor(yz[:, :, c], py[j % 2][:, 0:L].rearrange("p (a c) -> p a c", a=TB), xo[:, po, :, c], ALU.add).then_inc(s["y1_ok"], 1)
                    dve.wait_ge(s["y1_ok"], PU * n + j + 1)
                    dve.wait_ge(s["silu_ok"], 4 * n + 4)
                    V.tensor_tensor(yz[:, :, c], yz[:, :, c], sz[:, po, :, c], ALU.mult).then_inc(s["y2_ok"], 1)

                for h in range(HU):
                    if not first:
                        weigh(h)
                        if h % 2 == 0 and h >= 2:
                            gate((h - 2) // 2)
                    if h % 2 == 1 and not last:
                        rotate(h // 2)
                if first:
                    return
                gate(PU - 1)
                dve.wait_ge(s["o_ps"], n + 1)
                bn = b if par == 1 else b - 1
                att = keep["att"][:, bass.ds(TB * bn, TB), :]
                o = pp[0][:, 0:TB * DM].rearrange("p (a c) -> p a c", a=TB)
                if po == 0:
                    V.tensor_copy(att, o).then_inc(s["o_ok"], 1)
                else:
                    dve.wait_ge(s["o_ok"], n)
                    V.tensor_tensor(att, o, att, ALU.add).then_inc(s["o_ok"], 1)

            slots(dve, slot)


def first_unit(n):
    return isinstance(n, int) and n == 0


def moe_phase(nc, ins, keep, out):
    st = ExitStack()
    with st:
        u = sbuf(nc, st, "mo_u", [128, NT, DM])
        xr = sbuf(nc, st, "mo_x", [128, NT, DM])
        sq = sbuf(nc, st, "mo_sq", [128, NT, DM])
        x1T = sbuf(nc, st, "mo_xT", [128, TOK])
        wg = sbuf(nc, st, "mo_wg", [128, EXP])
        w1 = sbuf(nc, st, "mo_w1", [128, 2, FF])
        w2 = sbuf(nc, st, "mo_w2", [128, 2, FF // 128, DM])
        low = sbuf(nc, st, "mo_low", [128, 128], BF16)
        oneb = sbuf(nc, st, "mo_oneb", [128, 128], BF16)
        pref = sbuf(nc, st, "mo_pref", [128, EXP])
        half = sbuf(nc, st, "mo_half", [128, NT])
        tot = sbuf(nc, st, "mo_tot", [128, NT])
        rs = sbuf(nc, st, "mo_rs", [128, NT])
        t1 = sbuf(nc, st, "mo_t1", [128, NT])
        lg = sbuf(nc, st, "mo_lg", [128, NT, EXP])
        m12 = sbuf(nc, st, "mo_m12", [128, 2, NT])
        km = sbuf(nc, st, "mo_km", [128, NT])
        ky = sbuf(nc, st, "mo_ky", [128, NT, EXP])
        oh = sbuf(nc, st, "mo_oh", [128, 2, NT, EXP])
        ohb = sbuf(nc, st, "mo_ohb", [128, 2, NT, EXP], BF16)
        pr = sbuf(nc, st, "mo_pr", [128, 2, NT])
        rk = sbuf(nc, st, "mo_rk", [128, 2, NT, EXP])
        sa = sbuf(nc, st, "mo_sa", [128, 2, NT + 1, EXP])
        sb_ = sbuf(nc, st, "mo_sb", [128, 2, NT + 1, EXP])
        gate = sbuf(nc, st, "mo_gate", [128, EXP, NT])
        hr = sbuf(nc, st, "mo_hr", [128, 2, 512])
        hh = sbuf(nc, st, "mo_hh", [128, 2, FF // 128, 512])
        acc = sbuf(nc, st, "mo_acc", [128, NT, DM])
        pu = [st.enter_context(nc.psum_tensor(f"mo_pu{i}", [128, 512], F32)) for i in range(4)]
        pd = [st.enter_context(nc.psum_tensor(f"mo_pd{i}", [128, 4, DM], F32)) for i in range(2)]
        pr_ = [st.enter_context(nc.psum_tensor(f"mo_pr{i}", [128, 512], F32)) for i in range(2)]
        s = semaphores(nc, st, "m_in m_dve m_ms m_rs m_x1 m_xt_ps m_xt m_lg_ps m_oh m_rk_ps m_e m_e2 m_gate w_in0 w_in1 up_ps relu_ok h_ok "
                               "dn_ps dn_ok m_var m_std m_out m_store m_act")
        blk = st.enter_context(nc.Block())
        KF = FF // 128
        GR = TOK // 512

        @blk.sync
        def _(sp):
            for dst, src in ((u[:], ins["u"].rearrange("(t p) c -> p t c", p=128)), (wg[:], ins["w_g"][:, :]), (low[:], ins["low"][:, :]),
                             (pref[:], ins["pref"].partition_broadcast(128))):
                sp.dma_start(dst, src).then_inc(s["m_in"], 16)

            def load(e, k):
                sp.dma_start(w1[:, k], ins["c_fc"][bass.ds(e, 1)].rearrange("o c f -> (o c) f")).then_inc(s[f"w_in{k}"], 16)
                sp.dma_start(w2[:, k], ins["c_proj"][bass.ds(e, 1)].rearrange("o (k p) c -> p (o k) c", p=128)).then_inc(s[f"w_in{k}"], 16)

            load(0, 0)
            load(1, 1)
            with sp.Fori(1, EXP // 2) as e:
                for k in range(2):
                    sp.wait_ge(s["dn_ps"], GR * (2 * e + k - 1))
                    load(2 * e + k, k)
            for g in range(GR):
                sp.wait_ge(s["m_out"], g + 1)
                sp.dma_start(out.rearrange("(t p) c -> p t c", p=128)[:, 4 * g:4 * g + 4, :], sq[:, 4 * g:4 * g + 4, :]).then_inc(s["m_store"], 16)
            sp.wait_ge(s["m_store"], 16 * GR)

        @blk.gpsimd
        def _(pool):
            nc.gpsimd.memset(oneb[:], 1.0).then_inc(s["m_e"], 1)
            nc.gpsimd.memset(sa[:], 0.0).then_inc(s["m_e"], 1)
            nc.gpsimd.memset(acc[:], 0.0).then_inc(s["m_e"], 1)

        @blk.tensor
        def _(pe):
            for i in range(NT):
                if i % 4 == 0:
                    pe.wait_ge(s["m_x1"], i // 4 + 1)
                last = nc.tensor.transpose(pu[i // 4][:, (i % 4) * 128:(i % 4 + 1) * 128], xr[:, i, :], keep["ident"][:])
                if i % 4 == 3:
                    last.then_inc(s["m_xt_ps"], 1)
            for i in range(NT):
                if i % 4 == 0:
                    pe.wait_ge(s["m_xt"], i // 4 + 1)
                last = nc.tensor.matmul(pr_[0][:, i * EXP:(i + 1) * EXP], x1T[:, i * 128:(i + 1) * 128], wg[:], start=True, stop=True)
            last.then_inc(s["m_lg_ps"], 1)
            pe.wait_ge(s["m_oh"], 1)
            pe.wait_ge(s["m_e"], 1)
            nc.tensor.matmul(pr_[1][:, 0:256], low[:], ohb[:].rearrange("p k t e -> p (k t e)"), start=True, stop=True)
            nc.tensor.matmul(pr_[1][:, 256:512], oneb[:], ohb[:].rearrange("p k t e -> p (k t e)"), start=True, stop=True).then_inc(s["m_rk_ps"], 1)

            def up(c, k, g):
                for f in range(KF):
                    i = KF * c + KF * g + f
                    if not (isinstance(c, int) and c == 0 and g == 0):
                        pe.wait_ge(s["relu_ok"], i - KF + 1)
                    nc.tensor.matmul(pu[f][:], w1[:, k, f * 128:(f + 1) * 128], x1T[:, g * 512:(g + 1) * 512],
                                     start=True, stop=True).then_inc(s["up_ps"], 1)

            def down(c, k, g):
                if not (isinstance(c, int) and c == 0 and g < 2):
                    pe.wait_ge(s["dn_ok"], c + g - 1)
                pe.wait_ge(s["h_ok"], KF * (c + g + 1))
                for tt in range(4):
                    for f in range(KF):
                        last = nc.tensor.matmul(pd[g % 2][:, tt, :], hh[:, g % 2, f, tt * 128:(tt + 1) * 128], w2[:, k, f, :],
                                                start=(f == 0), stop=(f == KF - 1))
                last.then_inc(s["dn_ps"], 1)

            def pair(e):
                for k in range(2):
                    c = GR * (2 * e + k)
                    pe.wait_ge(s[f"w_in{k}"], 32 * (e + 1))
                    up(c, k, 0)
                    for g in range(GR):
                        if g + 1 < GR:
                            up(c, k, g + 1)
                        down(c, k, g)

            pair(0)
            with pe.Fori(1, EXP // 2) as e:
                pair(e)

        @blk.scalar
        def _(act):
            act.wait_ge(s["m_ms"], 1)
            nc.scalar.activation(rs[:], t1[:], ACT.Sqrt).then_inc(s["m_rs"], 1)
            act.wait_ge(s["m_ms"], 2)
            nc.scalar.activation(rs[:], t1[:], ACT.Sqrt).then_inc(s["m_rs"], 1)
            for g in range(4):
                act.wait_ge(s["m_xt_ps"], g + 1)
                nc.scalar.activation(x1T[:, g * 512:(g + 1) * 512], pu[g][:], ACT.Copy).then_inc(s["m_xt"], 1)

            act.wait_ge(s["m_lg_ps"], 1)
            nc.scalar.activation(lg[:].rearrange("p t e -> p (t e)"), pr_[0][:, 0:NT * EXP], ACT.Copy).then_inc(s["m_act"], 1)
            act.wait_ge(s["m_e2"], 1)
            nc.scalar.activation(pr[:, 1], pr[:, 0], ACT.Exp).then_inc(s["m_act"], 1)
            act.wait_ge(s["m_act"], 2)
            act.wait_ge(s["m_xt"], 4)

            def relu(c, g, f):
                i = KF * (c + g) + f
                act.wait_ge(s["up_ps"], i + 1)
                if not (isinstance(c, int) and c == 0 and KF * g + f < 2):
                    act.wait_ge(s["h_ok"], i - 1)
                nc.scalar.activation(hr[:, f % 2], pu[f][:], ACT.Relu).then_inc(s["relu_ok"], 1)

            def pair(e):
                for k in range(2):
                    for g in range(GR):
                        for f in range(KF):
                            relu(GR * (2 * e + k), g, f)

            pair(0)
            with act.Fori(1, EXP // 2) as e:
                pair(e)
            act.wait_ge(s["m_var"], 1)
            nc.scalar.activation(rs[:], t1[:], ACT.Sqrt).then_inc(s["m_std"], 1)

        @blk.vector
        def _(dve):
            V = nc.vector
            chain = [0]

            def link(ins_):
                chain[0] += 1
                ins_.then_inc(s["m_dve"], 1)
                dve.wait_ge(s["m_dve"], chain[0])

            def newton():
                link(V.tensor_tensor(t1[:], rs[:], rs[:], ALU.mult))
                link(V.tensor_tensor(t1[:], t1[:], tot[:], ALU.mult))
                link(V.tensor_scalar(t1[:], t1[:], -0.5, 1.5, ALU.mult, ALU.add))
                link(V.tensor_tensor(rs[:], rs[:], t1[:], ALU.mult))

            def wide(a):
                return a.unsqueeze(2).to_broadcast([128, NT, DM])

            def centre(x):
                link(V.tensor_reduce(half[:], x[:], AX.X, ALU.add))
                link(V.tensor_scalar(half[:], half[:], 1.0 / DM, None, ALU.mult))
                link(V.tensor_tensor(x[:], x[:], wide(half[:]), ALU.subtract))
                link(V.tensor_tensor(sq[:], x[:], x[:], ALU.mult))
                link(V.tensor_reduce(tot[:], sq[:], AX.X, ALU.add))
                link(V.tensor_scalar(tot[:], tot[:], 1.0 / DM, EPS, ALU.mult, ALU.add))

            sv = keep["ssq"][:].rearrange("p (b f t) -> p b f t", f=HALVES, t=TB)
            tv = tot[:].rearrange("p (b t) -> p b t", t=TB)
            link(V.tensor_tensor(tv, sv[:, :, 0, :], sv[:, :, 1, :], ALU.add))
            link(V.tensor_scalar(tot[:], tot[:], 1.0 / DI, EPS, ALU.mult, ALU.add))
            V.reciprocal(t1[:], tot[:]).then_inc(s["m_ms"], 1)
            dve.wait_ge(s["m_rs"], 1)
            newton()
            dve.wait_ge(s["m_in"], 64)
            link(V.tensor_tensor(xr[:], keep["att"][:], wide(rs[:]), ALU.mult))
            link(V.tensor_tensor(xr[:], xr[:], u[:], ALU.add))
            centre(xr)
            V.reciprocal(t1[:], tot[:]).then_inc(s["m_ms"], 1)
            dve.wait_ge(s["m_rs"], 2)
            newton()
            for g in range(4):
                V.tensor_tensor(xr[:, 4 * g:4 * g + 4], xr[:, 4 * g:4 * g + 4],
                                rs[:, 4 * g:4 * g + 4].unsqueeze(2).to_broadcast([128, 4, DM]), ALU.mult).then_inc(s["m_x1"], 1)
            dve.wait_ge(s["m_act"], 1)
            w8 = lambda a: a.unsqueeze(2).to_broadcast([128, NT, EXP])
            for k in range(2):
                link(V.tensor_reduce(m12[:, k], lg[:], AX.X, ALU.max))
                link(V.tensor_tensor(ky[:], lg[:], w8(m12[:, k]), ALU.is_equal))
                link(V.tensor_tensor(ky[:], ky[:], pref[:].unsqueeze(1).to_broadcast([128, NT, EXP]), ALU.mult))
                link(V.tensor_reduce(km[:], ky[:], AX.X, ALU.max))
                link(V.tensor_tensor(oh[:, k], ky[:], w8(km[:]), ALU.is_equal))
                if k == 0:
                    link(V.scalar_tensor_tensor(lg[:], oh[:, 0], NEG, lg[:], ALU.mult, ALU.add))
            link(V.tensor_copy(ohb[:], oh[:]))
            V.tensor_tensor(pr[:, 0], m12[:, 1], m12[:, 0], ALU.subtract).then_inc(s["m_e2"], 1)
            V.memset(t1[:], 0.0).then_inc(s["m_oh"], 1)
            dve.wait_ge(s["m_act"], 2)
            link(V.tensor_scalar(km[:], pr[:, 1], 1.0, None, ALU.add))
            link(V.reciprocal(pr[:, 0], km[:]))
            link(V.tensor_tensor(pr[:, 1], pr[:, 1], pr[:, 0], ALU.mult))
            dve.wait_ge(s["m_rk_ps"], 1)
            dve.wait_ge(s["m_e"], 3)
            tots = pr_[1][:, 256:512].rearrange("p (k t e) -> p k t e", k=2, e=EXP)
            link(V.tensor_copy(sa[:, :, 1:NT + 1, :], tots))
            a, b = sa, sb_
            for d in (1, 2, 4, 8):
                for k in range(2):
                    link(V.tensor_copy(b[:, k, 0:d, :], a[:, k, 0:d, :]))
                    link(V.tensor_tensor(b[:, k, d:NT + 1, :], a[:, k, d:NT + 1, :], a[:, k, 0:NT + 1 - d, :], ALU.add))
                a, b = b, a
            link(V.tensor_tensor(rk[:], pr_[1][:, 0:256].rearrange("p (k t e) -> p k t e", k=2, e=EXP), a[:, :, 0:NT, :], ALU.add))
            link(V.tensor_tensor(rk[:, 1], rk[:, 1], a[:, 0, NT:NT + 1, :].to_broadcast([128, NT, EXP]), ALU.add))
            for k in range(2):
                link(V.tensor_scalar(rk[:, k], rk[:, k], float(CAP), None, ALU.is_lt))
                link(V.tensor_tensor(rk[:, k], rk[:, k], oh[:, k], ALU.mult))
                link(V.tensor_tensor(rk[:, k], rk[:, k], w8(pr[:, k]), ALU.mult))
            V.tensor_tensor(gate[:].rearrange("p e t -> p t e"), rk[:, 0], rk[:, 1], ALU.add).then_inc(s["m_gate"], 1)
            dve.wait_ge(s["m_gate"], 1)

            def square(c, g, f):
                i = KF * (c + g) + f
                dve.wait_ge(s["relu_ok"], i + 1)
                if not (isinstance(c, int) and c == 0 and g < 2):
                    dve.wait_ge(s["dn_ps"], c + g - 1)
                V.tensor_tensor(hh[:, g % 2, f], hr[:, f % 2], hr[:, f % 2], ALU.mult).then_inc(s["h_ok"], 1)

            def collect(e, c, g):
                dve.wait_ge(s["dn_ps"], c + g + 1)
                if not (isinstance(c, int) and c == 0):
                    dve.wait_ge(s["dn_ok"], c - GR + g + 1)
                for tt in range(4):
                    i = 4 * g + tt
                    last = V.scalar_tensor_tensor(acc[:, i, :], pd[g % 2][:, tt, :], gate[:, bass.ds(e, 1), i:i + 1].rearrange("p o t -> p (o t)"),
                                                  acc[:, i, :], ALU.mult, ALU.add)
                last.then_inc(s["dn_ok"], 1)

            def pair(e):
                for k in range(2):
                    c = GR * (2 * e + k)
                    for f in range(KF):
                        square(c, 0, f)
                    for g in range(GR):
                        if g + 1 < GR:
                            for f in range(KF):
                                square(c, g + 1, f)
                        collect(2 * e + k, c, g)

            pair(0)
            with dve.Fori(1, EXP // 2) as e:
                pair(e)
            dve.wait_ge(s["dn_ok"], GR * EXP)
            link(V.tensor_tensor(acc[:], acc[:], xr[:], ALU.add))
            centre(acc)
            V.reciprocal(t1[:], tot[:]).then_inc(s["m_var"], 1)
            dve.wait_ge(s["m_std"], 1)
            newton()
            for g in range(4):
                V.tensor_tensor(sq[:, 4 * g:4 * g + 4], acc[:, 4 * g:4 * g + 4],
                                rs[:, 4 * g:4 * g + 4].unsqueeze(2).to_broadcast([128, 4, DM]), ALU.mult).then_inc(s["m_out"], 1)


def build(nc, ins, out):
    st = ExitStack()
    with st:
        keep = {
            "w_theta": sbuf(nc, st, "w_theta", [128, H * 2 * NH]),
            "w_x": sbuf(nc, st, "w_x", [128, DI]),
            "w_z": sbuf(nc, st, "w_z", [128, DI]),
            "w_out": sbuf(nc, st, "w_out", [128, DI // 128, DM]),
            "norm_w": sbuf(nc, st, "norm_w", [128, DI // 128]),
            "bias": sbuf(nc, st, "bias", [128, 4, H // 2]),
            "mask": sbuf(nc, st, "mask", [128, 128], BF16),
            "hot": sbuf(nc, st, "hot", [128, HU], BF16),
            "ident": sbuf(nc, st, "ident", [128, 128]),
            "ident_b": sbuf(nc, st, "ident_b", [128, 128], BF16),
            "half_pi": sbuf(nc, st, "half_pi", [128, 1]),
            "LS": sbuf(nc, st, "LS", [128, HALVES, TOK], BF16),
            "w": sbuf(nc, st, "w_tok", [128, NT, H]),
            "own": sbuf(nc, st, "own_tok", [128, NT, H]),
        }
        dram = {
            "cum": nc.dram_tensor("scratch_cum", [128, TOK], F32, kind="Internal").ap(),
            "cT": nc.dram_tensor("scratch_cT", [HALVES, CR, TOK], BF16, kind="Internal").ap(),
            "v": nc.dram_tensor("scratch_v", [BATCH, 128, 4, L], F32, kind="Internal").ap(),
        }
        ready = st.enter_context(nc.semaphore("half_pi_set"))
        with nc.Block() as blk:
            @blk.vector
            def _(dve):
                nc.vector.memset(keep["half_pi"][:], HALF_PI).then_inc(ready, 1)
                dve.wait_ge(ready, 1)
        setup_phase(nc, ins, keep, dram)
        keep["att"] = sbuf(nc, st, "att", [128, NT, DM])
        keep["ssq"] = sbuf(nc, st, "ssq", [128, UNITS * TB])
        attention_phase(nc, ins, keep, dram)
        moe_phase(nc, ins, keep, out)


def kernel(L0_attn_u, L0_attn_in_proj_w, L0_attn_dt_bias, L0_attn_A_log, L0_attn_D, L0_attn_B_norm_w, L0_attn_C_norm_w,
           L0_attn_B_bias, L0_attn_C_bias, L0_attn_norm_w, L0_attn_out_proj_w, L0_ffn_w_g, L0_ffn_c_fc, L0_ffn_c_proj):
    import concourse.bacc as bacc
    import ml_dtypes
    from concourse.bass_utils import run_bass_kernel_spmd

    def lay(a):
        return np.ascontiguousarray(a)

    u = np.asarray(L0_attn_u).reshape(TOK, DM)
    wT = np.asarray(L0_attn_in_proj_w).T
    off = 2 * DI + 2 * N
    th0 = off + H
    w_theta = wT[:, th0:th0 + H * NH].reshape(DM, H, 1, NH)
    w_theta = np.broadcast_to(w_theta, (DM, H, 2, NH)).reshape(DM, H * 2 * NH)
    w_small = np.concatenate([wT[:, 2 * DI:off + H], wT[:, th0 + H * NH:]], 1)
    nrm = np.asarray(L0_attn_norm_w)

    def bias_rows(a):
        a = np.asarray(a)
        straight = a.reshape(H // 2, 2 * N).T
        first, second = a[:, :NH], a[:, NH:]
        swapped = np.concatenate([second, first], 1).reshape(H // 2, 2 * N).T
        return straight, swapped

    b0, b1 = bias_rows(L0_attn_B_bias)
    c0, c1 = bias_rows(L0_attn_C_bias)
    f32, b16 = np.float32, ml_dtypes.bfloat16
    i = np.arange(128)
    hot = np.zeros((128, HU), b16)
    for k in range(3):
        hot[CN + k * HU + np.arange(HU), np.arange(HU)] = 1
    arrays = {
        "uT": lay(u.T), "u": lay(u), "w_small": lay(w_small), "w_theta": lay(w_theta),
        "w_z": lay(wT[:, 0:DI]), "w_x": lay(wT[:, DI:2 * DI]),
        "w_out": lay(np.asarray(L0_attn_out_proj_w).T.reshape(DI // 128, 128, DM).transpose(1, 0, 2)),
        "norm_w": lay(nrm.reshape(DI // 128, 128).T),
        "bias": lay(np.stack([b0, b1, c0, c1], 1)),
        "dt_bias": lay(L0_attn_dt_bias), "A_log": lay(L0_attn_A_log), "D": lay(L0_attn_D),
        "B_norm": lay(L0_attn_B_norm_w), "C_norm": lay(L0_attn_C_norm_w),
        "B_biasT": lay(np.asarray(L0_attn_B_bias).T), "C_biasT": lay(np.asarray(L0_attn_C_bias).T),
        "w_g": lay(np.asarray(L0_ffn_w_g).T), "c_fc": lay(L0_ffn_c_fc), "c_proj": lay(L0_ffn_c_proj),
        "tri": (i[:, None] <= i[None, :]).astype(f32),
        "low": (i[:, None] < i[None, :]).astype(b16),
        "ident": np.eye(128, dtype=f32), "ident_b": np.eye(128, dtype=b16),
        "mask": np.where(i[:, None] < i[None, :], 0.0, NEG).astype(b16),
        "hot": hot,
        "pref": np.arange(EXP, 0, -1).astype(f32),
    }
    nc = bacc.Bacc("TRN2", target_bir_lowering=False, num_devices=1)
    ins = {k: nc.dram_tensor(f"in_{k}", a.shape, mybir.dt.from_np(a.dtype), kind="ExternalInput").ap() for k, a in arrays.items()}
    out = nc.dram_tensor("out", [TOK, DM], F32, kind="ExternalOutput").ap()
    build(nc, ins, out)
    r = run_bass_kernel_spmd(nc, [{f"in_{k}": a for k, a in arrays.items()}], core_ids=[0])
    return r.results[0]["out"].reshape(BATCH, L, DM)
```

```python
from contextlib import ExitStack

import concourse.bass as bass
import numpy as np
from concourse import mybir

F32 = mybir.dt.float32
BF16 = mybir.dt.bfloat16
ALU = mybir.AluOpType
ACT = mybir.ActivationFunctionType
AX = mybir.AxisListType

BATCH, L, DM = 8, 256, 128
H, P, N = 32, 64, 64
DI = H * P
NH = N // 2
TOK = BATCH * L
TP = 128
NT = TOK // TP
TB = L // TP
EXP, TOPK, FF = 8, 2, 4 * DM
CAP = max(4, int(1.25 * TOK * TOPK / EXP))
EPS = 1e-5

HALVES = 2
HU = H // HALVES
PU = HU // 2
UNITS = BATCH * HALVES
DU = HU * P
W_S = L + TP

CR = 3 * HU
CN = 64

ROUND = float(1.5 * 2 ** 23)
TWO_PI = float(np.nextafter(np.float32(2 * np.pi), np.float32(0)))
HALF_PI = float(np.float32(np.pi / 2))
NEG = -1e30


def sbuf(nc, stack, name, shape, dt=F32):
    return stack.enter_context(nc.sbuf_tensor(name, shape, dt))


def semaphores(nc, stack, names):
    return {n: stack.enter_context(nc.semaphore(n)) for n in names.split()}


def setup_phase(nc, ins, keep, dram):
    st = ExitStack()
    with st:
        uT = sbuf(nc, st, "su_uT", [128, TOK + 1])
        uni = sbuf(nc, st, "su_uni", [128, L])
        cum = sbuf(nc, st, "su_cum", [128, TOK])
        wsm = sbuf(nc, st, "su_wsm", [128, 2 * N + 2 * H])
        raw = sbuf(nc, st, "su_raw", [128, NT, 2 * N + 4 * H])
        tri = sbuf(nc, st, "su_tri", [128, 128])
        ones = sbuf(nc, st, "su_ones", [128, 128])
        dtb = sbuf(nc, st, "su_dtb", [128, H])
        alog = sbuf(nc, st, "su_alog", [128, H])
        dsk = sbuf(nc, st, "su_dsk", [128, H])
        nw = sbuf(nc, st, "su_nw", [128, 2, N])
        bbT = sbuf(nc, st, "su_bbT", [128, 2, H])
        bcp = sbuf(nc, st, "su_bcp", [128, H])
        identb = sbuf(nc, st, "su_identb", [128, 128], BF16)
        ident = sbuf(nc, st, "su_ident", [128, 128])
        x2 = sbuf(nc, st, "su_x2", [128, NT, 2, H])
        ab2 = sbuf(nc, st, "su_ab2", [128, NT, 2, H])
        dt2 = sbuf(nc, st, "su_dt2", [128, NT, 2, H])
        sg = sbuf(nc, st, "su_sg", [128, NT, 2, H])
        expa = sbuf(nc, st, "su_expa", [128, H])
        gam = sbuf(nc, st, "su_gam", [128, NT, H])
        dA = sbuf(nc, st, "su_dA", [128, 2, BATCH, H])
        cA = sbuf(nc, st, "su_cA", [128, BATCH, 2, H])
        rem = sbuf(nc, st, "su_rem", [128, BATCH, 2, H])
        cs = sbuf(nc, st, "su_cs", [128, NT, HALVES, 128], BF16)
        cT = sbuf(nc, st, "su_cT", [64, HALVES, TOK], BF16)
        sq = sbuf(nc, st, "su_sq", [128, NT, 2, N])
        ss = sbuf(nc, st, "su_ss", [128, NT, 2])
        ms = sbuf(nc, st, "su_ms", [128, NT, 2])
        rs = sbuf(nc, st, "su_rs", [128, NT, 2])
        nt = sbuf(nc, st, "su_nt", [128, NT, 2])
        nb = sbuf(nc, st, "su_nb", [128, NT, 2, N])
        vin = sbuf(nc, st, "su_vin", [128, NT, 4, 128])
        bcd = sbuf(nc, st, "su_bcd", [128, NT])
        ps = [st.enter_context(nc.psum_tensor(f"su_ps{i}", [128, 512], F32)) for i in range(6)]
        pb = [st.enter_context(nc.psum_tensor(f"su_pb{i}", [128, 1024], BF16)) for i in range(2)]
        s = semaphores(nc, st, "su_u su_small su_a_ld su_raw_ps su_raw_sb su_dve su_dt_x su_dt_l su_cA_ps su_cs su_ct_ps su_ct_sb "
                               "su_ms su_rs su_vin su_vin2 su_v_ps su_v_sb su_bc_ps su_cum su_memset su_out su_act su_expa su_bcp")
        blk = st.enter_context(nc.Block())

        @blk.sync
        def _(sp):
            sp.dma_start(uT[:, 0:TOK], ins["uT"][:, :]).then_inc(s["su_u"], 16)
            sp.dma_start(wsm[:], ins["w_small"][:, :]).then_inc(s["su_u"], 16)
            for dst, src in ((tri[:], ins["tri"][:, :]), (ident[:], ins["ident"][:, :]), (identb[:], ins["ident_b"][:, :]),
                             (dtb[:], ins["dt_bias"].partition_broadcast(128)), (alog[:], ins["A_log"].partition_broadcast(128)),
                             (dsk[:], ins["D"].partition_broadcast(128)),
                             (nw[:, 0, :], ins["B_norm"].partition_broadcast(128)), (nw[:, 1, :], ins["C_norm"].partition_broadcast(128)),
                             (bbT[0:N, 0, :], ins["B_biasT"][:, :]), (bbT[0:N, 1, :], ins["C_biasT"][:, :])):
                sp.dma_start(dst, src).then_inc(s["su_small"], 16)
            for name in ("w_theta", "w_x", "w_z", "w_out", "norm_w", "bias", "mask", "hot"):
                t = keep[name]
                sp.dma_start(t[:], ins[name]).then_inc(s["su_a_ld"], 16)
            sp.dma_start(keep["ident"][:], ins["ident"][:, :]).then_inc(s["su_a_ld"], 16)
            sp.dma_start(keep["ident_b"][:], ins["ident_b"][:, :]).then_inc(s["su_a_ld"], 16)
            sp.wait_ge(s["su_cum"], 1)
            sp.dma_start(dram["cum"][:, :], cum[:]).then_inc(s["su_out"], 16)
            sp.wait_ge(s["su_ct_sb"], 2 * 8)
            sp.dma_start(dram["cT"].rearrange("h r t -> r h t"), cT[0:CR]).then_inc(s["su_out"], 16)
            sp.wait_ge(s["su_v_sb"], NT)
            for tt in range(TB):
                for b in range(BATCH):
                    sp.dma_start(dram["v"][b, :, :, tt * TP:(tt + 1) * TP], vin[:, TB * b + tt]).then_inc(s["su_out"], 16)
            sp.wait_ge(s["su_out"], 32 + 16 * NT)
            sp.wait_ge(s["su_a_ld"], 160)

        @blk.gpsimd
        def _(pool):
            nc.gpsimd.memset(ones[:], 1.0).then_inc(s["su_memset"], 1)
            nc.gpsimd.memset(cs[:], 0.0).then_inc(s["su_memset"], 1)
            pool.wait_ge(s["su_memset"], 2)
            nc.gpsimd.memset(bbT[N:128], 0.0).then_inc(s["su_memset"], 1)
            pool.wait_ge(s["su_memset"], 3)
            nc.gpsimd.memset(bcp[N:128], 0.0).then_inc(s["su_memset"], 1)
            pool.wait_ge(s["su_memset"], 4)
            nc.gpsimd.memset(keep["LS"][0:64], 1.0).then_inc(s["su_memset"], 1)
            pool.wait_ge(s["su_memset"], 5)
            pool.wait_ge(s["su_vin"], 1)
            for k in range(2):
                for o in range(2):
                    nc.gpsimd.tensor_copy(vin[:, :, 2 * k, o * N:(o + 1) * N], nb[:, :, k, :]).then_inc(s["su_vin2"], 1)

        @blk.tensor
        def _(pe):
            pe.wait_ge(s["su_u"], 32)
            pe.wait_ge(s["su_memset"], 5)
            pe.wait_ge(s["su_dve"], 1)
            for i in range(NT):
                if i >= 4:
                    pe.wait_ge(s["su_raw_sb"], i - 3)
                o = ps[i % 4]
                nc.tensor.matmul(o[:, 0:192], uT[:, i * TP:(i + 1) * TP], wsm[:], start=True, stop=True)
                nc.tensor.matmul(o[:, 192:256], uT[:, i * TP + 1:(i + 1) * TP + 1], wsm[:, 128:192],
                                 start=True, stop=True).then_inc(s["su_raw_ps"], 1)
            pe.wait_ge(s["su_small"], 160)
            pe.wait_ge(s["su_dt_l"], 2)
            nc.tensor.matmul(ps[4][:, 0:256], tri[:], dA[:, 0], start=True, stop=True)
            nc.tensor.matmul(ps[4][:, 256:512], tri[:], dA[:, 1], start=True, stop=False)
            nc.tensor.matmul(ps[4][:, 256:512], ones[:], dA[:, 0], start=False, stop=True).then_inc(s["su_cA_ps"], 1)
            pe.wait_ge(s["su_vin"], 2)
            pe.wait_ge(s["su_vin2"], 4)
            for i in range(NT):
                if i >= 4:
                    pe.wait_ge(s["su_v_sb"], i - 3)
                else:
                    pe.wait_ge(s["su_raw_sb"], NT)
                for k in range(4):
                    last = nc.tensor.transpose(ps[i % 4][:, k * 128:(k + 1) * 128], vin[:, i, k, :], ident[:])
                last.then_inc(s["su_v_ps"], 1)
            pe.wait_ge(s["su_cs"], 1)
            for i in range(8):
                if i >= 2:
                    pe.wait_ge(s["su_ct_sb"], 2 * (i - 1))
                for q in range(4):
                    last = nc.tensor.transpose(pb[i % 2][:, q * 128:(q + 1) * 128], cs[:, 2 * i + q % 2, q // 2, :], identb[:])
                last.then_inc(s["su_ct_ps"], 1)
            pe.wait_ge(s["su_v_sb"], NT)
            pe.wait_ge(s["su_bcp"], 1)
            for i in range(NT):
                o = ps[5][:, i * H:(i + 1) * H]
                nc.tensor.matmul(o, vin[:, i, 0, :], bbT[:, 1, :], start=True, stop=False)
                nc.tensor.matmul(o, vin[:, i, 2, :], bbT[:, 0, :], start=False, stop=False)
                last = nc.tensor.matmul(o, ones[:], bcp[:], start=False, stop=True)
            last.then_inc(s["su_bc_ps"], 1)

        @blk.scalar
        def _(act):
            for i in range(NT):
                act.wait_ge(s["su_raw_ps"], i + 1)
                nc.scalar.activation(raw[:, i, :], ps[i % 4][:, 0:256], ACT.Copy).then_inc(s["su_raw_sb"], 1)
            act.wait_ge(s["su_raw_sb"], NT)
            nc.scalar.activation(sg[:, :, 0, :], raw[:, :, 160:192], ACT.Sigmoid).then_inc(s["su_act"], 1)
            nc.scalar.activation(sg[:, :, 1, :], raw[:, :, 224:256], ACT.Sigmoid, scale=-1.0).then_inc(s["su_act"], 1)
            act.wait_ge(s["su_ms"], 1)
            nc.scalar.activation(rs[:], nt[:], ACT.Sqrt).then_inc(s["su_rs"], 1)
            act.wait_ge(s["su_small"], 160)
            nc.scalar.activation(expa[:], alog[:], ACT.Exp).then_inc(s["su_expa"], 1)
            act.wait_ge(s["su_dt_x"], 1)
            nc.scalar.activation(ab2[:], ab2[:], ACT.Exp, scale=-1.0).then_inc(s["su_act"], 1)
            act.wait_ge(s["su_act"], 3)
            nc.scalar.activation(ab2[:], ab2[:], ACT.Ln, bias=1.0).then_inc(s["su_dt_l"], 1)
            for i in range(NT):
                act.wait_ge(s["su_v_ps"], i + 1)
                nc.scalar.activation(vin[:, i], ps[i % 4][:].rearrange("p (k t) -> p k t", k=4), ACT.Copy).then_inc(s["su_v_sb"], 1)

        @blk.vector
        def _(dve):
            chain = [0]

            def link(ins_):
                chain[0] += 1
                ins_.then_inc(s["su_dve"], 1)
                dve.wait_ge(s["su_dve"], chain[0])

            V = nc.vector
            link(V.memset(uT[:, TOK:TOK + 1], 0.0))
            link(V.memset(uni[:], 1.0))
            dve.wait_ge(s["su_u"], 32)
            for b in range(BATCH):
                V.tensor_tensor_scan(cum[:, b * L:(b + 1) * L], uni[:], uT[:, b * L:(b + 1) * L],
                                     0.0, ALU.mult, ALU.add).then_inc(s["su_dve"], 1)
            chain[0] += BATCH
            dve.wait_ge(s["su_dve"], chain[0])
            V.tensor_scalar(cum[:], cum[:], float(1 / (2 * np.pi)), None, ALU.mult).then_inc(s["su_cum"], 1)
            dve.wait_ge(s["su_small"], 160)
            dve.wait_ge(s["su_memset"], 5)
            V.tensor_tensor(bcp[0:N], bbT[0:N, 0, :], bbT[0:N, 1, :], ALU.mult).then_inc(s["su_bcp"], 1)
            dve.wait_ge(s["su_raw_sb"], NT)
            bc = raw[:, :, 0:2 * N].rearrange("p t (k n) -> p t k n", k=2)
            link(V.tensor_tensor(sq[:], bc, bc, ALU.mult))
            link(V.tensor_reduce(ss[:], sq[:], AX.X, ALU.add))
            link(V.tensor_scalar(ms[:], ss[:], 1.0 / N, EPS, ALU.mult, ALU.add))
            V.reciprocal(nt[:], ms[:]).then_inc(s["su_ms"], 1)
            for k in range(2):
                c = 128 + 64 * k
                link(V.tensor_tensor(x2[:, :, k, :], raw[:, :, c:c + H], dtb[:].unsqueeze(1).to_broadcast([128, NT, H]), ALU.add))
            link(V.tensor_scalar(dt2[:], x2[:], -1.0, None, ALU.mult))
            V.tensor_tensor(ab2[:], x2[:], dt2[:], ALU.max).then_inc(s["su_dt_x"], 1)
            dve.wait_ge(s["su_rs"], 1)
            link(V.tensor_tensor(nt[:], rs[:], rs[:], ALU.mult))
            link(V.tensor_tensor(nt[:], nt[:], ms[:], ALU.mult))
            link(V.tensor_scalar(nt[:], nt[:], -0.5, 1.5, ALU.mult, ALU.add))
            link(V.tensor_tensor(rs[:], rs[:], nt[:], ALU.mult))
            link(V.tensor_tensor(nb[:], bc, rs[:].unsqueeze(3).to_broadcast([128, NT, 2, N]), ALU.mult))
            V.tensor_tensor(nb[:], nb[:], nw[:].unsqueeze(1).to_broadcast([128, NT, 2, N]), ALU.mult).then_inc(s["su_vin"], 1)
            dve.wait_ge(s["su_vin"], 1)
            for k in range(2):
                for o in range(2):
                    link(V.tensor_scalar(vin[:, :, 2 * k + 1, 64 * o:64 * o + NH], nb[:, :, k, NH:N], -1.0, None, ALU.mult))
                    link(V.tensor_copy(vin[:, :, 2 * k + 1, 64 * o + NH:64 * o + N], nb[:, :, k, 0:NH]))
            V.tensor_tensor(sq[:, :, 0, :], nb[:, :, 0, :], nb[:, :, 1, :], ALU.mult).then_inc(s["su_vin"], 1)
            dve.wait_ge(s["su_dt_l"], 1)
            dve.wait_ge(s["su_act"], 3)
            dve.wait_ge(s["su_expa"], 1)
            link(V.scalar_tensor_tensor(dt2[:], x2[:], 0.0, ab2[:], ALU.max, ALU.add))
            link(V.tensor_tensor(gam[:], sg[:, :, 0, :], dt2[:, :, 0, :], ALU.mult))
            link(V.tensor_tensor(sg[:, :, 1, :], sg[:, :, 1, :], dt2[:, :, 1, :], ALU.mult))
            link(V.tensor_tensor(keep["w"][:], gam[:], sg[:, :, 1, :], ALU.add))
            for a in range(2):
                ins_ = V.scalar_tensor_tensor(dA[:, a], dt2[:, :, 0, :].rearrange("p (b a) h -> p b a h", a=2)[:, :, a, :],
                                              -1.0, expa[:].unsqueeze(1).to_broadcast([128, BATCH, H]), ALU.mult, ALU.mult)
                if a == 0:
                    link(ins_)
                else:
                    ins_.then_inc(s["su_dt_l"], 1)
            dve.wait_ge(s["su_cA_ps"], 1)
            link(V.tensor_copy(cA[:].rearrange("p b a h -> p a b h"), ps[4][:].rearrange("p (a b h) -> p a b h", a=2, h=H)))
            ca = cA[:].rearrange("p b a (f h) -> p (b a) f h", f=HALVES)
            re = rem[:].rearrange("p b a (f h) -> p (b a) f h", f=HALVES)
            part = [cs[:, :, :, k * HU:(k + 1) * HU] for k in range(3)]
            link(V.tensor_copy(part[0], ca))
            link(V.tensor_tensor(re, ca, part[0], ALU.subtract))
            link(V.tensor_copy(part[1], re))
            link(V.tensor_tensor(re, re, part[1], ALU.subtract))
            link(V.tensor_copy(part[2], re))
            V.tensor_scalar(cs[:, :, :, CN:CN + CR], cs[:, :, :, 0:CR], -1.0, None, ALU.mult).then_inc(s["su_cs"], 1)
            for i in range(8):
                dve.wait_ge(s["su_ct_ps"], i + 1)
                src = pb[i % 2][:, 0:512].rearrange("p (f t) -> p f t", f=2)
                V.tensor_copy(cT[:, :, i * 256:(i + 1) * 256], src[0:64]).then_inc(s["su_ct_sb"], 1)
                V.tensor_copy(keep["LS"][64:128, :, i * 256:(i + 1) * 256], src[64:128]).then_inc(s["su_ct_sb"], 1)
            dve.wait_ge(s["su_vin"], 2)
            link(V.tensor_reduce(bcd[:], sq[:, :, 0, :], AX.X, ALU.add))
            dve.wait_ge(s["su_bc_ps"], 1)
            own = keep["own"]
            link(V.tensor_tensor(own[:], ps[5][:].rearrange("p (t h) -> p t h", h=H), bcd[:].unsqueeze(2).to_broadcast([128, NT, H]), ALU.add))
            link(V.tensor_tensor(own[:], own[:], gam[:], ALU.mult))
            link(V.tensor_tensor(own[:], own[:], dsk[:].unsqueeze(1).to_broadcast([128, NT, H]), ALU.add))
            dve.wait_ge(s["su_a_ld"], 160)
            for k in (1, 3):
                for q in (0, 64):
                    link(V.tensor_scalar(keep["bias"][q:q + NH, k, :], keep["bias"][q:q + NH, k, :], -1.0, None, ALU.mult))
            dve.wait_ge(s["su_a_ld"], 160)
            link(V.tensor_tensor(keep["w_out"][:], keep["w_out"][:], keep["norm_w"][:].unsqueeze(2).to_broadcast([128, DI // 128, DM]), ALU.mult))


def attention_phase(nc, ins, keep, dram):
    AHEAD = 7
    RING = AHEAD + 1
    FIRST = 4
    EXPS = [[] for _ in range(HU)]
    for i in range(HU):
        EXPS[FIRST + i * (HU - FIRST) // HU].append(AHEAD + i)
    TURN = {2 * j + 5: j for j in range(PU - 2)}
    st = ExitStack()
    with st:
        ub = sbuf(nc, st, "at_u", [128, L])
        cb_ = sbuf(nc, st, "at_cum", [128, L])
        v = sbuf(nc, st, "at_v", [128, 4, L])
        rh = [sbuf(nc, st, f"at_rh{i}", [128, HU, L], BF16) for i in range(2)]
        km = sbuf(nc, st, "at_km", [128, 512])
        sn = sbuf(nc, st, "at_sin", [128, 4, 512])
        co = sbuf(nc, st, "at_cos", [128, 4, 512])
        tmp = sbuf(nc, st, "at_tmp", [128, 2, 4, L])
        Br = sbuf(nc, st, "at_B", [128, PU, L])
        Cr = sbuf(nc, st, "at_C", [128, PU, 2, L])
        ex = sbuf(nc, st, "at_ex", [128, RING, W_S])
        G = sbuf(nc, st, "at_G", [128, 2, W_S])
        xw = sbuf(nc, st, "at_xw", [128, 2, TB, DU])
        xo = sbuf(nc, st, "at_xo", [128, 2, TB, DU])
        sz = sbuf(nc, st, "at_sz", [128, 2, TB, DU])
        yz = sbuf(nc, st, "at_yz", [128, TB, DU])
        yT = sbuf(nc, st, "at_yT", [128, PU, L])
        junk = sbuf(nc, st, "at_junk", [128, DU // 2], BF16)
        pp, pc, pe_ = ([st.enter_context(nc.psum_tensor(f"at_{n}{i}", [128, 512], F32)) for i in range(2)] for n in ("pp", "pc", "pe"))
        py = st.enter_context(nc.psum_tensor("at_py", [128, 512], F32))
        pt = st.enter_context(nc.psum_tensor("at_pt", [128, 512], F32))
        s = semaphores(nc, st, "c_zero c_low u_in cum_in v_in rh_in0 rh_in1 zeroed th_ps z_ps x_ps km_ok r_ok abs_ok sc_ok zc_ok silu_ok "
                               "xw_ok xs_ok xo_ok rope_ok b_ok c_ok e_ps e_ok c_ps g_ok y_ps y1_ok y2_ok t_ps t_ok sq_ok o_ps o_ok")
        blk = st.enter_context(nc.Block())
        w_theta, w_x, w_z, w_out = keep["w_theta"], keep["w_x"], keep["w_z"], keep["w_out"]
        bias, mask, identb, ident, LS = keep["bias"], keep["mask"], keep["ident_b"], keep["ident"], keep["LS"]

        def slots(eng, slot):
            slot(0, 0, 0, 0, 1)
            with eng.Fori(1, BATCH - 1) as b:
                slot(2 * b - 1, 1, b - 1, b, b)
                slot(2 * b, 0, b, b, b + 1)
            slot(UNITS - 3, 1, BATCH - 2, BATCH - 1, BATCH - 1)
            slot(UNITS - 2, 0, BATCH - 1, BATCH - 1, None)
            slot(UNITS - 1, 1, BATCH - 1, None, None)

        @blk.sync
        def _(sp):
            sp.wait_ge(s["zeroed"], 2)

            def load_sums(b):
                sp.dma_start(cb_[:], dram["cum"][:, bass.ds(b * L, L)]).then_inc(s["cum_in"], 16)

            def load_u(b):
                sp.dma_start(ub[:], ins["uT"][:, bass.ds(b * L, L)]).then_inc(s["u_in"], 16)

            def load_rows(b):
                sp.dma_start(v[:], dram["v"][bass.ds(b, 1)].rearrange("o p k t -> (o p) k t")).then_inc(s["v_in"], 16)

            def load_decays(par, b):
                for h in range(HU):
                    sp.dma_start(rh[par][h:CR:HU, h, :], dram["cT"][par, h:CR:HU, bass.ds(b * L, L)]).then_inc(s[f"rh_in{par}"], 16)

            def slot(n, par, bn, ba, bc):
                if ba is None:
                    return
                if not first(n):
                    sp.wait_ge(s["e_ps"], HU * n)
                load_decays(1 - par, ba)
                if par == 0 and bc is not None:
                    sp.wait_ge(s["th_ps"], 4 * (n + 2))
                    load_sums(bn + 1)
                    sp.wait_ge(s["z_ps"], 4 * (n + 2))
                    load_u(bn + 1)
                    sp.wait_ge(s["rope_ok"], PU * (n + 2))
                    load_rows(bn + 1)

            load_sums(0)
            load_u(0)
            load_rows(0)
            load_decays(0, 0)
            slots(sp, slot)

        @blk.tensor
        def _(pe):
            def angles(a, par, b, q):
                if q == 0:
                    pe.wait_ge(s["cum_in"], 16 * (b + 1))
                if q >= 2:
                    pe.wait_ge(s["r_ok"], 4 * a + q - 1)
                elif not first(a):
                    pe.wait_ge(s["zc_ok"], 4 * a + q - 1)
                for k in range(2):
                    j = par * PU + 2 * q + k
                    last = nc.tensor.matmul(pp[q % 2][:, k * L:(k + 1) * L], w_theta[:, j * 128:(j + 1) * 128], cb_[:],
                                            start=True, stop=True)
                last.then_inc(s["th_ps"], 1)

            def project(a, par, b, q, w_, ready, done, before):
                tt, c = divmod(q, 2)
                if q < 2:
                    pe.wait_ge(s[before], 4 * a + q + 3)
                else:
                    pe.wait_ge(s[done], 4 * a + q - 1)
                if done == "xs_ok" and q == 0:
                    pe.wait_ge(s["u_in"], 16 * (b + 1))
                o = par * DU + c * 512
                nc.tensor.matmul(pp[q % 2][:], ub[:, tt * TP:(tt + 1) * TP], w_[:, o:o + 512], start=True, stop=True).then_inc(s[ready], 1)

            def decay(n, par, b, h):
                if h == 0:
                    pe.wait_ge(s[f"rh_in{par}"], 16 * HU * (b + 1))
                if not (first(n) and h < 2):
                    pe.wait_ge(s["e_ok"], HU * n + h - 1)
                e = pe_[h % 2]
                nc.tensor.matmul(e[:, 0:L], LS[:, par, bass.ds(b * L, TP)], rh[par][:, h, :], start=True, stop=False)
                nc.tensor.matmul(e[:, 0:TP], identb[:], mask[:], start=False, stop=True)
                nc.tensor.matmul(e[:, L:W_S], LS[:, par, bass.ds(b * L + TP, TP)], rh[par][:, h, TP:L], start=True, stop=False)
                nc.tensor.matmul(e[:, L:W_S], identb[:], mask[:], start=False, stop=True).then_inc(s["e_ps"], 1)

            def scores(n, h):
                j, k = divmod(h, 2)
                if k == 0:
                    pe.wait_ge(s["c_ok"], PU * n + j + 1)
                if not (first(n) and h < 2):
                    pe.wait_ge(s["g_ok"], HU * n + h - 1)
                c = pc[h % 2]
                nc.tensor.matmul(c[:, 0:L], Br[:, j, 0:TP], Cr[:, j, k, :], start=True, stop=True)
                nc.tensor.matmul(c[:, L:W_S], Br[:, j, TP:L], Cr[:, j, k, TP:L], start=True, stop=True).then_inc(s["c_ps"], 1)

            def output(n, par, h):
                j, k = divmod(h, 2)
                if h == 0:
                    pe.wait_ge(s["xw_ok"], 4 * n + 4)
                pe.wait_ge(s["g_ok"], HU * n + h + 1)
                if k == 0 and not (first(n) and j == 0):
                    pe.wait_ge(s["y1_ok"], PU * n + j)
                y = py[:, 0:L].rearrange("p (a c) -> p a c", a=TB)[:, :, k * P:(k + 1) * P]
                g = G[:, h % 2]
                c = slice(h * P, (h + 1) * P)
                nc.tensor.matmul(y[:, 0], g[:, 0:TP], xw[:, par, 0, c], start=True, stop=True)
                nc.tensor.matmul(y[:, 1], g[:, TP:L], xw[:, par, 0, c], start=True, stop=False)
                nc.tensor.matmul(y[:, 1], g[:, L:W_S], xw[:, par, 1, c], start=False, stop=True).then_inc(s["y_ps"], 1)

            def turn(n, j):
                pe.wait_ge(s["y2_ok"], PU * n + j + 1)
                if j > 0:
                    pe.wait_ge(s["t_ok"], PU * n + j)
                elif not first(n):
                    pe.wait_ge(s["o_ok"], n)
                for tt in range(TB):
                    last = nc.tensor.transpose(pt[:, tt * TP:(tt + 1) * TP], yz[:, tt, j * 128:(j + 1) * 128], ident[:])
                last.then_inc(s["t_ps"], 1)

            def project_out(n, par):
                pe.wait_ge(s["t_ok"], PU * n + PU)
                for k in range(PU):
                    last = nc.tensor.matmul(pt[:, 0:L], w_out[:, par * PU + k, :], yT[:, k, :], start=(k == 0), stop=(k == PU - 1))
                last.then_inc(s["o_ps"], 1)

            def slot(n, par, bn, ba, bc):
                a, pa = n + 1, 1 - par
                for h in range(HU):
                    scores(n, h)
                    if h >= 1:
                        output(n, par, h - 1)
                    elif not first(n):
                        output(n - 1, pa, HU - 1)
                    if h < 2 and ba is not None:
                        angles(a, pa, ba, 2 + h)
                    if h >= HU - 2 and bc is not None:
                        angles(n + 2, par, bc, h - (HU - 2))
                    if not first(n):
                        if h in (1, 2):
                            turn(n - 1, PU - 3 + h)
                        if h == 4:
                            project_out(n - 1, pa)
                    if h in TURN:
                        turn(n, TURN[h])
                    for i in EXPS[h]:
                        if i < HU:
                            decay(n, par, bn, i)
                        elif ba is not None:
                            decay(a, pa, ba, i - HU)
                    if ba is not None:
                        if 5 <= h < 9:
                            project(a, pa, ba, h - 5, w_x, "x_ps", "xs_ok", "r_ok")
                        elif 9 <= h < 13:
                            project(a, pa, ba, h - 9, w_z, "z_ps", "zc_ok", "xs_ok")

            for q in range(4):
                angles(0, 0, 0, q)
            for q in range(4):
                project(0, 0, 0, q, w_x, "x_ps", "xs_ok", "r_ok")
            for q in range(4):
                project(0, 0, 0, q, w_z, "z_ps", "zc_ok", "xs_ok")
            for h in range(AHEAD):
                decay(0, 0, 0, h)
            angles(1, 1, 0, 0)
            angles(1, 1, 0, 1)
            slots(pe, slot)
            n = UNITS - 1
            output(n, 1, HU - 1)
            turn(n, PU - 2)
            turn(n, PU - 1)
            project_out(n, 1)

        @blk.scalar
        def _(act):
            def angles(a, q):
                act.wait_ge(s["r_ok"], 4 * a + q + 1)
                if not first(a):
                    act.wait_ge(s["rope_ok"], PU * (a - 1) + 2 * q + 2)
                nc.scalar.activation(co[:, q, :], sn[:, q, :], ACT.Abs).then_inc(s["abs_ok"], 1)
                act.wait_ge(s["abs_ok"], 4 * a + q + 1)
                nc.scalar.activation(sn[:, q, :], sn[:, q, :], ACT.Sin, scale=-TWO_PI).then_inc(s["sc_ok"], 1)
                nc.scalar.activation(co[:, q, :], co[:, q, :], ACT.Sin, scale=-TWO_PI, bias=keep["half_pi"][:, 0:1]).then_inc(s["sc_ok"], 1)

            def keep_x(a, pa, q):
                tt, c = divmod(q, 2)
                act.wait_ge(s["x_ps"], 4 * a + q + 1)
                if q == 0 and not first(a) and not (isinstance(a, int) and a == 1):
                    act.wait_ge(s["y1_ok"], PU * (a - 1))
                nc.scalar.activation(xo[:, pa, tt, c * 512:(c + 1) * 512], pp[q % 2][:], ACT.Copy).then_inc(s["xs_ok"], 1)

            def keep_z(a, pa, q):
                tt, c = divmod(q, 2)
                act.wait_ge(s["z_ps"], 4 * a + q + 1)
                if q == 0 and not first(a) and not (isinstance(a, int) and a == 1):
                    act.wait_ge(s["y2_ok"], PU * (a - 1))
                nc.scalar.activation(sz[:, pa, tt, c * 512:(c + 1) * 512], pp[q % 2][:], ACT.Copy).then_inc(s["zc_ok"], 1)

            def silu(n, par):
                act.wait_ge(s["zc_ok"], 4 * n + 4)
                for tt in range(TB):
                    nc.scalar.activation(sz[:, par, tt, :], sz[:, par, tt, :], ACT.Silu).then_inc(s["silu_ok"], 1)

            def decay(n, h):
                act.wait_ge(s["e_ps"], HU * n + h + 1)
                if not (first(n) and h < RING):
                    act.wait_ge(s["g_ok"], HU * n + h + 1 - RING)
                nc.scalar.activation(ex[:, h % RING], pe_[h % 2][:, 0:W_S], ACT.Exp).then_inc(s["e_ok"], 1)

            def turn(n, j):
                act.wait_ge(s["t_ps"], PU * n + j + 1)
                if j == 0 and not first(n):
                    act.wait_ge(s["o_ps"], n)
                nc.scalar.activation(yT[:, j, :], pt[:, 0:L], ACT.Copy).then_inc(s["t_ok"], 1)

            def squares(n, f):
                act.wait_ge(s["y2_ok"], PU * n + PU // 2 * (f + 1))
                for tt in range(TB):
                    if f or tt or not first(n):
                        act.wait_ge(s["sq_ok"], 2 * TB * n + TB * f + tt)
                    nc.scalar.activation(junk[:], yz[:, tt, f * 512:(f + 1) * 512], ACT.Square,
                                         accum_out=keep["ssq"][:, bass.ds(2 * TB * n + TB * f + tt, 1)]).then_inc(s["sq_ok"], 1)

            def slot(n, par, bn, ba, bc):
                a, pa = n + 1, 1 - par
                silu(n, par)
                for q in range(4):
                    if ba is not None:
                        angles(a, q)
                    if not first(n):
                        if q < 2:
                            turn(n - 1, PU - 2 + q)
                        if q == 1:
                            squares(n - 1, 1)
                for h in range(FIRST, HU):
                    if h in TURN:
                        turn(n, TURN[h])
                    for i in EXPS[h]:
                        if i < HU:
                            decay(n, i)
                        elif ba is not None:
                            decay(a, i - HU)
                    if h == 12:
                        squares(n, 0)
                    if ba is not None:
                        if 5 <= h < 9:
                            keep_x(a, pa, h - 5)
                        elif 9 <= h < 13:
                            keep_z(a, pa, h - 9)

            for q in range(4):
                angles(0, q)
            for q in range(4):
                keep_x(0, 0, q)
            for q in range(4):
                keep_z(0, 0, q)
            for h in range(AHEAD):
                decay(0, h)
            slots(act, slot)
            n = UNITS - 1
            turn(n, PU - 2)
            turn(n, PU - 1)
            squares(n, 1)

        @blk.gpsimd
        def _(pool):
            nc.gpsimd.memset(Cr[0:64, :, 1, :], 0.0).then_inc(s["c_zero"], 1)
            pool.wait_ge(s["c_zero"], 1)
            nc.gpsimd.memset(Cr[64:128, :, 0, :], 0.0).then_inc(s["c_zero"], 1)
            pool.wait_ge(s["c_zero"], 2)

            def scale_x(a, pa, b, q):
                tt, c = divmod(q, 2)
                x3 = xo[:, pa, tt, c * 512:(c + 1) * 512].rearrange("p (h e) -> p h e", e=P)
                xw3 = xw[:, pa, tt, c * 512:(c + 1) * 512].rearrange("p (h e) -> p h e", e=P)
                w8, own8 = (keep[k][:, bass.ds(TB * b + tt, 1), pa * HU + c * 8:pa * HU + c * 8 + 8].rearrange("p o h -> p (o h)")
                            .unsqueeze(2).to_broadcast([128, 8, P]) for k in ("w", "own"))
                pool.wait_ge(s["xs_ok"], 4 * a + q + 1)
                if q == 0 and not first(a) and not (isinstance(a, int) and a == 1):
                    pool.wait_ge(s["y_ps"], HU * (a - 1))
                nc.gpsimd.tensor_tensor(xw3, x3, w8, ALU.mult).then_inc(s["xw_ok"], 1)
                nc.gpsimd.tensor_tensor(x3, x3, own8, ALU.mult).then_inc(s["xo_ok"], 1)

            def rotate(a, j):
                t = tmp[:, j % 2]
                pool.wait_ge(s["rope_ok"], PU * a + j + 1)
                if not first(a):
                    pool.wait_ge(s["c_ps"], HU * (a - 1) + 2 * j + 2)
                nc.gpsimd.tensor_tensor(Br[:, j, :], t[:, 0], t[:, 1], ALU.add).then_inc(s["b_ok"], 1)
                pool.wait_ge(s["b_ok"], PU * a + j + 1)
                nc.gpsimd.tensor_tensor(Cr[0:64, j, 0, :], t[0:64, 2], t[0:64, 3], ALU.add).then_inc(s["c_low"], 1)
                pool.wait_ge(s["c_low"], PU * a + j + 1)
                nc.gpsimd.tensor_tensor(Cr[64:128, j, 1, :], t[64:128, 2], t[64:128, 3], ALU.add).then_inc(s["c_ok"], 1)
                pool.wait_ge(s["c_ok"], PU * a + j + 1)

            def unit(a, pa, b):
                for j in range(PU):
                    rotate(a, j)
                    if 1 <= j < 5:
                        scale_x(a, pa, b, j - 1)

            def slot(n, par, bn, ba, bc):
                if ba is not None:
                    unit(n + 1, 1 - par, ba)

            unit(0, 0, 0)
            slots(pool, slot)

        @blk.vector
        def _(dve):
            V = nc.vector
            for i in range(2):
                V.memset(rh[i][0:64], 0.0).then_inc(s["zeroed"], 1)
                V.tensor_copy(rh[i][64:128], keep["hot"][64:128].unsqueeze(2).to_broadcast([64, HU, L])).then_inc(s["km_ok"], 1)

            def fold(a, q):
                dve.wait_ge(s["th_ps"], 4 * a + q + 1)
                if q > 0 or not first(a):
                    dve.wait_ge(s["r_ok"], 4 * a + q)
                V.tensor_scalar(km[:], pp[q % 2][:], ROUND, None, ALU.add).then_inc(s["km_ok"], 1)
                dve.wait_ge(s["km_ok"], 2 + 4 * a + q + 1)
                if not first(a):
                    dve.wait_ge(s["rope_ok"], PU * (a - 1) + 2 * q + 2)
                V.scalar_tensor_tensor(sn[:, q, :], km[:], ROUND, pp[q % 2][:], ALU.subtract, ALU.subtract).then_inc(s["r_ok"], 1)

            def rotate(a, pa, b, j):
                q, k = divmod(j, 2)
                J = pa * PU + j
                dve.wait_ge(s["sc_ok"], 8 * a + 2 * q + 2)
                if j == 0:
                    dve.wait_ge(s["v_in"], 16 * (b + 1))
                if not (first(a) and j < 2):
                    dve.wait_ge(s["c_ok"], PU * a + j - 1)
                for kind in range(4):
                    angle = (co, sn)[kind % 2][:, q, k * L:(k + 1) * L]
                    last = V.scalar_tensor_tensor(tmp[:, j % 2, kind], v[:, kind, :], bias[:, kind, J:J + 1], angle, ALU.add, ALU.mult)
                last.then_inc(s["rope_ok"], 1)

            def weigh(n, h):
                dve.wait_ge(s["e_ok"], HU * n + h + 1)
                dve.wait_ge(s["c_ps"], HU * n + h + 1)
                if not (first(n) and h < 2):
                    dve.wait_ge(s["y_ps"], HU * n + h - 1)
                V.tensor_tensor(G[:, h % 2], pc[h % 2][:, 0:W_S], ex[:, h % RING], ALU.mult).then_inc(s["g_ok"], 1)

            def gate(n, par, j):
                c = slice(j * 128, (j + 1) * 128)
                dve.wait_ge(s["y_ps"], HU * n + 2 * j + 2)
                if j == 0:
                    dve.wait_ge(s["xo_ok"], 4 * n + 4)
                    if not first(n):
                        dve.wait_ge(s["t_ps"], PU * n)
                        dve.wait_ge(s["sq_ok"], 2 * TB * n - TB)
                if j == PU // 2 and not first(n):
                    dve.wait_ge(s["sq_ok"], 2 * TB * n)
                V.tensor_tensor(yz[:, :, c], py[:, 0:L].rearrange("p (a c) -> p a c", a=TB), xo[:, par, :, c], ALU.add).then_inc(s["y1_ok"], 1)
                dve.wait_ge(s["y1_ok"], PU * n + j + 1)
                dve.wait_ge(s["silu_ok"], TB * n + TB)
                V.tensor_tensor(yz[:, :, c], yz[:, :, c], sz[:, par, :, c], ALU.mult).then_inc(s["y2_ok"], 1)

            def collect(n, par, b):
                dve.wait_ge(s["o_ps"], n + 1)
                att = keep["att"][:, bass.ds(b * L, L)]
                if par == 0:
                    V.tensor_copy(att, pt[:, 0:L]).then_inc(s["o_ok"], 1)
                else:
                    dve.wait_ge(s["o_ok"], n)
                    V.tensor_tensor(att, pt[:, 0:L], att, ALU.add).then_inc(s["o_ok"], 1)

            def slot(n, par, bn, ba, bc):
                a, pa = n + 1, 1 - par
                for h in range(HU):
                    weigh(n, h)
                    if h % 2 == 0:
                        if h >= 2:
                            gate(n, par, h // 2 - 1)
                        elif not first(n):
                            gate(n - 1, pa, PU - 1)
                    if h < 2 and ba is not None:
                        fold(a, 2 + h)
                    if h == 5 and not first(n):
                        collect(n - 1, pa, bn if par == 1 else bn - 1)
                    if h % 2 == 1 and h >= 3 and ba is not None:
                        rotate(a, pa, ba, (h - 3) // 2)
                    if h >= HU - 2 and bc is not None:
                        fold(n + 2, h - (HU - 2))
                if ba is not None:
                    rotate(a, pa, ba, PU - 1)

            for q in range(4):
                fold(0, q)
            for j in range(PU):
                rotate(0, 0, 0, j)
            fold(1, 0)
            fold(1, 1)
            slots(dve, slot)
            n = UNITS - 1
            gate(n, 1, PU - 1)
            collect(n, 1, BATCH - 1)


def first(n):
    return isinstance(n, int) and n == 0


def moe_phase(nc, ins, keep, out):
    st = ExitStack()
    with st:
        u = sbuf(nc, st, "mo_u", [128, NT, DM])
        xr = sbuf(nc, st, "mo_x", [128, NT, DM])
        sq = sbuf(nc, st, "mo_sq", [128, NT, DM])
        x1T = sbuf(nc, st, "mo_xT", [128, TOK])
        wg = sbuf(nc, st, "mo_wg", [128, EXP])
        w1 = sbuf(nc, st, "mo_w1", [128, 2, FF])
        w2 = sbuf(nc, st, "mo_w2", [128, 2, FF // 128, DM])
        low = sbuf(nc, st, "mo_low", [128, 128], BF16)
        oneb = sbuf(nc, st, "mo_oneb", [128, 128], BF16)
        pref = sbuf(nc, st, "mo_pref", [128, EXP])
        half = sbuf(nc, st, "mo_half", [128, NT])
        tot = sbuf(nc, st, "mo_tot", [128, NT])
        rs = sbuf(nc, st, "mo_rs", [128, NT])
        t1 = sbuf(nc, st, "mo_t1", [128, NT])
        lg = sbuf(nc, st, "mo_lg", [128, NT, EXP])
        m12 = sbuf(nc, st, "mo_m12", [128, 2, NT])
        km = sbuf(nc, st, "mo_km", [128, NT])
        ky = sbuf(nc, st, "mo_ky", [128, NT, EXP])
        oh = sbuf(nc, st, "mo_oh", [128, 2, NT, EXP])
        ohb = sbuf(nc, st, "mo_ohb", [128, 2, NT, EXP], BF16)
        pr = sbuf(nc, st, "mo_pr", [128, 2, NT])
        rk = sbuf(nc, st, "mo_rk", [128, 2, NT, EXP])
        sa = sbuf(nc, st, "mo_sa", [128, 2, NT + 1, EXP])
        sb_ = sbuf(nc, st, "mo_sb", [128, 2, NT + 1, EXP])
        gate = sbuf(nc, st, "mo_gate", [128, EXP, NT])
        hr = sbuf(nc, st, "mo_hr", [128, 2, 512])
        hh = sbuf(nc, st, "mo_hh", [128, 2, FF // 128, 512])
        acc = sbuf(nc, st, "mo_acc", [128, NT, DM])
        pu = [st.enter_context(nc.psum_tensor(f"mo_pu{i}", [128, 512], F32)) for i in range(4)]
        pd = [st.enter_context(nc.psum_tensor(f"mo_pd{i}", [128, 4, DM], F32)) for i in range(2)]
        pr_ = [st.enter_context(nc.psum_tensor(f"mo_pr{i}", [128, 512], F32)) for i in range(2)]
        s = semaphores(nc, st, "m_at_ps m_in m_dve m_ms m_rs m_x1 m_xt_ps m_xt m_lg_ps m_oh m_rk_ps m_e m_e2 m_gate w_in0 w_in1 up_ps relu_ok h_ok "
                               "dn_ps dn_ok m_var m_std m_out m_store m_act")
        blk = st.enter_context(nc.Block())
        KF = FF // 128
        GR = TOK // 512

        @blk.sync
        def _(sp):
            for dst, src in ((u[:], ins["u"].rearrange("(t p) c -> p t c", p=128)), (wg[:], ins["w_g"][:, :]), (low[:], ins["low"][:, :]),
                             (pref[:], ins["pref"].partition_broadcast(128))):
                sp.dma_start(dst, src).then_inc(s["m_in"], 16)

            def load(e, k):
                sp.dma_start(w1[:, k], ins["c_fc"][bass.ds(e, 1)].rearrange("o c f -> (o c) f")).then_inc(s[f"w_in{k}"], 16)
                sp.dma_start(w2[:, k], ins["c_proj"][bass.ds(e, 1)].rearrange("o (k p) c -> p (o k) c", p=128)).then_inc(s[f"w_in{k}"], 16)

            load(0, 0)
            load(1, 1)
            with sp.Fori(1, EXP // 2) as e:
                for k in range(2):
                    sp.wait_ge(s["dn_ps"], GR * (2 * e + k - 1))
                    load(2 * e + k, k)
            for g in range(GR):
                sp.wait_ge(s["m_out"], g + 1)
                sp.dma_start(out.rearrange("(t p) c -> p t c", p=128)[:, 4 * g:4 * g + 4, :], sq[:, 4 * g:4 * g + 4, :]).then_inc(s["m_store"], 16)
            sp.wait_ge(s["m_store"], 16 * GR)

        @blk.gpsimd
        def _(pool):
            nc.gpsimd.memset(oneb[:], 1.0).then_inc(s["m_e"], 1)
            nc.gpsimd.memset(sa[:], 0.0).then_inc(s["m_e"], 1)
            nc.gpsimd.memset(acc[:], 0.0).then_inc(s["m_e"], 1)

        @blk.tensor
        def _(pe):
            for i in range(NT):
                last = nc.tensor.transpose(pu[i // 4][:, (i % 4) * 128:(i % 4 + 1) * 128], keep["att"][:, i * 128:(i + 1) * 128],
                                           keep["ident"][:])
            last.then_inc(s["m_at_ps"], 1)
            for i in range(NT):
                if i % 4 == 0:
                    pe.wait_ge(s["m_x1"], i // 4 + 1)
                last = nc.tensor.transpose(pu[i // 4][:, (i % 4) * 128:(i % 4 + 1) * 128], xr[:, i, :], keep["ident"][:])
                if i % 4 == 3:
                    last.then_inc(s["m_xt_ps"], 1)
            for i in range(NT):
                if i % 4 == 0:
                    pe.wait_ge(s["m_xt"], i // 4 + 1)
                last = nc.tensor.matmul(pr_[0][:, i * EXP:(i + 1) * EXP], x1T[:, i * 128:(i + 1) * 128], wg[:], start=True, stop=True)
            last.then_inc(s["m_lg_ps"], 1)
            pe.wait_ge(s["m_oh"], 1)
            pe.wait_ge(s["m_e"], 1)
            nc.tensor.matmul(pr_[1][:, 0:256], low[:], ohb[:].rearrange("p k t e -> p (k t e)"), start=True, stop=True)
            nc.tensor.matmul(pr_[1][:, 256:512], oneb[:], ohb[:].rearrange("p k t e -> p (k t e)"), start=True, stop=True).then_inc(s["m_rk_ps"], 1)

            def up(c, k, g):
                for f in range(KF):
                    i = KF * c + KF * g + f
                    if not (isinstance(c, int) and c == 0 and g == 0):
                        pe.wait_ge(s["relu_ok"], i - KF + 1)
                    nc.tensor.matmul(pu[f][:], w1[:, k, f * 128:(f + 1) * 128], x1T[:, g * 512:(g + 1) * 512],
                                     start=True, stop=True).then_inc(s["up_ps"], 1)

            def down(c, k, g):
                if not (isinstance(c, int) and c == 0 and g < 2):
                    pe.wait_ge(s["dn_ok"], c + g - 1)
                pe.wait_ge(s["h_ok"], KF * (c + g + 1))
                for tt in range(4):
                    for f in range(KF):
                        last = nc.tensor.matmul(pd[g % 2][:, tt, :], hh[:, g % 2, f, tt * 128:(tt + 1) * 128], w2[:, k, f, :],
                                                start=(f == 0), stop=(f == KF - 1))
                last.then_inc(s["dn_ps"], 1)

            def pair(e):
                for k in range(2):
                    c = GR * (2 * e + k)
                    pe.wait_ge(s[f"w_in{k}"], 32 * (e + 1))
                    up(c, k, 0)
                    for g in range(GR):
                        if g + 1 < GR:
                            up(c, k, g + 1)
                        down(c, k, g)

            pair(0)
            with pe.Fori(1, EXP // 2) as e:
                pair(e)

        @blk.scalar
        def _(act):
            act.wait_ge(s["m_ms"], 1)
            nc.scalar.activation(rs[:], t1[:], ACT.Sqrt).then_inc(s["m_rs"], 1)
            act.wait_ge(s["m_ms"], 2)
            nc.scalar.activation(rs[:], t1[:], ACT.Sqrt).then_inc(s["m_rs"], 1)
            for g in range(4):
                act.wait_ge(s["m_xt_ps"], g + 1)
                nc.scalar.activation(x1T[:, g * 512:(g + 1) * 512], pu[g][:], ACT.Copy).then_inc(s["m_xt"], 1)

            act.wait_ge(s["m_lg_ps"], 1)
            nc.scalar.activation(lg[:].rearrange("p t e -> p (t e)"), pr_[0][:, 0:NT * EXP], ACT.Copy).then_inc(s["m_act"], 1)
            act.wait_ge(s["m_e2"], 1)
            nc.scalar.activation(pr[:, 1], pr[:, 0], ACT.Exp).then_inc(s["m_act"], 1)
            act.wait_ge(s["m_act"], 2)
            act.wait_ge(s["m_xt"], 4)

            def relu(c, g, f):
                i = KF * (c + g) + f
                act.wait_ge(s["up_ps"], i + 1)
                if not (isinstance(c, int) and c == 0 and KF * g + f < 2):
                    act.wait_ge(s["h_ok"], i - 1)
                nc.scalar.activation(hr[:, f % 2], pu[f][:], ACT.Relu).then_inc(s["relu_ok"], 1)

            def pair(e):
                for k in range(2):
                    for g in range(GR):
                        for f in range(KF):
                            relu(GR * (2 * e + k), g, f)

            pair(0)
            with act.Fori(1, EXP // 2) as e:
                pair(e)
            act.wait_ge(s["m_var"], 1)
            nc.scalar.activation(rs[:], t1[:], ACT.Sqrt).then_inc(s["m_std"], 1)

        @blk.vector
        def _(dve):
            V = nc.vector
            chain = [0]

            def link(ins_):
                chain[0] += 1
                ins_.then_inc(s["m_dve"], 1)
                dve.wait_ge(s["m_dve"], chain[0])

            def newton():
                link(V.tensor_tensor(t1[:], rs[:], rs[:], ALU.mult))
                link(V.tensor_tensor(t1[:], t1[:], tot[:], ALU.mult))
                link(V.tensor_scalar(t1[:], t1[:], -0.5, 1.5, ALU.mult, ALU.add))
                link(V.tensor_tensor(rs[:], rs[:], t1[:], ALU.mult))

            def wide(a):
                return a.unsqueeze(2).to_broadcast([128, NT, DM])

            def centre(x):
                link(V.tensor_reduce(half[:], x[:], AX.X, ALU.add))
                link(V.tensor_scalar(half[:], half[:], 1.0 / DM, None, ALU.mult))
                link(V.tensor_tensor(x[:], x[:], wide(half[:]), ALU.subtract))
                link(V.tensor_tensor(sq[:], x[:], x[:], ALU.mult))
                link(V.tensor_reduce(tot[:], sq[:], AX.X, ALU.add))
                link(V.tensor_scalar(tot[:], tot[:], 1.0 / DM, EPS, ALU.mult, ALU.add))

            sv = keep["ssq"][:].rearrange("p (b f t) -> p b t f", f=2 * HALVES, t=TB)
            link(V.tensor_reduce(tot[:].rearrange("p (b t) -> p b t", t=TB), sv, AX.X, ALU.add))
            link(V.tensor_scalar(tot[:], tot[:], 1.0 / DI, EPS, ALU.mult, ALU.add))
            V.reciprocal(t1[:], tot[:]).then_inc(s["m_ms"], 1)
            dve.wait_ge(s["m_rs"], 1)
            newton()
            dve.wait_ge(s["m_in"], 64)
            dve.wait_ge(s["m_at_ps"], 1)
            for g in range(4):
                c = slice(4 * g, 4 * g + 4)
                link(V.tensor_tensor(xr[:, c], pu[g][:].rearrange("p (t c) -> p t c", t=4),
                                     rs[:, c].unsqueeze(2).to_broadcast([128, 4, DM]), ALU.mult))
            link(V.tensor_tensor(xr[:], xr[:], u[:], ALU.add))
            centre(xr)
            V.reciprocal(t1[:], tot[:]).then_inc(s["m_ms"], 1)
            dve.wait_ge(s["m_rs"], 2)
            newton()
            for g in range(4):
                V.tensor_tensor(xr[:, 4 * g:4 * g + 4], xr[:, 4 * g:4 * g + 4],
                                rs[:, 4 * g:4 * g + 4].unsqueeze(2).to_broadcast([128, 4, DM]), ALU.mult).then_inc(s["m_x1"], 1)
            dve.wait_ge(s["m_act"], 1)
            w8 = lambda a: a.unsqueeze(2).to_broadcast([128, NT, EXP])
            for k in range(2):
                link(V.tensor_reduce(m12[:, k], lg[:], AX.X, ALU.max))
                link(V.tensor_tensor(ky[:], lg[:], w8(m12[:, k]), ALU.is_equal))
                link(V.tensor_tensor(ky[:], ky[:], pref[:].unsqueeze(1).to_broadcast([128, NT, EXP]), ALU.mult))
                link(V.tensor_reduce(km[:], ky[:], AX.X, ALU.max))
                link(V.tensor_tensor(oh[:, k], ky[:], w8(km[:]), ALU.is_equal))
                if k == 0:
                    link(V.scalar_tensor_tensor(lg[:], oh[:, 0], NEG, lg[:], ALU.mult, ALU.add))
            link(V.tensor_copy(ohb[:], oh[:]))
            V.tensor_tensor(pr[:, 0], m12[:, 1], m12[:, 0], ALU.subtract).then_inc(s["m_e2"], 1)
            V.memset(t1[:], 0.0).then_inc(s["m_oh"], 1)
            dve.wait_ge(s["m_act"], 2)
            link(V.tensor_scalar(km[:], pr[:, 1], 1.0, None, ALU.add))
            link(V.reciprocal(pr[:, 0], km[:]))
            link(V.tensor_tensor(pr[:, 1], pr[:, 1], pr[:, 0], ALU.mult))
            dve.wait_ge(s["m_rk_ps"], 1)
            dve.wait_ge(s["m_e"], 3)
            tots = pr_[1][:, 256:512].rearrange("p (k t e) -> p k t e", k=2, e=EXP)
            link(V.tensor_copy(sa[:, :, 1:NT + 1, :], tots))
            a, b = sa, sb_
            for d in (1, 2, 4, 8):
                for k in range(2):
                    link(V.tensor_copy(b[:, k, 0:d, :], a[:, k, 0:d, :]))
                    link(V.tensor_tensor(b[:, k, d:NT + 1, :], a[:, k, d:NT + 1, :], a[:, k, 0:NT + 1 - d, :], ALU.add))
                a, b = b, a
            link(V.tensor_tensor(rk[:], pr_[1][:, 0:256].rearrange("p (k t e) -> p k t e", k=2, e=EXP), a[:, :, 0:NT, :], ALU.add))
            link(V.tensor_tensor(rk[:, 1], rk[:, 1], a[:, 0, NT:NT + 1, :].to_broadcast([128, NT, EXP]), ALU.add))
            for k in range(2):
                link(V.tensor_scalar(rk[:, k], rk[:, k], float(CAP), None, ALU.is_lt))
                link(V.tensor_tensor(rk[:, k], rk[:, k], oh[:, k], ALU.mult))
                link(V.tensor_tensor(rk[:, k], rk[:, k], w8(pr[:, k]), ALU.mult))
            V.tensor_tensor(gate[:].rearrange("p e t -> p t e"), rk[:, 0], rk[:, 1], ALU.add).then_inc(s["m_gate"], 1)
            dve.wait_ge(s["m_gate"], 1)

            def square(c, g, f):
                i = KF * (c + g) + f
                dve.wait_ge(s["relu_ok"], i + 1)
                if not (isinstance(c, int) and c == 0 and g < 2):
                    dve.wait_ge(s["dn_ps"], c + g - 1)
                V.tensor_tensor(hh[:, g % 2, f], hr[:, f % 2], hr[:, f % 2], ALU.mult).then_inc(s["h_ok"], 1)

            def collect(e, c, g):
                dve.wait_ge(s["dn_ps"], c + g + 1)
                if not (isinstance(c, int) and c == 0):
                    dve.wait_ge(s["dn_ok"], c - GR + g + 1)
                for tt in range(4):
                    i = 4 * g + tt
                    last = V.scalar_tensor_tensor(acc[:, i, :], pd[g % 2][:, tt, :], gate[:, bass.ds(e, 1), i:i + 1].rearrange("p o t -> p (o t)"),
                                                  acc[:, i, :], ALU.mult, ALU.add)
                last.then_inc(s["dn_ok"], 1)

            def pair(e):
                for k in range(2):
                    c = GR * (2 * e + k)
                    for f in range(KF):
                        square(c, 0, f)
                    for g in range(GR):
                        if g + 1 < GR:
                            for f in range(KF):
                                square(c, g + 1, f)
                        collect(2 * e + k, c, g)

            pair(0)
            with dve.Fori(1, EXP // 2) as e:
                pair(e)
            dve.wait_ge(s["dn_ok"], GR * EXP)
            link(V.tensor_tensor(acc[:], acc[:], xr[:], ALU.add))
            centre(acc)
            V.reciprocal(t1[:], tot[:]).then_inc(s["m_var"], 1)
            dve.wait_ge(s["m_std"], 1)
            newton()
            for g in range(4):
                V.tensor_tensor(sq[:, 4 * g:4 * g + 4], acc[:, 4 * g:4 * g + 4],
                                rs[:, 4 * g:4 * g + 4].unsqueeze(2).to_broadcast([128, 4, DM]), ALU.mult).then_inc(s["m_out"], 1)


def build(nc, ins, out):
    st = ExitStack()
    with st:
        keep = {
            "w_theta": sbuf(nc, st, "w_theta", [128, H * 2 * NH]),
            "w_x": sbuf(nc, st, "w_x", [128, DI]),
            "w_z": sbuf(nc, st, "w_z", [128, DI]),
            "w_out": sbuf(nc, st, "w_out", [128, DI // 128, DM]),
            "norm_w": sbuf(nc, st, "norm_w", [128, DI // 128]),
            "bias": sbuf(nc, st, "bias", [128, 4, H // 2]),
            "mask": sbuf(nc, st, "mask", [128, 128], BF16),
            "hot": sbuf(nc, st, "hot", [128, HU], BF16),
            "ident": sbuf(nc, st, "ident", [128, 128]),
            "ident_b": sbuf(nc, st, "ident_b", [128, 128], BF16),
            "half_pi": sbuf(nc, st, "half_pi", [128, 1]),
            "LS": sbuf(nc, st, "LS", [128, HALVES, TOK], BF16),
            "w": sbuf(nc, st, "w_tok", [128, NT, H]),
            "own": sbuf(nc, st, "own_tok", [128, NT, H]),
        }
        dram = {
            "cum": nc.dram_tensor("scratch_cum", [128, TOK], F32, kind="Internal").ap(),
            "cT": nc.dram_tensor("scratch_cT", [HALVES, CR, TOK], BF16, kind="Internal").ap(),
            "v": nc.dram_tensor("scratch_v", [BATCH, 128, 4, L], F32, kind="Internal").ap(),
        }
        ready = st.enter_context(nc.semaphore("half_pi_set"))
        with nc.Block() as blk:
            @blk.vector
            def _(dve):
                nc.vector.memset(keep["half_pi"][:], HALF_PI).then_inc(ready, 1)
                dve.wait_ge(ready, 1)
        setup_phase(nc, ins, keep, dram)
        keep["att"] = sbuf(nc, st, "att", [128, TOK])
        keep["ssq"] = sbuf(nc, st, "ssq", [128, UNITS * 2 * TB])
        attention_phase(nc, ins, keep, dram)
        moe_phase(nc, ins, keep, out)


def kernel(L0_attn_u, L0_attn_in_proj_w, L0_attn_dt_bias, L0_attn_A_log, L0_attn_D, L0_attn_B_norm_w, L0_attn_C_norm_w,
           L0_attn_B_bias, L0_attn_C_bias, L0_attn_norm_w, L0_attn_out_proj_w, L0_ffn_w_g, L0_ffn_c_fc, L0_ffn_c_proj):
    import concourse.bacc as bacc
    import ml_dtypes
    from concourse.bass_utils import run_bass_kernel_spmd

    def lay(a):
        return np.ascontiguousarray(a)

    u = np.asarray(L0_attn_u).reshape(TOK, DM)
    wT = np.asarray(L0_attn_in_proj_w).T
    off = 2 * DI + 2 * N
    th0 = off + H
    w_theta = wT[:, th0:th0 + H * NH].reshape(DM, H, 1, NH)
    w_theta = np.broadcast_to(w_theta, (DM, H, 2, NH)).reshape(DM, H * 2 * NH)
    w_small = np.concatenate([wT[:, 2 * DI:off + H], wT[:, th0 + H * NH:]], 1)
    nrm = np.asarray(L0_attn_norm_w)

    def bias_rows(a):
        a = np.asarray(a)
        straight = a.reshape(H // 2, 2 * N).T
        first, second = a[:, :NH], a[:, NH:]
        swapped = np.concatenate([second, first], 1).reshape(H // 2, 2 * N).T
        return straight, swapped

    b0, b1 = bias_rows(L0_attn_B_bias)
    c0, c1 = bias_rows(L0_attn_C_bias)
    f32, b16 = np.float32, ml_dtypes.bfloat16
    i = np.arange(128)
    hot = np.zeros((128, HU), b16)
    for k in range(3):
        hot[CN + k * HU + np.arange(HU), np.arange(HU)] = 1
    arrays = {
        "uT": lay(u.T), "u": lay(u), "w_small": lay(w_small), "w_theta": lay(w_theta),
        "w_z": lay(wT[:, 0:DI]), "w_x": lay(wT[:, DI:2 * DI]),
        "w_out": lay(np.asarray(L0_attn_out_proj_w).T.reshape(DI // 128, 128, DM).transpose(1, 0, 2)),
        "norm_w": lay(nrm.reshape(DI // 128, 128).T),
        "bias": lay(np.stack([b0, b1, c0, c1], 1)),
        "dt_bias": lay(L0_attn_dt_bias), "A_log": lay(L0_attn_A_log), "D": lay(L0_attn_D),
        "B_norm": lay(L0_attn_B_norm_w), "C_norm": lay(L0_attn_C_norm_w),
        "B_biasT": lay(np.asarray(L0_attn_B_bias).T), "C_biasT": lay(np.asarray(L0_attn_C_bias).T),
        "w_g": lay(np.asarray(L0_ffn_w_g).T), "c_fc": lay(L0_ffn_c_fc), "c_proj": lay(L0_ffn_c_proj),
        "tri": (i[:, None] <= i[None, :]).astype(f32),
        "low": (i[:, None] < i[None, :]).astype(b16),
        "ident": np.eye(128, dtype=f32), "ident_b": np.eye(128, dtype=b16),
        "mask": np.where(i[:, None] < i[None, :], 0.0, NEG).astype(b16),
        "hot": hot,
        "pref": np.arange(EXP, 0, -1).astype(f32),
    }
    nc = bacc.Bacc("TRN2", target_bir_lowering=False, num_devices=1)
    ins = {k: nc.dram_tensor(f"in_{k}", a.shape, mybir.dt.from_np(a.dtype), kind="ExternalInput").ap() for k, a in arrays.items()}
    out = nc.dram_tensor("out", [TOK, DM], F32, kind="ExternalOutput").ap()
    build(nc, ins, out)
    r = run_bass_kernel_spmd(nc, [{f"in_{k}": a for k, a in arrays.items()}], core_ids=[0])
    return r.results[0]["out"].reshape(BATCH, L, DM)
```

```python
from contextlib import ExitStack

import concourse.bass as bass
import numpy as np
from concourse import mybir

F32 = mybir.dt.float32
BF16 = mybir.dt.bfloat16
U32 = mybir.dt.uint32
ALU = mybir.AluOpType
ACT = mybir.ActivationFunctionType
AX = mybir.AxisListType

BATCH, L, DM = 8, 256, 128
H, P, N = 32, 64, 64
DI = H * P
NH = N // 2
TOK = BATCH * L
TP = 128
NT = TOK // TP
TB = L // TP
EXP, TOPK, FF = 8, 2, 4 * DM
CAP = max(4, int(1.25 * TOK * TOPK / EXP))
EPS = 1e-5

HALVES = 2
HU = H // HALVES
HQ = 128 // NH
PU = HU // 2
UNITS = BATCH * HALVES
DU = HU * P
W_S = L + TP

CR = 3 * HU
CN = 64

ROUND = float(1.5 * 2 ** 23)
TWO_PI = float(np.nextafter(np.float32(2 * np.pi), np.float32(0)))
HALF_PI = float(np.float32(np.pi / 2))
NEG = -1e30


def sbuf(nc, stack, name, shape, dt=F32):
    return stack.enter_context(nc.sbuf_tensor(name, shape, dt))


def semaphores(nc, stack, names):
    return {n: stack.enter_context(nc.semaphore(n)) for n in names.split()}


def setup_phase(nc, ins, keep, dram):
    CHUNKS = 4
    TC = TOK // CHUNKS
    st = ExitStack()
    with st:
        uT = sbuf(nc, st, "su_uT", [128, TOK + 1])
        uni = sbuf(nc, st, "su_uni", [128, L])
        cum = sbuf(nc, st, "su_cum", [128, TOK])
        wsm = sbuf(nc, st, "su_wsm", [128, 2 * N + 2 * H])
        raw = sbuf(nc, st, "su_raw", [128, NT, 2 * N + 4 * H])
        tri = sbuf(nc, st, "su_tri", [128, 128])
        ones = sbuf(nc, st, "su_ones", [128, 128])
        dtb = sbuf(nc, st, "su_dtb", [128, H])
        alog = sbuf(nc, st, "su_alog", [128, H])
        dsk = sbuf(nc, st, "su_dsk", [128, H])
        nw = sbuf(nc, st, "su_nw", [128, 2, N])
        bcT = sbuf(nc, st, "su_bcT", [128, H])
        bbT = sbuf(nc, st, "su_bbT", [128, H])
        bcp = sbuf(nc, st, "su_bcp", [128, H])
        kbc = sbuf(nc, st, "su_kbc", [128, H])
        x2 = sbuf(nc, st, "su_x2", [128, NT, 2, H])
        ab2 = sbuf(nc, st, "su_ab2", [128, NT, 2, H])
        dt2 = sbuf(nc, st, "su_dt2", [128, NT, 2, H])
        sg = sbuf(nc, st, "su_sg", [128, NT, 2, H])
        expa = sbuf(nc, st, "su_expa", [128, H])
        gam = sbuf(nc, st, "su_gam", [128, NT, H])
        dA = sbuf(nc, st, "su_dA", [128, 2, BATCH, H])
        rem = sbuf(nc, st, "su_rem", [128, 2, BATCH, HALVES, HU])
        cs = sbuf(nc, st, "su_cs", [128, NT, HALVES, 128], BF16)
        cT = sbuf(nc, st, "su_cT", [64, HALVES, TOK], BF16)
        sq = sbuf(nc, st, "su_sq", [128, NT, 2, N])
        cb = sbuf(nc, st, "su_cb", [128, NT, N])
        ss = sbuf(nc, st, "su_ss", [128, NT, 2])
        ms = sbuf(nc, st, "su_ms", [128, NT, 2])
        rs = sbuf(nc, st, "su_rs", [128, NT, 2])
        nt = sbuf(nc, st, "su_nt", [128, NT, 2])
        nb = sbuf(nc, st, "su_nb", [128, NT, 2, N])
        vT = sbuf(nc, st, "su_vT", [128, TOK])
        vN = sbuf(nc, st, "su_vN", [128, TOK])
        bcd = sbuf(nc, st, "su_bcd", [128, NT])
        ps = [st.enter_context(nc.psum_tensor(f"su_ps{i}", [128, 512], F32)) for i in range(6)]
        pb = [st.enter_context(nc.psum_tensor(f"su_pb{i}", [128, 1024], BF16)) for i in range(2)]
        s = semaphores(nc, st, "su_u0 su_u1 su_u2 su_u3 su_wsm su_small su_wout su_wbias su_hot su_ident su_identb su_a_ld su_raw_ps su_raw_act "
                               "su_raw_dve su_dve su_x2 su_ln su_dA su_cA_ps su_cs su_ct_ps su_ct_act su_ct_dve su_sq su_sg su_ms su_rs su_nb "
                               "su_v_ps su_vT su_vN su_bc_ps su_kb_ps su_scan su_cum su_set su_out su_abs su_ex su_expa su_bcp su_gam su_cb su_ones")
        blk = st.enter_context(nc.Block())
        BC, DT, LAM, DT1, LAM1 = slice(0, 2 * N), slice(2 * N, 2 * N + H), slice(2 * N + H, 2 * N + 2 * H), \
            slice(2 * N + 2 * H, 2 * N + 3 * H), slice(2 * N + 3 * H, 2 * N + 4 * H)
        RW = 2 * N + 4 * H

        @blk.sync
        def _(sp):
            sp.dma_start(wsm[:], ins["w_small"][:, :]).then_inc(s["su_wsm"], 16)
            sp.dma_start(keep["hot"][:], ins["hot"]).then_inc(s["su_hot"], 16)
            for c in range(CHUNKS):
                sp.dma_start(uT[:, c * TC:(c + 1) * TC], ins["uT"][:, c * TC:(c + 1) * TC]).then_inc(s[f"su_u{c}"], 16)
            for dst, src in ((tri[:], ins["tri"][:, :]),
                             (dtb[:], ins["dt_bias"].partition_broadcast(128)), (alog[:], ins["A_log"].partition_broadcast(128)),
                             (dsk[:], ins["D"].partition_broadcast(128)),
                             (nw[:, 0, :], ins["B_norm"].partition_broadcast(128)), (nw[:, 1, :], ins["C_norm"].partition_broadcast(128)),
                             (bcT[:], ins["CB_biasT"][:, :]), (bbT[0:N, :], ins["CB_biasT"][N:2 * N, :])):
                sp.dma_start(dst, src).then_inc(s["su_small"], 16)
            sp.dma_start(keep["ident"][:], ins["ident"][:, :]).then_inc(s["su_ident"], 16)
            sp.dma_start(keep["ident_b"][:], ins["ident_b"][:, :]).then_inc(s["su_identb"], 16)
            sp.dma_start(keep["bias"][:], ins["bias"]).then_inc(s["su_wbias"], 16)
            sp.dma_start(keep["norm_w"][:], ins["norm_w"]).then_inc(s["su_wout"], 16)
            sp.dma_start(keep["w_out"][:], ins["w_out"]).then_inc(s["su_wout"], 16)
            for name in ("mask", "w_theta", "w_x", "w_z"):
                sp.dma_start(keep[name][:], ins[name]).then_inc(s["su_a_ld"], 16)
            sp.dma_start(keep["u0"][:], ins["uT"][:, 0:L]).then_inc(s["su_a_ld"], 16)
            sp.wait_ge(s["su_cum"], 1)
            sp.dma_start(dram["cum"][:, :], cum[:]).then_inc(s["su_out"], 16)
            sp.dma_start(keep["cum0"][:], cum[:, 0:L]).then_inc(s["su_out"], 16)
            for c in range(2):
                t = slice(c * TOK // 2, (c + 1) * TOK // 2)
                sp.wait_ge(s["su_vT"], 2 * c + 2)
                sp.dma_start(dram["v"][0:2, :, t].rearrange("k r t -> (k r) t"), vT[:, t]).then_inc(s["su_out"], 16)
                for k in range(2):
                    sp.dma_start(dram["v"][2 + k, NH:N, t], vT[k * N:k * N + NH, t]).then_inc(s["su_out"], 16)
                sp.wait_ge(s["su_vN"], 2 * c + 2)
                for k in range(2):
                    sp.dma_start(dram["v"][2 + k, 0:NH, t], vN[k * N + NH:(k + 1) * N, t]).then_inc(s["su_out"], 16)
            sp.wait_ge(s["su_ct_act"], 8)
            sp.wait_ge(s["su_ct_dve"], 8)
            sp.dma_start(dram["cT"].rearrange("h r t -> r h t"), cT[0:CR]).then_inc(s["su_out"], 16)
            sp.wait_ge(s["su_out"], 13 * 16)
            sp.wait_ge(s["su_a_ld"], 80)

        @blk.gpsimd
        def _(pool):
            done = [0]

            def alone(ins_):
                done[0] += 1
                ins_.then_inc(s["su_set"], 1)
                pool.wait_ge(s["su_set"], done[0])

            P_ = nc.gpsimd
            alone(P_.memset(uT[:, TOK:TOK + 1], 0.0))
            alone(P_.memset(uni[:], 1.0))
            alone(P_.memset(ones[:], 1.0))
            alone(P_.memset(cs[:], 0.0))
            alone(P_.memset(bcp[N:128], 0.0))
            alone(P_.memset(keep["LS"][0:64], 1.0))
            alone(P_.memset(keep["half_pi"][:], HALF_PI))
            pool.wait_ge(s["su_small"], 16 * 8)
            P_.tensor_tensor(bcp[0:N], bbT[0:N], bcT[0:N], ALU.mult).then_inc(s["su_bcp"], 1)
            pool.wait_ge(s["su_bcp"], 1)
            for i in range(2):
                alone(P_.memset(keep["rh"][i][0:64], 0.0))
            pool.wait_ge(s["su_wbias"], 16)
            for k in (1, 3):
                for q in (0, 64):
                    alone(P_.tensor_scalar(keep["bias"][q:q + NH, k, :], keep["bias"][q:q + NH, k, :], -1.0, None, ALU.mult))
            pool.wait_ge(s["su_sg"], 2)
            pool.wait_ge(s["su_ln"], 2)
            P_.tensor_tensor(gam[:], sg[:, :, 0, :], dt2[:, :, 0, :], ALU.mult).then_inc(s["su_gam"], 1)
            P_.tensor_tensor(sg[:, :, 1, :], sg[:, :, 1, :], dt2[:, :, 1, :], ALU.mult).then_inc(s["su_gam"], 1)
            pool.wait_ge(s["su_gam"], 2)
            P_.tensor_tensor(keep["w"][:], gam[:], sg[:, :, 1, :], ALU.add).then_inc(s["su_gam"], 1)
            pool.wait_ge(s["su_nb"], 2 * NT)
            P_.tensor_tensor(cb[:], nb[:, :, 0, :], nb[:, :, 1, :], ALU.mult).then_inc(s["su_cb"], 1)
            alone(P_.memset(keep["Cr"][0:64, :, 1, :], 0.0))
            alone(P_.memset(keep["Cr"][64:128, :, 0, :], 0.0))
            pool.wait_ge(s["su_wout"], 32)
            alone(P_.tensor_tensor(keep["w_out"][:], keep["w_out"][:], keep["norm_w"][:].unsqueeze(2).to_broadcast([128, DI // 128, DM]), ALU.mult))
            pool.wait_ge(s["su_gam"], 3)

        @blk.tensor
        def _(pe):
            pe.wait_ge(s["su_wsm"], 16)
            pe.wait_ge(s["su_set"], 1)
            pe.wait_ge(s["su_u0"], 16)
            for i in range(NT):
                p, half = divmod(i, 2)
                if (i + 1) * TP % TC == 0 and i < NT - 1:
                    pe.wait_ge(s[f"su_u{(i + 1) * TP // TC}"], 16)
                if p >= 4 and half == 0:
                    pe.wait_ge(s["su_raw_act" if p % 2 == 0 else "su_raw_dve"], (p - 4) // 2 + 1)
                o = ps[p % 4][:, half * RW:(half + 1) * RW]
                nc.tensor.matmul(o[:, 0:2 * N + 2 * H], uT[:, i * TP:(i + 1) * TP], wsm[:], start=True, stop=True)
                last = nc.tensor.matmul(o[:, 2 * N + 2 * H:RW], uT[:, i * TP + 1:(i + 1) * TP + 1], wsm[:, 2 * N:2 * N + 2 * H], start=True, stop=True)
                if half:
                    last.then_inc(s["su_raw_ps"], 1)
            pe.wait_ge(s["su_small"], 16 * 8)
            pe.wait_ge(s["su_bcp"], 1)
            pe.wait_ge(s["su_set"], 5)
            pe.wait_ge(s["su_raw_act"], 4)
            pe.wait_ge(s["su_raw_dve"], 4)
            nc.tensor.matmul(ps[5][:, 0:H], ones[:], bcp[:], start=True, stop=True).then_inc(s["su_kb_ps"], 1)
            pe.wait_ge(s["su_dA"], 2)
            nc.tensor.matmul(ps[4][:, 0:256], tri[:], dA[:, 0], start=True, stop=True)
            nc.tensor.matmul(ps[4][:, 256:512], tri[:], dA[:, 1], start=True, stop=False)
            nc.tensor.matmul(ps[4][:, 256:512], ones[:], dA[:, 0], start=False, stop=True).then_inc(s["su_cA_ps"], 1)
            pe.wait_ge(s["su_ident"], 16)
            for i in range(NT):
                pe.wait_ge(s["su_nb"], 2 * i + 2)
                last = nc.tensor.transpose(ps[i // 4][:, (i % 4) * 128:(i % 4 + 1) * 128], nb[:, i], keep["ident"][:])
                if i % 4 == 3:
                    last.then_inc(s["su_v_ps"], 1)
            pe.wait_ge(s["su_kb_ps"], 2)
            for i in range(NT):
                if i % 4 == 0:
                    pe.wait_ge(s["su_vT"], i // 4 + 1)
                last = nc.tensor.matmul(ps[5][:, i * H:(i + 1) * H], vT[:, i * TP:(i + 1) * TP], bcT[:], start=True, stop=True)
            last.then_inc(s["su_bc_ps"], 1)
            pe.wait_ge(s["su_identb"], 16)
            pe.wait_ge(s["su_cs"], 1)
            for i in range(8):
                if i >= 2:
                    pe.wait_ge(s["su_ct_dve" if i % 2 else "su_ct_act"], 2 * (i // 2))
                for q in range(4):
                    last = nc.tensor.transpose(pb[i % 2][:, q * 128:(q + 1) * 128], cs[:, 2 * i + q % 2, q // 2, :], keep["ident_b"][:])
                last.then_inc(s["su_ct_ps"], 1)

        def decay_rows(eng, copy, i, ready):
            eng.wait_ge(s["su_ct_ps"], i + 1)
            src = pb[i % 2][:, 0:512].rearrange("p (f t) -> p f t", f=2)
            copy(cT[:, :, i * 256:(i + 1) * 256], src[0:64]).then_inc(ready, 1)
            copy(keep["LS"][64:128, :, i * 256:(i + 1) * 256], src[64:128]).then_inc(ready, 1)

        @blk.scalar
        def _(act):
            A = nc.scalar

            def ones_of_heads(i):
                A.activation(keep["rh"][i][64:128], keep["hot"][64:128].unsqueeze(2).to_broadcast([64, HU, L]), ACT.Copy).then_inc(s["su_ones"], 1)

            act.wait_ge(s["su_hot"], 16)
            ones_of_heads(0)
            for p in range(0, NT // 2, 2):
                act.wait_ge(s["su_raw_ps"], p + 1)
                A.activation(raw[:, 2 * p:2 * p + 2, :].rearrange("p a c -> p (a c)"), ps[p % 4][:], ACT.Copy).then_inc(s["su_raw_act"], 1)
            act.wait_ge(s["su_raw_act"], 4)
            act.wait_ge(s["su_raw_dve"], 4)
            A.activation(sq[:].rearrange("p t k n -> p t (k n)"), raw[:, :, BC], ACT.Square).then_inc(s["su_sq"], 1)
            A.activation(sg[:, :, 0, :], raw[:, :, LAM], ACT.Sigmoid).then_inc(s["su_sg"], 1)
            A.activation(sg[:, :, 1, :], raw[:, :, LAM1], ACT.Sigmoid, scale=-1.0).then_inc(s["su_sg"], 1)
            act.wait_ge(s["su_x2"], 2)
            A.activation(ab2[:], x2[:], ACT.Abs).then_inc(s["su_abs"], 1)
            act.wait_ge(s["su_abs"], 1)
            act.wait_ge(s["su_small"], 16 * 8)
            A.activation(expa[:], alog[:], ACT.Exp).then_inc(s["su_expa"], 1)
            A.activation(ab2[:], ab2[:], ACT.Exp, scale=-1.0).then_inc(s["su_ex"], 1)
            act.wait_ge(s["su_ex"], 1)
            A.activation(ab2[:], ab2[:], ACT.Ln, bias=1.0).then_inc(s["su_ln"], 1)
            act.wait_ge(s["su_ms"], 1)
            A.activation(rs[:], nt[:], ACT.Sqrt).then_inc(s["su_rs"], 1)
            act.wait_ge(s["su_scan"], BATCH)
            A.activation(cum[:], cum[:], ACT.Copy, scale=float(1 / (2 * np.pi))).then_inc(s["su_cum"], 1)
            ones_of_heads(1)
            for q in range(4):
                t = slice(q * 512, (q + 1) * 512)
                act.wait_ge(s["su_v_ps"], q + 1)
                A.activation(vT[:, t], ps[q][:], ACT.Copy).then_inc(s["su_vT"], 1)
                A.activation(vN[:, t], ps[q][:], ACT.Copy, scale=-1.0).then_inc(s["su_vN"], 1)
            for i in range(0, 8, 2):
                decay_rows(act, lambda o, i_: A.activation(o, i_, ACT.Copy), i, s["su_ct_act"])

        @blk.vector
        def _(dve):
            chain = [0]

            def link(ins_):
                chain[0] += 1
                ins_.then_inc(s["su_dve"], 1)
                dve.wait_ge(s["su_dve"], chain[0])

            V = nc.vector
            dve.wait_ge(s["su_set"], 2)
            for c in range(CHUNKS):
                dve.wait_ge(s[f"su_u{c}"], 16)
                for b in range(c * BATCH // CHUNKS, (c + 1) * BATCH // CHUNKS):
                    V.tensor_tensor_scan(cum[:, b * L:(b + 1) * L], uni[:], uT[:, b * L:(b + 1) * L], 0.0, ALU.mult, ALU.add).then_inc(s["su_scan"], 1)
            for p in range(1, NT // 2, 2):
                dve.wait_ge(s["su_raw_ps"], p + 1)
                V.tensor_copy(raw[:, 2 * p:2 * p + 2, :].rearrange("p a c -> p (a c)"), ps[p % 4][:]).then_inc(s["su_raw_dve"], 1)
            dve.wait_ge(s["su_raw_dve"], 4)
            dve.wait_ge(s["su_raw_act"], 4)
            dve.wait_ge(s["su_small"], 16 * 8)
            for k, c in enumerate((DT, DT1)):
                V.tensor_tensor(x2[:, :, k, :], raw[:, :, c], dtb[:].unsqueeze(1).to_broadcast([128, NT, H]), ALU.add).then_inc(s["su_x2"], 1)
            dve.wait_ge(s["su_kb_ps"], 1)
            V.tensor_copy(kbc[:], ps[5][:, 0:H]).then_inc(s["su_kb_ps"], 1)
            dve.wait_ge(s["su_sq"], 1)
            link(V.tensor_reduce(ss[:], sq[:], AX.X, ALU.add))
            link(V.tensor_scalar(ms[:], ss[:], 1.0 / N, EPS, ALU.mult, ALU.add))
            V.reciprocal(nt[:], ms[:]).then_inc(s["su_ms"], 1)
            dve.wait_ge(s["su_ln"], 1)
            dve.wait_ge(s["su_x2"], 2)
            V.scalar_tensor_tensor(dt2[:], x2[:], 0.0, ab2[:], ALU.max, ALU.add).then_inc(s["su_ln"], 1)
            dve.wait_ge(s["su_ln"], 2)
            dve.wait_ge(s["su_expa"], 1)
            for a in range(2):
                V.scalar_tensor_tensor(dA[:, a], dt2[:, :, 0, :].rearrange("p (b a) h -> p b a h", a=2)[:, :, a, :],
                                       -1.0, expa[:].unsqueeze(1).to_broadcast([128, BATCH, H]), ALU.mult, ALU.mult).then_inc(s["su_dA"], 1)
            dve.wait_ge(s["su_rs"], 1)
            link(V.tensor_tensor(nt[:], rs[:], rs[:], ALU.mult))
            link(V.tensor_tensor(nt[:], nt[:], ms[:], ALU.mult))
            link(V.tensor_scalar(nt[:], nt[:], -0.5, 1.5, ALU.mult, ALU.add))
            link(V.tensor_tensor(rs[:], rs[:], nt[:], ALU.mult))
            for i in range(NT):
                for k in range(2):
                    V.scalar_tensor_tensor(nb[:, i, k, :], raw[:, i, k * N:(k + 1) * N], rs[:, i, k:k + 1], nw[:, k, :], ALU.mult, ALU.mult).then_inc(s["su_nb"], 1)
            dve.wait_ge(s["su_cA_ps"], 1)
            dve.wait_ge(s["su_set"], 4)
            re = rem[:].rearrange("p a b f h -> p a b (f h)")
            csv = cs[:].rearrange("p (b a) f c -> p a b f c", a=2)
            ca = ps[4][:].rearrange("p (a b h) -> p a b h", a=2, h=H)

            def part(k, a):
                return csv[:, a, :, :, k * HU:(k + 1) * HU]

            def heads(x, a):
                return x[:, a].rearrange("p b (f h) -> p b f h", f=HALVES)

            for k in range(3):
                for a in range(2):
                    n = V.tensor_copy(part(k, a), heads(ca if k == 0 else re, a))
                    if a:
                        link(n)
                    else:
                        chain[0] += 1
                        n.then_inc(s["su_dve"], 1)
                if k == 2:
                    break
                for a in range(2):
                    n = V.tensor_tensor(heads(re, a), heads(ca if k == 0 else re, a), part(k, a), ALU.subtract)
                    if a:
                        link(n)
                    else:
                        chain[0] += 1
                        n.then_inc(s["su_dve"], 1)
            V.tensor_scalar(cs[:, :, :, CN:CN + CR], cs[:, :, :, 0:CR], -1.0, None, ALU.mult).then_inc(s["su_cs"], 1)
            dve.wait_ge(s["su_cb"], 1)
            link(V.tensor_reduce(bcd[:], cb[:], AX.X, ALU.add))
            dve.wait_ge(s["su_bc_ps"], 1)
            dve.wait_ge(s["su_kb_ps"], 2)
            dve.wait_ge(s["su_gam"], 1)
            own = keep["own"]
            tokens = [128, NT, H]
            link(V.tensor_tensor(own[:], ps[5][:].rearrange("p (t h) -> p t h", h=H), bcd[:].unsqueeze(2).to_broadcast(tokens), ALU.add))
            decay_rows(dve, V.tensor_copy, 1, s["su_ct_dve"])
            link(V.tensor_tensor(own[:], own[:], kbc[:].unsqueeze(1).to_broadcast(tokens), ALU.add))
            decay_rows(dve, V.tensor_copy, 3, s["su_ct_dve"])
            link(V.tensor_tensor(own[:], own[:], gam[:], ALU.mult))
            decay_rows(dve, V.tensor_copy, 5, s["su_ct_dve"])
            link(V.tensor_tensor(own[:], own[:], dsk[:].unsqueeze(1).to_broadcast(tokens), ALU.add))
            decay_rows(dve, V.tensor_copy, 7, s["su_ct_dve"])


def attention_phase(nc, ins, keep, dram):
    AHEAD = 7
    RING = AHEAD + 1
    FIRST = 4
    TURNED = 4
    EARLY = 8
    ROTATED = 4
    ANGLES = HU - 3
    EXPS = [[] for _ in range(HU)]
    for i in range(HU):
        EXPS[FIRST + i * (HU - FIRST) // HU].append(AHEAD + i)
    ROTATE = [[] for _ in range(HU)]
    for i in range(HU):
        ROTATE[TURNED + i * (HU - TURNED) // HU].append(divmod(i, 2))
    TURN = {2 * j + 5: j for j in range(PU - 2)}
    st = ExitStack()
    with st:
        ub, cb_ = keep["u0"], keep["cum0"]
        v = sbuf(nc, st, "at_v", [128, 4, L])
        rh, Cr = keep["rh"], keep["Cr"]
        sc = sbuf(nc, st, "at_sc", [128, 2, 2, 2, L])
        sc2 = sbuf(nc, st, "at_sc2", [128, 4, 2, 2, L])
        tmp = sbuf(nc, st, "at_tmp", [128, 2, 4, L])
        Br = sbuf(nc, st, "at_B", [128, PU, L])
        ex = sbuf(nc, st, "at_ex", [128, RING, W_S])
        G = sbuf(nc, st, "at_G", [128, 2, W_S])
        xw = sbuf(nc, st, "at_xw", [128, 2, TB, DU])
        xo = sbuf(nc, st, "at_xo", [128, 2, TB, DU])
        sz = sbuf(nc, st, "at_sz", [128, 2, TB, DU])
        yz = sbuf(nc, st, "at_yz", [128, TB, DU])
        yT = sbuf(nc, st, "at_yT", [128, PU, L])
        junk = sbuf(nc, st, "at_junk", [128, DU // 2], BF16)
        pp, pc, pe_ = ([st.enter_context(nc.psum_tensor(f"at_{n}{i}", [128, 512], F32)) for i in range(2)] for n in ("pp", "pc", "pe"))
        py = st.enter_context(nc.psum_tensor("at_py", [128, 512], F32))
        pt = st.enter_context(nc.psum_tensor("at_pt", [128, 512], F32))
        s = semaphores(nc, st, "c_low u_in cum_in v_in rh_early rh_late rh_in0 rh_in1 th_ps z_ps x_ps dup0 dup1 dup2 dup3 whole_ok r_ok abs_ok sc_ok zc_ok silu_ok "
                               "xw_ok xs_ok xo_ok rope_ok b_ok c_ok e_ps e_ok c_ps g_ok y_ps y1_ok y2_ok t_ps t_ok sq_ok o_ps o_ok")
        blk = st.enter_context(nc.Block())
        w_theta, w_x, w_z, w_out = keep["w_theta"], keep["w_x"], keep["w_z"], keep["w_out"]
        bias, mask, identb, ident, LS = keep["bias"], keep["mask"], keep["ident_b"], keep["ident"], keep["LS"]

        def slots(eng, slot):
            slot(0, 0, 0, 0, 1)
            with eng.Fori(1, BATCH - 1) as b:
                slot(2 * b - 1, 1, b - 1, b, b)
                slot(2 * b, 0, b, b, b + 1)
            slot(UNITS - 3, 1, BATCH - 2, BATCH - 1, BATCH - 1)
            slot(UNITS - 2, 0, BATCH - 1, BATCH - 1, None)
            slot(UNITS - 1, 1, BATCH - 1, None, None)

        @blk.sync
        def _(sp):
            def load_sums(b):
                sp.dma_start(cb_[:], dram["cum"][:, bass.ds(b * L, L)]).then_inc(s["cum_in"], 16)

            def load_u(b):
                sp.dma_start(ub[:], ins["uT"][:, bass.ds(b * L, L)]).then_inc(s["u_in"], 16)

            def load_rows(b):
                for d in range(2):
                    sp.dma_start(v[d * N:(d + 1) * N], dram["v"][:, :, bass.ds(b * L, L)].rearrange("k r t -> r k t")).then_inc(s["v_in"], 16)

            def load_decays(par, b, heads, arrived):
                for h in heads:
                    sp.dma_start(rh[par][h:CR:HU, h, :], dram["cT"][par, h:CR:HU, bass.ds(b * L, L)]).then_inc(s[arrived], 16)

            def duplicate(a, g):
                sp.wait_ge(s["sc_ok"], 4 * a + 2 * g + 2)
                if isinstance(a, int) and a == 1:
                    sp.wait_ge(s["rope_ok"], 4 * g + 4)
                for c in range(2):
                    for k in range(2):
                        p = (2 * c + k) * NH
                        for half in range(2):
                            sp.dma_start(sc2[k * 2 * NH + half * NH:k * 2 * NH + (half + 1) * NH, 2 * g + c], sc[p:p + NH, g]).then_inc(s[f"dup{2 * g + c}"], 16)

            def slot(n, par, bn, ba, bc):
                if ba is None:
                    return
                duplicate(n + 1, 0)
                if not first(n):
                    sp.wait_ge(s["e_ps"], HU * n)
                load_decays(1 - par, ba, range(HU), f"rh_in{1 - par}")
                duplicate(n + 1, 1)
                if par == 0 and bc is not None:
                    sp.wait_ge(s["th_ps"], 2 * (n + 2))
                    load_sums(bn + 1)
                    sp.wait_ge(s["z_ps"], 4 * (n + 2))
                    load_u(bn + 1)
                    sp.wait_ge(s["rope_ok"], PU * (n + 2))
                    load_rows(bn + 1)

            load_rows(0)
            load_decays(0, 0, range(EARLY), "rh_early")
            duplicate(0, 0)
            duplicate(0, 1)
            load_decays(0, 0, range(EARLY, HU), "rh_late")
            slots(sp, slot)

        @blk.tensor
        def _(pe):
            def angles(a, par, b, g):
                if g == 0 and not first(b):
                    pe.wait_ge(s["cum_in"], 16 * b)
                if not first(a):
                    pe.wait_ge(s["zc_ok"], 4 * a + g - 1)
                for k in range(2):
                    j = par * HU // HQ + 2 * g + k
                    last = nc.tensor.matmul(pp[g][:, k * L:(k + 1) * L], w_theta[:, j * 128:(j + 1) * 128], cb_[:],
                                            start=True, stop=True)
                last.then_inc(s["th_ps"], 1)

            def project(a, par, b, q, w_, ready, done, before):
                tt, c = divmod(q, 2)
                if q < 2:
                    pe.wait_ge(s[before], 2 * a + q + 1 if before == "r_ok" else 4 * a + q + 3)
                else:
                    pe.wait_ge(s[done], 4 * a + q - 1)
                if done == "xs_ok" and q == 0 and not first(b):
                    pe.wait_ge(s["u_in"], 16 * b)
                o = par * DU + c * 512
                nc.tensor.matmul(pp[q % 2][:], ub[:, tt * TP:(tt + 1) * TP], w_[:, o:o + 512], start=True, stop=True).then_inc(s[ready], 1)

            def decay(n, par, b, h):
                if first(n):
                    if h in (0, EARLY):
                        pe.wait_ge(s["rh_late" if h else "rh_early"], 16 * (HU - EARLY if h else EARLY))
                elif h == 0:
                    pe.wait_ge(s[f"rh_in{par}"], 16 * HU * (b + par))
                if not (first(n) and h < 2):
                    pe.wait_ge(s["e_ok"], HU * n + h - 1)
                e = pe_[h % 2]
                nc.tensor.matmul(e[:, 0:L], LS[:, par, bass.ds(b * L, TP)], rh[par][:, h, :], start=True, stop=False)
                nc.tensor.matmul(e[:, 0:TP], identb[:], mask[:], start=False, stop=True)
                nc.tensor.matmul(e[:, L:W_S], LS[:, par, bass.ds(b * L + TP, TP)], rh[par][:, h, TP:L], start=True, stop=False)
                nc.tensor.matmul(e[:, L:W_S], identb[:], mask[:], start=False, stop=True).then_inc(s["e_ps"], 1)

            def scores(n, h):
                j, k = divmod(h, 2)
                if k == 0:
                    pe.wait_ge(s["c_ok"], PU * n + j + 1)
                if not (first(n) and h < 2):
                    pe.wait_ge(s["g_ok"], HU * n + h - 1)
                c = pc[h % 2]
                nc.tensor.matmul(c[:, 0:L], Br[:, j, 0:TP], Cr[:, j, k, :], start=True, stop=True)
                nc.tensor.matmul(c[:, L:W_S], Br[:, j, TP:L], Cr[:, j, k, TP:L], start=True, stop=True).then_inc(s["c_ps"], 1)

            def output(n, par, h):
                j, k = divmod(h, 2)
                if h == 0:
                    pe.wait_ge(s["xw_ok"], 4 * n + 4)
                pe.wait_ge(s["g_ok"], HU * n + h + 1)
                if k == 0 and not (first(n) and j == 0):
                    pe.wait_ge(s["y1_ok"], PU * n + j)
                y = py[:, 0:L].rearrange("p (a c) -> p a c", a=TB)[:, :, k * P:(k + 1) * P]
                g = G[:, h % 2]
                c = slice(h * P, (h + 1) * P)
                nc.tensor.matmul(y[:, 0], g[:, 0:TP], xw[:, par, 0, c], start=True, stop=True)
                nc.tensor.matmul(y[:, 1], g[:, TP:L], xw[:, par, 0, c], start=True, stop=False)
                nc.tensor.matmul(y[:, 1], g[:, L:W_S], xw[:, par, 1, c], start=False, stop=True).then_inc(s["y_ps"], 1)

            def turn(n, j):
                pe.wait_ge(s["y2_ok"], PU * n + j + 1)
                if j > 0:
                    pe.wait_ge(s["t_ok"], PU * n + j)
                elif not first(n):
                    pe.wait_ge(s["o_ok"], n)
                for tt in range(TB):
                    last = nc.tensor.transpose(pt[:, tt * TP:(tt + 1) * TP], yz[:, tt, j * 128:(j + 1) * 128], ident[:])
                last.then_inc(s["t_ps"], 1)

            def project_out(n, par):
                pe.wait_ge(s["t_ok"], PU * n + PU)
                for k in range(PU):
                    last = nc.tensor.matmul(pt[:, 0:L], w_out[:, par * PU + k, :], yT[:, k, :], start=(k == 0), stop=(k == PU - 1))
                last.then_inc(s["o_ps"], 1)

            def slot(n, par, bn, ba, bc):
                a, pa = n + 1, 1 - par
                for h in range(HU):
                    scores(n, h)
                    if h >= 1:
                        output(n, par, h - 1)
                    elif not first(n):
                        output(n - 1, pa, HU - 1)
                    if ANGLES <= h < ANGLES + 2 and bc is not None:
                        angles(n + 2, par, bc, h - ANGLES)
                    if not first(n):
                        if h in (1, 2):
                            turn(n - 1, PU - 3 + h)
                        if h == 4:
                            project_out(n - 1, pa)
                    if h in TURN:
                        turn(n, TURN[h])
                    for i in EXPS[h]:
                        if i < HU:
                            decay(n, par, bn, i)
                        elif ba is not None:
                            decay(a, pa, ba, i - HU)
                    if ba is not None:
                        if 5 <= h < 9:
                            project(a, pa, ba, h - 5, w_x, "x_ps", "xs_ok", "r_ok")
                        elif 9 <= h < 13:
                            project(a, pa, ba, h - 9, w_z, "z_ps", "zc_ok", "xs_ok")

            for g in range(2):
                angles(0, 0, 0, g)
            for q in range(4):
                project(0, 0, 0, q, w_x, "x_ps", "xs_ok", "r_ok")
            for q in range(4):
                project(0, 0, 0, q, w_z, "z_ps", "zc_ok", "xs_ok")
            angles(1, 1, 0, 0)
            angles(1, 1, 0, 1)
            for h in range(AHEAD):
                decay(0, 0, 0, h)
            slots(pe, slot)
            n = UNITS - 1
            output(n, 1, HU - 1)
            turn(n, PU - 2)
            turn(n, PU - 1)
            project_out(n, 1)

        @blk.scalar
        def _(act):
            def angles(a, g):
                act.wait_ge(s["r_ok"], 2 * a + g + 1)
                if not (isinstance(a, int) and a < 2):
                    act.wait_ge(s["rope_ok"], PU * (a - 1) + 4 * g + 4)
                sine, cosine = sc[:, g, 0], sc[:, g, 1]
                nc.scalar.activation(cosine, sine, ACT.Abs).then_inc(s["abs_ok"], 1)
                act.wait_ge(s["abs_ok"], 2 * a + g + 1)
                nc.scalar.activation(sine, sine, ACT.Sin, scale=-TWO_PI).then_inc(s["sc_ok"], 1)
                nc.scalar.activation(cosine, cosine, ACT.Sin, scale=-TWO_PI, bias=keep["half_pi"][:, 0:1]).then_inc(s["sc_ok"], 1)

            def keep_x(a, pa, q):
                tt, c = divmod(q, 2)
                act.wait_ge(s["x_ps"], 4 * a + q + 1)
                if q == 0 and not first(a) and not (isinstance(a, int) and a == 1):
                    act.wait_ge(s["y1_ok"], PU * (a - 1))
                nc.scalar.activation(xo[:, pa, tt, c * 512:(c + 1) * 512], pp[q % 2][:], ACT.Copy).then_inc(s["xs_ok"], 1)

            def keep_z(a, pa, q):
                tt, c = divmod(q, 2)
                act.wait_ge(s["z_ps"], 4 * a + q + 1)
                if q == 0 and not first(a) and not (isinstance(a, int) and a == 1):
                    act.wait_ge(s["y2_ok"], PU * (a - 1))
                nc.scalar.activation(sz[:, pa, tt, c * 512:(c + 1) * 512], pp[q % 2][:], ACT.Copy).then_inc(s["zc_ok"], 1)

            def silu(n, par):
                act.wait_ge(s["zc_ok"], 4 * n + 4)
                for tt in range(TB):
                    nc.scalar.activation(sz[:, par, tt, :], sz[:, par, tt, :], ACT.Silu).then_inc(s["silu_ok"], 1)

            def decay(n, h):
                act.wait_ge(s["e_ps"], HU * n + h + 1)
                if not (first(n) and h < RING):
                    act.wait_ge(s["g_ok"], HU * n + h + 1 - RING)
                nc.scalar.activation(ex[:, h % RING], pe_[h % 2][:, 0:W_S], ACT.Exp).then_inc(s["e_ok"], 1)

            def turn(n, j):
                act.wait_ge(s["t_ps"], PU * n + j + 1)
                if j == 0 and not first(n):
                    act.wait_ge(s["o_ps"], n)
                nc.scalar.activation(yT[:, j, :], pt[:, 0:L], ACT.Copy).then_inc(s["t_ok"], 1)

            def squares(n, f):
                act.wait_ge(s["y2_ok"], PU * n + PU // 2 * (f + 1))
                for tt in range(TB):
                    if f or tt or not first(n):
                        act.wait_ge(s["sq_ok"], 2 * TB * n + TB * f + tt)
                    nc.scalar.activation(junk[:], yz[:, tt, f * 512:(f + 1) * 512], ACT.Square,
                                         accum_out=keep["ssq"][:, bass.ds(2 * TB * n + TB * f + tt, 1)]).then_inc(s["sq_ok"], 1)

            def slot(n, par, bn, ba, bc):
                a, pa = n + 1, 1 - par
                silu(n, par)
                if not first(n):
                    turn(n - 1, PU - 2)
                if ba is not None:
                    angles(a, 0)
                if not first(n):
                    turn(n - 1, PU - 1)
                if ba is not None:
                    angles(a, 1)
                for h in range(FIRST, HU):
                    if h in TURN:
                        turn(n, TURN[h])
                    for i in EXPS[h]:
                        if i < HU:
                            decay(n, i)
                        elif ba is not None:
                            decay(a, i - HU)
                    if h == 6 and not first(n):
                        squares(n - 1, 1)
                    if h == 12:
                        squares(n, 0)
                    if ba is not None:
                        if 5 <= h < 9:
                            keep_x(a, pa, h - 5)
                        elif 9 <= h < 13:
                            keep_z(a, pa, h - 9)

            for g in range(2):
                angles(0, g)
            for q in range(4):
                keep_x(0, 0, q)
            for q in range(4):
                keep_z(0, 0, q)
            for h in range(AHEAD):
                decay(0, h)
            slots(act, slot)
            n = UNITS - 1
            turn(n, PU - 2)
            turn(n, PU - 1)
            squares(n, 1)

        @blk.gpsimd
        def _(pool):
            def scale_x(a, pa, b, q):
                tt, c = divmod(q, 2)
                x3 = xo[:, pa, tt, c * 512:(c + 1) * 512].rearrange("p (h e) -> p h e", e=P)
                xw3 = xw[:, pa, tt, c * 512:(c + 1) * 512].rearrange("p (h e) -> p h e", e=P)
                w8, own8 = (keep[k][:, bass.ds(TB * b + tt, 1), pa * HU + c * 8:pa * HU + c * 8 + 8].rearrange("p o h -> p (o h)")
                            .unsqueeze(2).to_broadcast([128, 8, P]) for k in ("w", "own"))
                pool.wait_ge(s["xs_ok"], 4 * a + q + 1)
                if q == 0 and not first(a) and not (isinstance(a, int) and a == 1):
                    pool.wait_ge(s["y_ps"], HU * (a - 1))
                nc.gpsimd.tensor_tensor(xw3, x3, w8, ALU.mult).then_inc(s["xw_ok"], 1)
                nc.gpsimd.tensor_tensor(x3, x3, own8, ALU.mult).then_inc(s["xo_ok"], 1)

            def rotate(a, j):
                t = tmp[:, j % 2]
                pool.wait_ge(s["rope_ok"], PU * a + j + 1)
                if not first(a):
                    pool.wait_ge(s["c_ps"], HU * (a - 1) + 2 * j + 2)
                if not first(a):
                    nc.gpsimd.tensor_tensor(Br[:, j, :], t[:, 0], t[:, 1], ALU.add).then_inc(s["b_ok"], 1)
                pool.wait_ge(s["b_ok"], PU * a + j + 1)
                nc.gpsimd.tensor_tensor(Cr[0:64, j, 0, :], t[0:64, 2], t[0:64, 3], ALU.add).then_inc(s["c_low"], 1)
                pool.wait_ge(s["c_low"], PU * a + j + 1)
                nc.gpsimd.tensor_tensor(Cr[64:128, j, 1, :], t[64:128, 2], t[64:128, 3], ALU.add).then_inc(s["c_ok"], 1)
                pool.wait_ge(s["c_ok"], PU * a + j + 1)

            def unit(a, pa, b):
                for j in range(PU):
                    if first(a) and j < 2:
                        scale_x(0, 0, 0, 2 * j)
                        scale_x(0, 0, 0, 2 * j + 1)
                    rotate(a, j)
                    if first(a):
                        continue
                    if 1 <= j < 5:
                        scale_x(a, pa, b, j - 1)

            def slot(n, par, bn, ba, bc):
                if ba is not None:
                    unit(n + 1, 1 - par, ba)

            unit(0, 0, 0)
            slots(pool, slot)

        @blk.vector
        def _(dve):
            V = nc.vector

            def fold(a, g):
                dve.wait_ge(s["th_ps"], 2 * a + g + 1)
                turns = sc[:, g, 0].rearrange("p t l -> p (t l)")
                if not first(a):
                    for c in range(2):
                        dve.wait_ge(s[f"dup{2 * g + c}"], 64 * a)
                V.tensor_scalar(turns, pp[g][:], ROUND, None, ALU.add).then_inc(s["whole_ok"], 1)
                dve.wait_ge(s["whole_ok"], 2 * a + g + 1)
                V.scalar_tensor_tensor(turns, turns, ROUND, pp[g][:], ALU.subtract, ALU.subtract).then_inc(s["r_ok"], 1)

            def rotate(a, pa, b, j, which):
                J = pa * PU + j
                if which == 0:
                    dve.wait_ge(s[f"dup{2 * (j // 4) + j % 2}"], 64 * a + 64)
                    if j == 0:
                        dve.wait_ge(s["v_in"], 32 * (b + 1))
                    if not (first(a) and j < 2):
                        dve.wait_ge(s["c_ok"], PU * a + j - 1)
                for kind in (2 * which, 2 * which + 1):
                    angle = sc2[:, 2 * (j // 4) + j % 2, 1 - kind % 2, j // 2 % 2, :]
                    last = V.scalar_tensor_tensor(tmp[:, j % 2, kind], v[:, kind % 2 * 2 + kind // 2, :], bias[:, kind, J:J + 1], angle, ALU.add, ALU.mult)
                if which:
                    last.then_inc(s["rope_ok"], 1)

            def rotate_first(j):
                rotate(0, 0, 0, j, 0)
                rotate(0, 0, 0, j, 1)
                dve.wait_ge(s["rope_ok"], j + 1)
                V.tensor_tensor(Br[:, j, :], tmp[:, j % 2, 0], tmp[:, j % 2, 1], ALU.add).then_inc(s["b_ok"], 1)

            def weigh(n, h):
                dve.wait_ge(s["e_ok"], HU * n + h + 1)
                dve.wait_ge(s["c_ps"], HU * n + h + 1)
                if not (first(n) and h < 2):
                    dve.wait_ge(s["y_ps"], HU * n + h - 1)
                V.tensor_tensor(G[:, h % 2], pc[h % 2][:, 0:W_S], ex[:, h % RING], ALU.mult).then_inc(s["g_ok"], 1)

            def gate(n, par, j, parts=(0, 1)):
                if 0 in parts:
                    add_own(n, par, j)
                if 1 in parts:
                    c = slice(j * 128, (j + 1) * 128)
                    dve.wait_ge(s["y1_ok"], PU * n + j + 1)
                    dve.wait_ge(s["silu_ok"], TB * n + TB)
                    V.tensor_tensor(yz[:, :, c], yz[:, :, c], sz[:, par, :, c], ALU.mult).then_inc(s["y2_ok"], 1)

            def add_own(n, par, j):
                c = slice(j * 128, (j + 1) * 128)
                dve.wait_ge(s["y_ps"], HU * n + 2 * j + 2)
                if j == 0:
                    dve.wait_ge(s["xo_ok"], 4 * n + 4)
                    if not first(n):
                        dve.wait_ge(s["t_ps"], PU * n)
                        dve.wait_ge(s["sq_ok"], 2 * TB * n - TB)
                if j == PU // 2 and not first(n):
                    dve.wait_ge(s["sq_ok"], 2 * TB * n)
                V.tensor_tensor(yz[:, :, c], py[:, 0:L].rearrange("p (a c) -> p a c", a=TB), xo[:, par, :, c], ALU.add).then_inc(s["y1_ok"], 1)

            def collect(n, par, b):
                dve.wait_ge(s["o_ps"], n + 1)
                att = keep["att"][:, bass.ds(b * L, L)]
                if par == 0:
                    V.tensor_copy(att, pt[:, 0:L]).then_inc(s["o_ok"], 1)
                else:
                    dve.wait_ge(s["o_ok"], n)
                    V.tensor_tensor(att, pt[:, 0:L], att, ALU.add).then_inc(s["o_ok"], 1)

            def slot(n, par, bn, ba, bc):
                a, pa = n + 1, 1 - par
                for h in range(HU):
                    if h == 5 and not first(n):
                        collect(n - 1, pa, bn if par == 1 else bn - 1)
                    weigh(n, h)
                    if h % 2 == 0:
                        if h >= 2:
                            gate(n, par, h // 2 - 1, (0,) if h == 2 else (0, 1))
                        elif not first(n):
                            gate(n - 1, pa, PU - 1)
                    if h == 3:
                        gate(n, par, 0, (1,))
                    if first(n) and ROTATED + h < PU:
                        rotate_first(ROTATED + h)
                    if ba is not None:
                        for j, which in ROTATE[h]:
                            rotate(a, pa, ba, j, which)
                    if ANGLES <= h < ANGLES + 2 and bc is not None:
                        fold(n + 2, h - ANGLES)

            for g in range(2):
                fold(0, g)
            for j in range(ROTATED):
                rotate_first(j)
            fold(1, 0)
            fold(1, 1)
            slots(dve, slot)
            n = UNITS - 1
            gate(n, 1, PU - 1)
            collect(n, 1, BATCH - 1)


def first(n):
    return isinstance(n, int) and n == 0


def moe_phase(nc, ins, keep, dram, out):
    KF = FF // 128
    CT = CAP // 128
    G = [(0, (CT + 1) // 2), ((CT + 1) // 2, CT)]
    WG = (G[0][1] - G[0][0]) * 128
    QT = 4
    NQ = EXP * CT
    NK = TOPK * NT
    assert CAP % 128 == 0 and WG <= 512 and TOPK * TOK == 4096
    st = ExitStack()
    with st:
        u = sbuf(nc, st, "mo_u", [128, NT, DM])
        xr = sbuf(nc, st, "mo_x", [128, NT, DM])
        xc = sbuf(nc, st, "mo_xc", [128, NT, DM])
        x1T = sbuf(nc, st, "mo_xT", [128, TOK])
        zero = sbuf(nc, st, "mo_zero", [128, 4 * DM])
        rr = sbuf(nc, st, "mo_rr", [128, NT])
        places = sbuf(nc, st, "mo_places", [128, 128], BF16)
        tiles = sbuf(nc, st, "mo_tiles", [128, NQ])
        ids = sbuf(nc, st, "mo_ids", [128, 2, NK], BF16)
        at_ = sbuf(nc, st, "mo_at", [128, TOPK, NT])
        ap = sbuf(nc, st, "mo_ap", [128, TOPK, NT])
        isp = sbuf(nc, st, "mo_isp", [128, NK, 128], BF16)
        ist = sbuf(nc, st, "mo_ist", [128, NK, NQ], BF16)
        idt = sbuf(nc, st, "mo_idt", [128, NK, 2, NQ], BF16)
        tb = sbuf(nc, st, "mo_tb", [128, NQ])
        tz = sbuf(nc, st, "mo_tz", [128, NQ])
        wg = sbuf(nc, st, "mo_wg", [128, EXP])
        w1 = sbuf(nc, st, "mo_w1", [128, 2, FF])
        w2 = sbuf(nc, st, "mo_w2", [128, 2, KF, DM])
        low = sbuf(nc, st, "mo_low", [128, 128], BF16)
        oneb = sbuf(nc, st, "mo_oneb", [128, 128], BF16)
        pref = sbuf(nc, st, "mo_pref", [128, EXP])
        base = sbuf(nc, st, "mo_base", [128, EXP])
        notf = sbuf(nc, st, "mo_notf", [128, 2 * EXP, NT])
        tot = sbuf(nc, st, "mo_tot", [128, NT])
        rs = sbuf(nc, st, "mo_rs", [128, NT])
        t1 = sbuf(nc, st, "mo_t1", [128, NT])
        bs = sbuf(nc, st, "mo_bs", [128, NT, 6])
        mv = sbuf(nc, st, "mo_mv", [128, NT, 2])
        nm = sbuf(nc, st, "mo_nm", [128, NT])
        lg = sbuf(nc, st, "mo_lg", [128, NT, EXP])
        m12 = sbuf(nc, st, "mo_m12", [128, 2, NT])
        km = sbuf(nc, st, "mo_km", [128, NT])
        ky = sbuf(nc, st, "mo_ky", [128, NT, EXP])
        oh = sbuf(nc, st, "mo_oh", [128, 2, NT, EXP])
        ohb = sbuf(nc, st, "mo_ohb", [128, 2, EXP, NT], BF16)
        pr = sbuf(nc, st, "mo_pr", [128, 2, NT])
        run = sbuf(nc, st, "mo_run", [128, 2, EXP, NT])
        rk = sbuf(nc, st, "mo_rk", [128, 2, NT, EXP])
        ok = sbuf(nc, st, "mo_ok", [128, 2, NT, EXP])
        val = sbuf(nc, st, "mo_val", [128, 2, NT])
        gx = sbuf(nc, st, "mo_gx", [128, 2, NT])
        fetch = sbuf(nc, st, "mo_fetch", [128, NQ], U32)
        send = sbuf(nc, st, "mo_send", [128, NQ], U32)
        gate = sbuf(nc, st, "mo_gate", [128, 2, NT])
        xs = sbuf(nc, st, "mo_xs", [128, 2, CT, DM])
        xsT = sbuf(nc, st, "mo_xsT", [128, 2, WG])
        hr = sbuf(nc, st, "mo_hr", [128, 2, WG])
        hh = sbuf(nc, st, "mo_hh", [128, 2, KF, WG])
        ys = sbuf(nc, st, "mo_ys", [128, 2, CT, DM])
        gy = sbuf(nc, st, "mo_gy", [128, NT, 2, DM])
        diag = sbuf(nc, st, "mo_diag", [128, NT, 2, DM])
        pu = [st.enter_context(nc.psum_tensor(f"mo_pu{i}", [128, 512], F32)) for i in range(4)]
        pd = [st.enter_context(nc.psum_tensor(f"mo_pd{i}", [128, 4, DM], F32)) for i in range(2)]
        px = [st.enter_context(nc.psum_tensor(f"mo_px{i}", [128, 512], F32)) for i in range(2)]
        s = semaphores(nc, st, "m_at_ps m_in m_zero m_zeroed m_dve m_rr m_rr_sq m_ms m_rs m_stat m_x1 m_xt_ps m_xt m_lg_ps m_oh m_rk_ps m_e m_e2 "
                               "m_pr m_isp m_ist m_idt m_tb_ps m_fetch m_gate m_send m_x1_out w_in0 w_in1 xs_in00 xs_in01 xs_in10 xs_in11 tr_ps xt_ok up_ps relu_ok h_ok "
                               "dn_ps ys_ok y_out0 y_out1 m_var m_std m_norm m_out m_store m_gy0 m_gy1 m_gy2 m_gy3 m_diag m_sum_ps m_u0 m_u1 m_u2 m_u3")
        blk = st.enter_context(nc.Block())
        x1d, back = dram["x1"], dram["back"]

        @blk.sync
        def _(sp):
            for q in range(NT // QT):
                sp.dma_start(u[:, QT * q:QT * (q + 1), :], ins["u"].rearrange("(t p) c -> p t c", p=128)[:, QT * q:QT * (q + 1), :]).then_inc(s[f"m_u{q}"], 16)
            for dst, src in ((wg[:], ins["w_g"][:, :]), (low[:], ins["low"][:, :]), (places[:], ins["places"]), (tiles[:], ins["tiles"]),
                             (ids[:], ins["ids"]), (pref[:], ins["pref"].partition_broadcast(128)), (base[:], ins["base"].partition_broadcast(128))):
                sp.dma_start(dst, src).then_inc(s["m_in"], 16)
            sp.wait_ge(s["m_zero"], 1)
            for i in range(NK // 4):
                sp.dma_start(back[i * 512:(i + 1) * 512, :].rearrange("(p r) c -> p (r c)", p=128), zero[:]).then_inc(s["m_zeroed"], 16)

            def load_weights(e, k):
                sp.dma_start(w1[:, k], ins["c_fc"][bass.ds(e, 1)].rearrange("o c f -> (o c) f")).then_inc(s[f"w_in{k}"], 16)
                sp.dma_start(w2[:, k], ins["c_proj"][bass.ds(e, 1)].rearrange("o (k p) c -> p (o k) c", p=128)).then_inc(s[f"w_in{k}"], 16)

            load_weights(0, 0)
            load_weights(1, 1)
            for q in range(NT // QT):
                sp.wait_ge(s["m_x1"], QT * (q + 1))
                sp.dma_start(x1d[q * QT * 128:(q + 1) * QT * 128, :].rearrange("(t p) c -> p t c", p=128), xr[:, QT * q:QT * (q + 1), :]).then_inc(s["m_x1_out"], 16)
            with sp.Fori(0, EXP // 2 - 1) as h:
                for k in range(2):
                    e = 2 * h + k
                    sp.wait_ge(s["dn_ps"], 2 * e + 2)
                    load_weights(e + 2, k)
            sp.wait_ge(s["m_x1_out"], 16 * (NT // QT))
            sp.wait_ge(s["y_out0"], 16 * CT * EXP // 2)
            sp.wait_ge(s["y_out1"], 16 * CT * EXP // 2)
            for q in range(NT // QT):
                for k in range(TOPK):
                    r = (k * NT + QT * q) * 128
                    sp.dma_start(gy[:, QT * q:QT * (q + 1), k, :], back[r:r + QT * 128, :].rearrange("(t p) c -> p t c", p=128)).then_inc(s[f"m_gy{q}"], 16)
            for q in range(NT // QT):
                sp.wait_ge(s["m_out"], QT * (q + 1))
                sp.dma_start(out.rearrange("(t p) c -> p t c", p=128)[:, QT * q:QT * (q + 1), :], xc[:, QT * q:QT * (q + 1), :]).then_inc(s["m_store"], 16)
            sp.wait_ge(s["m_store"], 16 * (NT // QT))

        @blk.gpsimd
        def _(pool):
            nc.gpsimd.memset(zero[:], 0.0).then_inc(s["m_zero"], 1)
            nc.gpsimd.memset(oneb[:], 1.0).then_inc(s["m_e"], 1)
            nc.gpsimd.memset(notf[:], 1.0).then_inc(s["m_e"], 1)
            pool.wait_ge(s["m_e"], 2)
            nc.gpsimd.memset(notf[:, :, 0:1], 0.0).then_inc(s["m_e"], 1)
            pool.wait_ge(s["m_ist"], 1)
            pool.wait_ge(s["m_in"], 16 * 7)
            nc.gpsimd.tensor_tensor(idt[:, :, 1, :], ist[:], ids[:, 1].unsqueeze(2).to_broadcast([128, NK, NQ]), ALU.mult).then_inc(s["m_idt"], 1)

            def gather(e):
                for g in range(2):
                    for t in range(*G[g]):
                        i = e * CT + t
                        nc.gpsimd.indirect_dma_start(xs[:, e % 2, t, :], None, x1d[:, :], bass.IndirectOffsetOnAxis(ap=fetch[:, i:i + 1], axis=0),
                                                     bounds_check=TOK - 1, oob_is_err=False).then_inc(s[f"xs_in{e % 2}{g}"], 16)

            def scatter(e):
                for g in range(2):
                    pool.wait_ge(s["ys_ok"], 2 * e + g + 1)
                    for t in range(*G[g]):
                        i = e * CT + t
                        nc.gpsimd.indirect_dma_start(back[:, :], bass.IndirectOffsetOnAxis(ap=send[:, i:i + 1], axis=0), ys[:, e % 2, t, :], None,
                                                     bounds_check=TOPK * TOK - 1, oob_is_err=False).then_inc(s[f"y_out{e % 2}"], 16)

            pool.wait_ge(s["m_fetch"], 1)
            pool.wait_ge(s["m_x1_out"], 16 * (NT // QT))
            gather(0)
            gather(1)
            pool.wait_ge(s["m_send"], 1)
            pool.wait_ge(s["m_zeroed"], 16 * (NK // 4))
            for e in range(EXP):
                if e + 2 < EXP:
                    pool.wait_ge(s["tr_ps"], 2 * e + 2)
                    gather(e + 2)
                scatter(e)

        @blk.tensor
        def _(pe):
            def router(q):
                pe.wait_ge(s["m_xt"], q + 1)
                pe.wait_ge(s["m_in"], 16 * 7)
                for i in range(4 * q, 4 * q + 4):
                    last = nc.tensor.matmul(px[0][:, i * EXP:(i + 1) * EXP], x1T[:, i * 128:(i + 1) * 128], wg[:], start=True, stop=True)
                if q == 3:
                    last.then_inc(s["m_lg_ps"], 1)

            for i in range(NT):
                last = nc.tensor.transpose(pu[i // 4][:, (i % 4) * 128:(i % 4 + 1) * 128], keep["att"][:, i * 128:(i + 1) * 128],
                                           keep["ident"][:])
                if i % 4 == 3:
                    last.then_inc(s["m_at_ps"], 1)
            for q in range(4):
                pe.wait_ge(s["m_x1"], 4 * q + 4)
                for i in range(4 * q, 4 * q + 4):
                    last = nc.tensor.transpose(pu[q][:, (i % 4) * 128:(i % 4 + 1) * 128], xr[:, i, :], keep["ident"][:])
                last.then_inc(s["m_xt_ps"], 1)
                if q:
                    router(q - 1)
            router(3)
            pe.wait_ge(s["m_oh"], 1)
            pe.wait_ge(s["m_e"], 1)
            nc.tensor.matmul(px[1][:, 0:256], low[:], ohb[:].rearrange("p k e t -> p (k e t)"), start=True, stop=True)
            nc.tensor.matmul(px[1][:, 256:512], oneb[:], ohb[:].rearrange("p k e t -> p (k e t)"), start=True, stop=True).then_inc(s["m_rk_ps"], 1)
            pe.wait_ge(s["m_idt"], 2)
            for i in range(NK):
                pe.wait_ge(s["m_isp"], i + 1)
                last = nc.tensor.matmul(px[0][:, 0:2 * NQ], isp[:, i, :], idt[:, i].rearrange("p a q -> p (a q)"), start=(i == 0), stop=(i == NK - 1))
            last.then_inc(s["m_tb_ps"], 1)
            pe.wait_ge(s["m_send"], 1)

            def turn(e, k, g, start):
                i = 2 * e + g
                nt = G[g][1] - G[g][0]
                pe.wait_ge(s[f"xs_in{k}{g}"], 16 * nt if start else 8 * nt * (e - k) + 16 * nt)
                if not start:
                    pe.wait_ge(s["xt_ok"], i - 1)
                for t in range(*G[g]):
                    c = (t - G[g][0]) * 128
                    last = nc.tensor.transpose(px[g][:, c:c + 128], xs[:, k, t, :], keep["ident"][:])
                last.then_inc(s["tr_ps"], 1)

            def up(e, k, g, start):
                i = 2 * e + g
                w = (G[g][1] - G[g][0]) * 128
                if g == 0:
                    pe.wait_ge(s[f"w_in{k}"], 32 if start else 16 * (e - k) + 32)
                pe.wait_ge(s["xt_ok"], i + 1)
                for f in range(KF):
                    if not start:
                        pe.wait_ge(s["relu_ok"], KF * (i - 1) + f + 1)
                    nc.tensor.matmul(pu[f][:, 0:w], w1[:, k, f * 128:(f + 1) * 128], xsT[:, g, 0:w], start=True, stop=True).then_inc(s["up_ps"], 1)

            def down(e, k, g, start):
                i = 2 * e + g
                if not start:
                    pe.wait_ge(s["ys_ok"], i - 1)
                pe.wait_ge(s["h_ok"], KF * (i + 1))
                for t in range(G[g][1] - G[g][0]):
                    for f in range(KF):
                        last = nc.tensor.matmul(pd[g][:, t, :], hh[:, g, f, t * 128:(t + 1) * 128], w2[:, k, f, :],
                                                start=(f == 0), stop=(f == KF - 1))
                last.then_inc(s["dn_ps"], 1)

            def pair(h, end):
                start = isinstance(h, int) and h == 0
                for k in range(2):
                    for g in range(2):
                        if not (end and k == 1):
                            turn(2 * h + k + 1, 1 - k, g, False)
                        if not (end and k == 1 and g == 1):
                            up(2 * h + k + g, (k + g) % 2, 1 - g, False)
                        down(2 * h + k, k, g, start and k == 0)

            turn(0, 0, 0, True)
            turn(0, 0, 1, True)
            up(0, 0, 0, True)
            pair(0, False)
            with pe.Fori(1, EXP // 2 - 1) as h:
                pair(h, False)
            pair(EXP // 2 - 1, True)
            pe.wait_ge(s["m_diag"], NK)
            pe.wait_ge(s["relu_ok"], 2 * KF * EXP)
            for q in range(NT // QT):
                pe.wait_ge(s[f"m_gy{q}"], 16 * TOPK)
                for i in range(QT * q, QT * (q + 1)):
                    o = pu[q][:, (i % QT) * DM:(i % QT + 1) * DM]
                    nc.tensor.matmul(o, keep["ident"][:], xr[:, i, :], start=True, stop=False)
                    nc.tensor.matmul(o, diag[:, i, 0, :], gy[:, i, 0, :], start=False, stop=False)
                    last = nc.tensor.matmul(o, diag[:, i, 1, :], gy[:, i, 1, :], start=False, stop=True)
                last.then_inc(s["m_sum_ps"], 1)

        @blk.scalar
        def _(act):
            act.wait_ge(s["m_rr"], 1)
            nc.scalar.activation(rr[:], t1[:], ACT.Sqrt).then_inc(s["m_rr_sq"], 1)

            def root(q):
                c = slice(QT * q, QT * (q + 1))
                act.wait_ge(s["m_ms"], q + 1)
                nc.scalar.activation(rs[:, c], t1[:, c], ACT.Sqrt).then_inc(s["m_rs"], 1)

            def turned(q):
                act.wait_ge(s["m_xt_ps"], q + 1)
                nc.scalar.activation(x1T[:, q * 512:(q + 1) * 512], pu[q][:], ACT.Copy).then_inc(s["m_xt"], 1)

            for q in range(NT // QT):
                root(q)
                act.wait_ge(s["m_stat"], q + 1)
                for i in range(QT * q, QT * (q + 1)):
                    nc.scalar.activation(xr[:, i, :], xc[:, i, :], ACT.Identity, scale=rs[:, i:i + 1], bias=nm[:, i:i + 1]).then_inc(s["m_x1"], 1)
                if q:
                    turned(q - 1)
            turned(NT // QT - 1)
            act.wait_ge(s["m_e2"], 1)
            nc.scalar.activation(pr[:, 1], pr[:, 0], ACT.Exp).then_inc(s["m_pr"], 1)

            def relus(e, g, start):
                i = 2 * e + g
                w = (G[g][1] - G[g][0]) * 128
                for f in range(KF):
                    act.wait_ge(s["up_ps"], KF * i + f + 1)
                    if not (start and f < 2):
                        act.wait_ge(s["h_ok"], KF * i + f - 1)
                    nc.scalar.activation(hr[:, f % 2, 0:w], pu[f][:, 0:w], ACT.Relu).then_inc(s["relu_ok"], 1)

            def leave(e, k, g):
                act.wait_ge(s["dn_ps"], 2 * e + g + 1)
                if g == 0 and not (isinstance(e, int) and e < 2):
                    act.wait_ge(s[f"y_out{k}"], 8 * CT * (e - k))
                nc.scalar.activation(ys[:, k, G[g][0]:G[g][1], :], pd[g][:, 0:G[g][1] - G[g][0], :], ACT.Copy).then_inc(s["ys_ok"], 1)

            def pair(h, end):
                for k in range(2):
                    for g in range(2):
                        if not (end and k == 1 and g == 1):
                            relus(2 * h + k + g, 1 - g, False)
                        leave(2 * h + k, k, g)

            act.wait_ge(s["m_gate"], 1)
            for i in range(NT):
                for k in range(TOPK):
                    nc.scalar.activation(diag[:, i, k, :], keep["ident"][:], ACT.Copy, scale=gate[:, k, i:i + 1]).then_inc(s["m_diag"], 1)
            relus(0, 0, True)
            pair(0, False)
            with act.Fori(1, EXP // 2 - 1) as h:
                pair(h, False)
            pair(EXP // 2 - 1, True)
            def last_root(q):
                c = slice(QT * q, QT * (q + 1))
                act.wait_ge(s["m_var"], q + 1)
                nc.scalar.activation(rs[:, c], t1[:, c], ACT.Sqrt).then_inc(s["m_std"], 1)

            for q in range(NT // QT):
                last_root(q)
                act.wait_ge(s["m_norm"], q + 1)
                for i in range(QT * q, QT * (q + 1)):
                    nc.scalar.activation(xc[:, i, :], pu[q][:, (i % QT) * DM:(i % QT + 1) * DM], ACT.Identity,
                                         scale=rs[:, i:i + 1], bias=nm[:, i:i + 1]).then_inc(s["m_out"], 1)

        @blk.vector
        def _(dve):
            V = nc.vector
            chain = [0]

            def link(ins_):
                chain[0] += 1
                ins_.then_inc(s["m_dve"], 1)
                dve.wait_ge(s["m_dve"], chain[0])

            def newton(r, c):
                link(V.tensor_tensor(t1[:, c], r[:, c], r[:, c], ALU.mult))
                link(V.tensor_tensor(t1[:, c], t1[:, c], tot[:, c], ALU.mult))
                link(V.tensor_scalar(t1[:, c], t1[:, c], -0.5, 1.5, ALU.mult, ALU.add))
                link(V.tensor_tensor(r[:, c], r[:, c], t1[:, c], ALU.mult))

            def run_of(instructions):
                for n in instructions:
                    chain[0] += 1
                    n.then_inc(s["m_dve"], 1)
                dve.wait_ge(s["m_dve"], chain[0])

            def moments(x, lo, hi, ready):
                run_of(V.bn_stats(bs[:, i, :], x(i)) for i in range(lo, hi))
                run_of(V.bn_aggr(mv[:, i, :], bs[:, i, :]) for i in range(lo, hi))
                link(V.tensor_scalar(tot[:, lo:hi], mv[:, lo:hi, 1], EPS, None, ALU.add))
                V.reciprocal(t1[:, lo:hi], tot[:, lo:hi]).then_inc(ready, 1)

            def shift(lo, hi, ready):
                V.scalar_tensor_tensor(nm[:, lo:hi], mv[:, lo:hi, 0], -1.0, rs[:, lo:hi], ALU.mult, ALU.mult).then_inc(ready, 1)

            sv = keep["ssq"][:].rearrange("p (b f t) -> p b t f", f=2 * HALVES, t=TB)
            link(V.tensor_reduce(tot[:].rearrange("p (b t) -> p b t", t=TB), sv, AX.X, ALU.add))
            link(V.tensor_scalar(tot[:], tot[:], 1.0 / DI, EPS, ALU.mult, ALU.add))
            V.reciprocal(t1[:], tot[:]).then_inc(s["m_rr"], 1)
            dve.wait_ge(s["m_rr_sq"], 1)
            newton(rr, slice(0, NT))

            def residual(q):
                dve.wait_ge(s["m_at_ps"], q + 1)
                dve.wait_ge(s[f"m_u{q}"], 16)
                run_of(V.scalar_tensor_tensor(xc[:, i, :], pu[q][:, (i % 4) * 128:(i % 4 + 1) * 128], rr[:, i:i + 1], u[:, i, :], ALU.mult, ALU.add)
                       for i in range(4 * q, 4 * q + 4))
                moments(lambda i: xc[:, i, :], 4 * q, 4 * q + 4, s["m_ms"])

            def norm(q):
                dve.wait_ge(s["m_rs"], q + 1)
                newton(rs, slice(4 * q, 4 * q + 4))
                shift(4 * q, 4 * q + 4, s["m_stat"])

            for q in range(NT // QT):
                residual(q)
                norm(q)
            dve.wait_ge(s["m_in"], 16 * 7)
            dve.wait_ge(s["m_lg_ps"], 1)
            link(V.tensor_copy(lg[:].rearrange("p t e -> p (t e)"), px[0][:, 0:NT * EXP]))
            w8 = lambda a: a.unsqueeze(2).to_broadcast([128, NT, EXP])
            e8 = lambda a: a[:].unsqueeze(1).to_broadcast([128, NT, EXP])
            for k in range(2):
                link(V.tensor_reduce(m12[:, k], lg[:], AX.X, ALU.max))
                link(V.tensor_tensor(ky[:], lg[:], w8(m12[:, k]), ALU.is_equal))
                link(V.tensor_tensor(ky[:], ky[:], e8(pref), ALU.mult))
                link(V.tensor_reduce(km[:], ky[:], AX.X, ALU.max))
                link(V.tensor_tensor(oh[:, k], ky[:], w8(km[:]), ALU.is_equal))
                if k == 0:
                    link(V.scalar_tensor_tensor(lg[:], oh[:, 0], NEG, lg[:], ALU.mult, ALU.add))
            V.tensor_copy(ohb[:].rearrange("p k e t -> p k t e"), oh[:]).then_inc(s["m_oh"], 1)
            V.tensor_tensor(pr[:, 0], m12[:, 1], m12[:, 0], ALU.subtract).then_inc(s["m_e2"], 1)
            dve.wait_ge(s["m_rk_ps"], 1)
            dve.wait_ge(s["m_e"], 3)
            link(V.tensor_tensor_scan(run[:].rearrange("p k e t -> p (k e t)"), notf[:].rearrange("p a t -> p (a t)"),
                                      px[1][:, 256:512], 0.0, ALU.mult, ALU.add))
            by_expert = "p k t e -> p k e t"
            link(V.tensor_tensor(rk[:].rearrange(by_expert), px[1][:, 0:256].rearrange("p (k e t) -> p k e t", k=TOPK, t=NT), run[:], ALU.add))
            link(V.tensor_tensor(rk[:, 1].rearrange("p t e -> p e t"), rk[:, 1].rearrange("p t e -> p e t"),
                                 run[:, 0, :, NT - 1:NT].to_broadcast([128, EXP, NT]), ALU.add))
            flat = [x[:].rearrange("p k t e -> p (k t) e") for x in (rk, oh, ok)]
            link(V.scalar_tensor_tensor(flat[2], flat[0], float(CAP), flat[1], ALU.is_lt, ALU.mult))
            link(V.tensor_reduce(val[:].rearrange("p k t -> p (k t)"), flat[2], AX.X, ALU.add))
            link(V.tensor_tensor(flat[0], flat[0], base[:].unsqueeze(1).to_broadcast([128, NK, EXP]), ALU.add))
            link(V.tensor_tensor(flat[0], flat[0], flat[2], ALU.mult))
            link(V.tensor_reduce(gx[:].rearrange("p k t -> p (k t)"), flat[0], AX.X, ALU.add))
            link(V.tensor_scalar(at_[:], gx[:], 1.0 / 128, -63.5 / 128, ALU.mult, ALU.add))
            link(V.tensor_scalar(at_[:], at_[:], ROUND, None, ALU.add))
            link(V.tensor_scalar(at_[:], at_[:], ROUND, None, ALU.subtract))
            link(V.scalar_tensor_tensor(ap[:], at_[:], -128.0, gx[:], ALU.mult, ALU.add))
            link(V.scalar_tensor_tensor(at_[:], at_[:], 1.0, val[:], ALU.add, ALU.mult))
            link(V.tensor_scalar(at_[:], at_[:], -1.0, None, ALU.add))
            V.tensor_tensor(ist[:], tiles[:].unsqueeze(1).to_broadcast([128, NK, NQ]), at_[:].rearrange("p k t -> p (k t)").unsqueeze(2).to_broadcast([128, NK, NQ]),
                            ALU.is_equal).then_inc(s["m_ist"], 1)
            dve.wait_ge(s["m_ist"], 1)
            V.tensor_tensor(idt[:, :, 0, :], ist[:], ids[:, 0].unsqueeze(2).to_broadcast([128, NK, NQ]), ALU.mult).then_inc(s["m_idt"], 1)
            for i in range(NK):
                V.tensor_scalar(isp[:, i, :], places[:], ap[:, i // NT, i % NT:i % NT + 1], None, ALU.is_equal).then_inc(s["m_isp"], 1)
            dve.wait_ge(s["m_pr"], 1)
            link(V.tensor_scalar(km[:], pr[:, 1], 1.0, None, ALU.add))
            link(V.reciprocal(pr[:, 0], km[:]))
            link(V.tensor_tensor(pr[:, 1], pr[:, 1], pr[:, 0], ALU.mult))
            V.tensor_tensor(gate[:], pr[:], val[:], ALU.mult).then_inc(s["m_gate"], 1)
            dve.wait_ge(s["m_tb_ps"], 1)
            link(V.tensor_copy(tz[:], px[0][:, NQ:2 * NQ]))
            link(V.tensor_tensor(tb[:], px[0][:, 0:NQ], tz[:], ALU.add))
            link(V.tensor_scalar(tz[:], tb[:], float(TOK), -float(TOK), ALU.is_gt, ALU.mult))
            link(V.scalar_tensor_tensor(tz[:], tb[:], -1.0, tz[:], ALU.add, ALU.add))
            V.tensor_scalar(fetch[:], tz[:], 0.0, None, ALU.max).then_inc(s["m_fetch"], 1)
            dve.wait_ge(s["m_fetch"], 1)
            link(V.tensor_scalar(tz[:], tb[:], 0.0, float(TOPK * TOK + 1), ALU.is_equal, ALU.mult))
            V.scalar_tensor_tensor(send[:], tb[:], -1.0, tz[:], ALU.add, ALU.add).then_inc(s["m_send"], 1)
            def take(e, g, start):
                i = 2 * e + g
                w = (G[g][1] - G[g][0]) * 128
                dve.wait_ge(s["tr_ps"], i + 1)
                if not start:
                    dve.wait_ge(s["up_ps"], KF * (i - 1))
                V.tensor_copy(xsT[:, g, 0:w], px[g][:, 0:w]).then_inc(s["xt_ok"], 1)

            def squares(e, g, start):
                i = 2 * e + g
                w = (G[g][1] - G[g][0]) * 128
                if not start:
                    dve.wait_ge(s["dn_ps"], i - 1)
                for f in range(KF):
                    dve.wait_ge(s["relu_ok"], KF * i + f + 1)
                    V.tensor_tensor(hh[:, g, f, 0:w], hr[:, f % 2, 0:w], hr[:, f % 2, 0:w], ALU.mult).then_inc(s["h_ok"], 1)

            def pair(h, end):
                start = isinstance(h, int) and h == 0
                for k in range(2):
                    for g in range(2):
                        if not (end and k == 1):
                            take(2 * h + k + 1, g, False)
                        if not (end and k == 1 and g == 1):
                            squares(2 * h + k + g, 1 - g, start and k == 0 and g == 0)

            take(0, 0, True)
            take(0, 1, True)
            squares(0, 0, True)
            pair(0, False)
            with dve.Fori(1, EXP // 2 - 1) as h:
                pair(h, False)
            pair(EXP // 2 - 1, True)
            def summed(q):
                lo = QT * q
                dve.wait_ge(s["m_sum_ps"], q + 1)
                moments(lambda i: pu[q][:, (i - lo) * DM:(i - lo + 1) * DM], lo, lo + QT, s["m_var"])

            def last_norm(q):
                dve.wait_ge(s["m_std"], q + 1)
                newton(rs, slice(QT * q, QT * (q + 1)))
                shift(QT * q, QT * (q + 1), s["m_norm"])

            for q in range(NT // QT):
                summed(q)
                last_norm(q)


def build(nc, ins, out):
    st = ExitStack()
    with st:
        keep = {
            "w_theta": sbuf(nc, st, "w_theta", [128, H * NH]),
            "w_x": sbuf(nc, st, "w_x", [128, DI]),
            "w_z": sbuf(nc, st, "w_z", [128, DI]),
            "w_out": sbuf(nc, st, "w_out", [128, DI // 128, DM]),
            "norm_w": sbuf(nc, st, "norm_w", [128, DI // 128]),
            "bias": sbuf(nc, st, "bias", [128, 4, H // 2]),
            "mask": sbuf(nc, st, "mask", [128, 128], BF16),
            "hot": sbuf(nc, st, "hot", [128, HU], BF16),
            "ident": sbuf(nc, st, "ident", [128, 128]),
            "ident_b": sbuf(nc, st, "ident_b", [128, 128], BF16),
            "half_pi": sbuf(nc, st, "half_pi", [128, 1]),
            "LS": sbuf(nc, st, "LS", [128, HALVES, TOK], BF16),
            "w": sbuf(nc, st, "w_tok", [128, NT, H]),
            "own": sbuf(nc, st, "own_tok", [128, NT, H]),
        }
        dram = {
            "cum": nc.dram_tensor("scratch_cum", [128, TOK], F32, kind="Internal").ap(),
            "cT": nc.dram_tensor("scratch_cT", [HALVES, CR, TOK], BF16, kind="Internal").ap(),
            "x1": nc.dram_tensor("scratch_x1", [TOK, DM], F32, kind="Internal").ap(),
            "back": nc.dram_tensor("scratch_back", [TOPK * TOK, DM], F32, kind="Internal").ap(),
            "v": nc.dram_tensor("scratch_v", [4, N, TOK], F32, kind="Internal").ap(),
        }
        keep["att"] = sbuf(nc, st, "att", [128, TOK])
        keep["ssq"] = sbuf(nc, st, "ssq", [128, UNITS * 2 * TB])
        with ExitStack() as att:
            keep["rh"] = [sbuf(nc, att, f"at_rh{i}", [128, HU, L], BF16) for i in range(2)]
            keep["u0"] = sbuf(nc, att, "at_u", [128, L])
            keep["cum0"] = sbuf(nc, att, "at_cum", [128, L])
            keep["Cr"] = sbuf(nc, att, "at_C", [128, PU, 2, L])
            setup_phase(nc, ins, keep, dram)
            attention_phase(nc, ins, keep, dram)
        moe_phase(nc, ins, keep, dram, out)


def kernel(L0_attn_u, L0_attn_in_proj_w, L0_attn_dt_bias, L0_attn_A_log, L0_attn_D, L0_attn_B_norm_w, L0_attn_C_norm_w,
           L0_attn_B_bias, L0_attn_C_bias, L0_attn_norm_w, L0_attn_out_proj_w, L0_ffn_w_g, L0_ffn_c_fc, L0_ffn_c_proj):
    import concourse.bacc as bacc
    import ml_dtypes
    from concourse.bass_utils import run_bass_kernel_spmd

    def lay(a):
        return np.ascontiguousarray(a)

    u = np.asarray(L0_attn_u).reshape(TOK, DM)
    wT = np.asarray(L0_attn_in_proj_w).T
    off = 2 * DI + 2 * N
    th0 = off + H
    w_small = np.concatenate([wT[:, 2 * DI:off + H], wT[:, th0 + H * NH:]], 1)
    nrm = np.asarray(L0_attn_norm_w)

    def bias_rows(a):
        a = np.asarray(a)
        straight = a.reshape(H // 2, 2 * N).T
        first, second = a[:, :NH], a[:, NH:]
        swapped = np.concatenate([second, first], 1).reshape(H // 2, 2 * N).T
        return straight, swapped

    b0, b1 = bias_rows(L0_attn_B_bias)
    c0, c1 = bias_rows(L0_attn_C_bias)
    f32, b16 = np.float32, ml_dtypes.bfloat16
    i = np.arange(128)
    hot = np.zeros((128, HU), b16)
    for k in range(3):
        hot[CN + k * HU + np.arange(HU), np.arange(HU)] = 1
    entry = 1 + 128 * np.arange(TOPK * NT)[None, :] + i[:, None]
    arrays = {
        "uT": lay(u.T), "u": lay(u), "w_small": lay(w_small), "w_theta": lay(wT[:, th0:th0 + H * NH]),
        "w_z": lay(wT[:, 0:DI]), "w_x": lay(wT[:, DI:2 * DI]),
        "w_out": lay(np.asarray(L0_attn_out_proj_w).T.reshape(DI // 128, 128, DM).transpose(1, 0, 2)),
        "norm_w": lay(nrm.reshape(DI // 128, 128).T),
        "bias": lay(np.stack([b0, b1, c0, c1], 1)),
        "dt_bias": lay(L0_attn_dt_bias), "A_log": lay(L0_attn_A_log), "D": lay(L0_attn_D),
        "B_norm": lay(L0_attn_B_norm_w), "C_norm": lay(L0_attn_C_norm_w),
        "CB_biasT": lay(np.concatenate([np.asarray(L0_attn_C_bias).T, np.asarray(L0_attn_B_bias).T])),
        "w_g": lay(np.asarray(L0_ffn_w_g).T), "c_fc": lay(L0_ffn_c_fc), "c_proj": lay(L0_ffn_c_proj),
        "tri": (i[:, None] <= i[None, :]).astype(f32),
        "low": np.where(i[:, None] < i[None, :], 0.0, -1.0).astype(b16),
        "base": (CAP * np.arange(EXP)).astype(f32),
        "ident": np.eye(128, dtype=f32), "ident_b": np.eye(128, dtype=b16),
        "mask": np.where(i[:, None] < i[None, :], 0.0, NEG).astype(b16),
        "hot": hot,
        "places": np.broadcast_to(i, (128, 128)).astype(b16),
        "tiles": np.broadcast_to(np.arange(EXP * CAP // 128), (128, EXP * CAP // 128)).astype(f32),
        "ids": np.stack([entry // 16 * 16, entry % 16], 1).astype(b16),
        "pref": np.arange(EXP, 0, -1).astype(f32),
    }
    nc = bacc.Bacc("TRN2", target_bir_lowering=False, num_devices=1)
    ins = {k: nc.dram_tensor(f"in_{k}", a.shape, mybir.dt.from_np(a.dtype), kind="ExternalInput").ap() for k, a in arrays.items()}
    out = nc.dram_tensor("out", [TOK, DM], F32, kind="ExternalOutput").ap()
    build(nc, ins, out)
    r = run_bass_kernel_spmd(nc, [{f"in_{k}": a for k, a in arrays.items()}], core_ids=[0])
    return r.results[0]["out"].reshape(BATCH, L, DM)
```
